# Optimizing a Trainium2 kernel written in Bass

```python
import numpy as np
import jax
import jax.numpy as jnp

def _softmax(x, axis=-1):
    return jax.nn.softmax(x, axis=axis)

def _gelu(x):
    return jax.nn.gelu(x, approximate=True)

def _silu(x):
    return jax.nn.silu(x)

def _sigmoid(x):
    return jax.nn.sigmoid(x)

def _layernorm(x, axis=-1, eps=1e-05):
    m = jnp.mean(x, axis=axis, keepdims=True)
    v = jnp.var(x, axis=axis, keepdims=True)
    return (x - m) / jnp.sqrt(v + eps)

def _scatter_add(tgt, idx, src, axis=0):
    return tgt.at[idx].add(src)

def _segment_sum(src, seg, n):
    return jax.ops.segment_sum(src, seg, n)
kernel_name = 'mk_macaron_d1_jaxref_r8_f73259'

def setup_inputs(seed: int=0):
    np.random.seed(seed)
    _w = jnp.asarray

    def _L0_attn_setup():
        import jax, jax.numpy as jnp
        import numpy as np
        import math
        DIM = 128
        NUM_HEADS = 16
        HEAD_DIM = DIM // NUM_HEADS
        MAX_BIAS = 8.0
        SCALE = HEAD_DIM ** (-0.5)

        def _alibi_slopes(n):

            def pow2(n):
                start = 2.0 ** (-2.0 ** (-(math.log2(n) - 3)))
                return [start * start ** i for i in range(n)]
            if math.log2(n).is_integer():
                return pow2(n)
            c = 2 ** math.floor(math.log2(n))
            return pow2(c) + _alibi_slopes(2 * c)[0::2][:n - c]

        def _rotate_half(t):
            t1, t2 = jnp.split(t, 2, axis=-1)
            return jnp.concatenate([-t2, t1], axis=-1)
        key = jax.random.key(seed)
        k1, k2, k3, k4 = jax.random.split(key, 4)
        B, N, C = (2, 256, DIM)
        x = jax.random.normal(k1, (B, N, C), dtype=jnp.float32)
        qkv_w = jax.random.normal(k2, (3 * C, C), dtype=jnp.float32) * C ** (-0.5)
        proj_w = jax.random.normal(k3, (C, C), dtype=jnp.float32) * C ** (-0.5)
        proj_b = jax.random.normal(k4, (C,), dtype=jnp.float32) * 0.01
        slopes = jnp.asarray(np.array(_alibi_slopes(NUM_HEADS), dtype=np.float32))
        return {'x': x, 'qkv_w': qkv_w, 'proj_w': proj_w, 'proj_b': proj_b, 'slopes': slopes}
    _L0_attn_in = _L0_attn_setup()

    def _L0_ffn_setup():
        import jax, jax.numpy as jnp
        import numpy as np
        DIM = 128
        LATENT = 64
        INTER = 64
        SHARED = 512
        E = 8
        TOPK = 2
        NGROUP = 2
        TOPKG = 1
        NORM_TOPK = True
        SCALE = 1.0
        B, S = (2, 128)

        def relu2(x):
            r = jnp.maximum(x, 0.0)
            return r * r
        key = jax.random.key(seed)
        ks = jax.random.split(key, 8)

        def w(k, shape, std=0.02):
            return jax.random.normal(k, shape, dtype=jnp.float32) * std
        return {'x': jax.random.normal(ks[0], (B, S, DIM), dtype=jnp.float32), 'gate': w(ks[1], (E, DIM)), 'corr_bias': jnp.zeros((E,), jnp.float32), 'w1': w(ks[2], (E, INTER, LATENT)), 'w2': w(ks[3], (E, LATENT, INTER)), 'fc1_w': w(ks[4], (LATENT, DIM)), 'fc2_w': w(ks[5], (DIM, LATENT)), 'up_w': w(ks[6], (SHARED, DIM)), 'down_w': w(ks[7], (DIM, SHARED))}
    _L0_ffn_in = _L0_ffn_setup()
    _d = {'L0_attn_x': _L0_attn_in['x'], 'L0_attn_qkv_w': _L0_attn_in['qkv_w'], 'L0_attn_proj_w': _L0_attn_in['proj_w'], 'L0_attn_proj_b': _L0_attn_in['proj_b'], 'L0_attn_slopes': _L0_attn_in['slopes'], 'L0_ffn_gate': _L0_ffn_in['gate'], 'L0_ffn_corr_bias': _L0_ffn_in['corr_bias'], 'L0_ffn_w1': _L0_ffn_in['w1'], 'L0_ffn_w2': _L0_ffn_in['w2'], 'L0_ffn_fc1_w': _L0_ffn_in['fc1_w'], 'L0_ffn_fc2_w': _L0_ffn_in['fc2_w'], 'L0_ffn_up_w': _L0_ffn_in['up_w'], 'L0_ffn_down_w': _L0_ffn_in['down_w']}
    _x0 = _d['L0_attn_x']
    _d['L0_attn_x'] = jax.random.normal(jax.random.fold_in(jax.random.key(seed), 1), (4, 1024, 128), dtype=_x0.dtype)
    del _x0
    return _d

def reference(L0_attn_x, L0_attn_qkv_w, L0_attn_proj_w, L0_attn_proj_b, L0_attn_slopes, L0_ffn_gate, L0_ffn_corr_bias, L0_ffn_w1, L0_ffn_w2, L0_ffn_fc1_w, L0_ffn_fc2_w, L0_ffn_up_w, L0_ffn_down_w):

    def _L0_attn_ref(x, qkv_w, proj_w, proj_b, slopes):
        import jax, jax.numpy as jnp
        import numpy as np
        import math
        DIM = 128
        NUM_HEADS = 16
        HEAD_DIM = DIM // NUM_HEADS
        MAX_BIAS = 8.0
        SCALE = HEAD_DIM ** (-0.5)

        def _alibi_slopes(n):

            def pow2(n):
                start = 2.0 ** (-2.0 ** (-(math.log2(n) - 3)))
                return [start * start ** i for i in range(n)]
            if math.log2(n).is_integer():
                return pow2(n)
            c = 2 ** math.floor(math.log2(n))
            return pow2(c) + _alibi_slopes(2 * c)[0::2][:n - c]

        def _rotate_half(t):
            t1, t2 = jnp.split(t, 2, axis=-1)
            return jnp.concatenate([-t2, t1], axis=-1)
        B, N, C = x.shape
        H, D = (NUM_HEADS, HEAD_DIM)
        qkv = (x @ qkv_w.T).reshape(B, N, 3, H, D).transpose(2, 0, 3, 1, 4)
        q, k, v = (qkv[0], qkv[1], qkv[2])
        inv_freq = 1.0 / 10000.0 ** (jnp.arange(0, D, 2, dtype=jnp.float32) / D)
        freqs = jnp.arange(N, dtype=jnp.float32)[:, None] * inv_freq[None, :]
        sin = jnp.tile(jnp.sin(freqs), (1, 2))
        cos = jnp.tile(jnp.cos(freqs), (1, 2))
        q = q * cos + _rotate_half(q) * sin
        k = k * cos + _rotate_half(k) * sin
        attn = jnp.einsum('bhqd,bhkd->bhqk', q, k) * SCALE
        pos = jnp.arange(N, dtype=jnp.float32)
        diff = pos[None, :] - pos[:, None]
        diff = jnp.where(diff > 0, 0.0, diff)
        alibi = diff[None, :, :] * slopes[:, None, None] * MAX_BIAS
        attn = attn + alibi[None]
        w = jax.nn.softmax(attn, axis=-1)
        out = jnp.einsum('bhqk,bhkd->bhqd', w, v)
        out = out.transpose(0, 2, 1, 3).reshape(B, N, C)
        return out @ proj_w.T + proj_b

    def _L0_ffn_ref(x, gate, corr_bias, w1, w2, fc1_w, fc2_w, up_w, down_w):
        import jax, jax.numpy as jnp
        import numpy as np
        DIM = 128
        LATENT = 64
        INTER = 64
        SHARED = 512
        E = 8
        TOPK = 2
        NGROUP = 2
        TOPKG = 1
        NORM_TOPK = True
        SCALE = 1.0
        B, S = (2, 128)

        def relu2(x):
            r = jnp.maximum(x, 0.0)
            return r * r
        Bv, Sv, D = x.shape
        xf = x.reshape(-1, D)
        N = xf.shape[0]
        scores = jax.nn.sigmoid(xf.astype(jnp.float32) @ gate.T)
        sfc = scores + corr_bias
        gs = E // NGROUP
        if NGROUP > 1:
            group_scores = jax.lax.top_k(sfc.reshape(N, NGROUP, gs), 2)[0].sum(-1)
            gidx = jax.lax.top_k(group_scores, TOPKG)[1]
            gmask = jnp.zeros((N, NGROUP), sfc.dtype).at[jnp.arange(N)[:, None], gidx].set(1.0)
            smask = jnp.repeat(gmask, gs, axis=1)
            sfc = jnp.where(smask > 0, sfc, 0.0)
        sel = jax.lax.top_k(sfc, TOPK)[1]
        top_scores = jnp.take_along_axis(scores, sel, axis=1)
        if NORM_TOPK:
            top_scores = top_scores / (top_scores.sum(-1, keepdims=True) + 1e-20)
        flat = sel.reshape(-1)
        perm = jnp.argsort(flat, stable=True)
        sorted_eid = flat[perm]
        scores_sorted = top_scores.reshape(-1)[perm]
        tok = perm // TOPK
        lat = xf @ fc1_w.T
        xs = lat[tok]
        out = jnp.zeros_like(xs)
        for e in range(E):
            he = relu2(xs @ w1[e].T) @ w2[e].T
            out = jnp.where((sorted_eid == e)[:, None], he, out)
        out = out * scores_sorted[:, None]
        comb = jnp.zeros((N, LATENT), out.dtype).at[tok].add(out)
        routed = comb @ fc2_w.T * SCALE
        shared = relu2(xf @ up_w.T) @ down_w.T
        return (routed + shared).reshape(Bv, Sv, D)
    x = L0_attn_x
    x = x + 0.5 * _L0_ffn_ref(_layernorm(x, axis=-1), L0_ffn_gate, L0_ffn_corr_bias, L0_ffn_w1, L0_ffn_w2, L0_ffn_fc1_w, L0_ffn_fc2_w, L0_ffn_up_w, L0_ffn_down_w)
    x = x + _L0_attn_ref(_layernorm(x, axis=-1), L0_attn_qkv_w, L0_attn_proj_w, L0_attn_proj_b, L0_attn_slopes)
    x = x + 0.5 * _L0_ffn_ref(_layernorm(x, axis=-1), L0_ffn_gate, L0_ffn_corr_bias, L0_ffn_w1, L0_ffn_w2, L0_ffn_fc1_w, L0_ffn_fc2_w, L0_ffn_up_w, L0_ffn_down_w)
    return x

_drawn_inputs = setup_inputs


def setup_inputs(seed=0):
    import zlib

    import numpy as np

    out = dict(_drawn_inputs(seed))
    spreads = {'L0_ffn_corr_bias': (0.0, 0.8)}
    factors = {'L0_attn_proj_b': 5.595,
     'L0_ffn_gate': 8.0,
     'L0_ffn_w1': 8.0,
     'L0_ffn_w2': 8.0,
     'L0_ffn_fc1_w': 8.0,
     'L0_ffn_fc2_w': 8.0,
     'L0_ffn_down_w': 3.131}
    for name, (base, spread) in spreads.items():
        noise = np.random.default_rng([zlib.crc32(name.encode()), seed]).standard_normal(out[name].shape)
        drawn = base * np.exp(spread * noise) if base else spread * noise
        out[name] = jnp.asarray(drawn.astype(out[name].dtype))
    for name, factor in factors.items():
        out[name] = (out[name] * factor).astype(out[name].dtype)
    return out
```

```python
from contextlib import ExitStack

import numpy as np

import concourse.bass as bass
from concourse import mybir

F32 = mybir.dt.float32
BF16 = mybir.dt.bfloat16
ALU = mybir.AluOpType
ACT = mybir.ActivationFunctionType
AX = mybir.AxisListType

P = 128
BATCH, SEQ, DIM = 4, 1024, 128
HEADS = 16
HD = DIM // HEADS
HALF = HD // 2
EXPERTS, LATENT, INTER, SHARED = 8, 64, 64, 512
GROUPS = 2
PER_GROUP = EXPERTS // GROUPS
HIDDEN = SHARED + EXPERTS * INTER
HT = HIDDEN // P
ST = SHARED // P
CHUNK = 512
TILES = CHUNK // P
CHUNKS = BATCH * SEQ // CHUNK
HALVES = SEQ // CHUNK
GH = 4
HG = HEADS // GH
NGRP = BATCH * HG
KT = SEQ // P
PARTS = 3
VW = HD + 1
EPS = 1e-5
SCALE = HD ** -0.5

QK_ROWS = PARTS * PARTS * HD
SHIFT_ROW = QK_ROWS
PLAIN_K = SHIFT_ROW + PARTS
BIAS_ROW = 96
BIAS_ROWS = PARTS + KT * PARTS + PARTS
FULL_K = BIAS_ROW + BIAS_ROWS
SHIFT_LIMIT = 32.0
SLOTS = 3
PSTEPS = 4
FILL_FROM = 8
UNITS = KT * GH
POOL_SQUARES = tuple(range(ST))
ROUTE_STEPS = 15


class Chunk:

    def __init__(self, pair, k):
        self.pair, self.k = pair, k
        self.n = 2 * pair + k
        self.batch = pair + k // 2
        self.half = k % 2
        self.seen = self.batch + 1
        self.at_least = self.n if isinstance(pair, int) else 2 + k

    def next(self, by=1):
        return Chunk(self.pair, self.k + by)


def in_chunks(eng, lead, body, tail):
    lead()
    for n in range(3):
        body(Chunk(0, n), False)
    with eng.Fori(1, CHUNKS // 2 - 1) as pair:
        body(Chunk(pair, 1), False)
        body(Chunk(pair, 2), False)
    body(Chunk(BATCH - 1, 1), True)
    tail(Chunk(BATCH - 1, 1))


def shape_constants():
    c = {}
    inv = (1.0 / np.float32(10000.0) ** (np.arange(0, HD, 2, dtype=np.float32) / np.float32(HD))).astype(np.float32)
    ang = (np.arange(SEQ, dtype=np.float32)[None, :] * inv[:, None]).astype(np.float32)
    rows = np.arange(P) % HD % HALF
    cos, sin = np.cos(ang.astype(np.float64))[rows], np.sin(ang.astype(np.float64))[rows]
    c["rope"] = np.stack([cos * SCALE, sin * SCALE, cos, sin], 1).astype(np.float32)
    pos = np.arange(SEQ)
    block, r = pos // P, pos % P
    part = np.arange(BIAS_ROWS) % PARTS
    kside, qside = np.zeros((BIAS_ROWS, SEQ)), np.zeros((BIAS_ROWS, SEQ))
    kside[:PARTS], qside[:PARTS] = r, 1.0
    for j in range(KT):
        at = PARTS * (1 + j)
        kside[at:at + PARTS] = P * (block - j)
        qside[at:at + PARTS] = block == j
    kside[-PARTS:], qside[-PARTS:] = 1.0, -r
    c["biasrows"] = np.stack([qside, kside], 1).astype(np.float32)
    sel = np.zeros((BIAS_ROWS, 2, 4), np.float32)
    for row in range(BIAS_ROWS):
        last = row >= BIAS_ROWS - PARTS
        sel[row, 0, 3 if last else part[row]] = 1.0
        sel[row, 1, part[row] if last else 3] = 1.0
    c["biassel"] = sel.reshape(BIAS_ROWS, 8)
    key, query = np.arange(P)[:, None], np.arange(P)[None, :]
    c["diag"] = np.stack([np.minimum(key - query, 0), np.minimum(query - key, 0)], 1).astype(np.float32)
    tri = np.tril(np.ones((EXPERTS, EXPERTS), np.float32), -1)
    c["earlier"] = np.broadcast_to(tri.reshape(1, -1), (P, EXPERTS * EXPERTS)).copy()
    c["ident"] = np.eye(P, dtype=np.float32)
    c["headsum"] = (np.arange(P)[:, None] // HD == np.arange(HEADS)[None, :]).astype(np.float32)
    return c


def program(nc, io, consts, out):
    ctx = ExitStack()
    with ctx:
        def sb(name, shape, dt=F32):
            return ctx.enter_context(nc.sbuf_tensor(name, shape, dt))

        def sem(name):
            return ctx.enter_context(nc.semaphore(name))

        x1_dram = nc.dram_tensor("x1_scratch", [BATCH * SEQ, DIM], F32)
        part_dram = [nc.dram_tensor(f"{n}_parts", [PARTS, BATCH * DIM, SEQ], BF16) for n in "qk"]
        shift_dram = nc.dram_tensor("shift_parts", [PARTS, BATCH * HEADS, SEQ], BF16)
        v_dram = nc.dram_tensor("v_scratch", [NGRP, P, KT, GH * VW], F32)
        o_dram = nc.dram_tensor("o_scratch", [BATCH * HEADS, VW, SEQ], F32)

        x_tiles = io["L0_attn_x"].rearrange("b (h t p) c -> (b h) p t c", p=P, t=TILES)
        x1_tiles = x1_dram[:, :].rearrange("(n t p) c -> n p t c", p=P, t=TILES)
        out_tiles = out.rearrange("b (h t p) c -> (b h) p t c", p=P, t=TILES)
        part_chunk = [d[:, :].rearrange("a (b c) (h t) -> b h c a t", b=BATCH, h=HALVES) for d in part_dram]
        part_group = [d[:, :].rearrange("a (g j d) t -> g a d j t", j=GH, d=HD) for d in part_dram]
        shift_group = shift_dram[:, :, :].rearrange("a (g j) t -> g a j t", j=GH)
        shift_heads = shift_dram[:, :, :].rearrange("a (b h) t -> a h b t", b=BATCH)
        shift_rows = shift_dram[:, :, :].rearrange("a (g j) (q r) -> g (j q) a r", j=GH, r=P)
        v_chunk = v_dram[:, :, :, :].rearrange("(b g) p (h k) c -> b h p g (k c)", b=BATCH, h=HALVES)
        v_group = v_dram[:, :, :, :]
        o_group = o_dram[:, :, :].rearrange("(g j) r t -> g j r t", j=GH)
        o_chunk = o_dram[:, :, :].rearrange("(b j) r (h t) -> b h j r t", b=BATCH, h=HALVES)

        ident = sb("ident", [P, P])
        earlier = sb("earlier", [P, EXPERTS, EXPERTS])
        corr = sb("corr", [P, EXPERTS])
        proj_bias = sb("proj_bias", [P, DIM])
        w_in = sb("w_in", [P, HIDDEN])
        w_out = sb("w_out", [P, HT, DIM])
        gate_t = sb("gate_t", [P, P])
        qkv_t = sb("qkv_t", [P, 3, DIM])
        rot_t = sb("rot_t", [P, 2, DIM])
        proj_t = sb("proj_t", [P, DIM])
        headsum = sb("headsum", [P, HEADS], BF16)
        norm_max = sb("norm_max", [HEADS, 2, CHUNKS])
        bound_ok = sb("bound_ok", [1, 1], mybir.dt.int32)
        head_scale = sb("head_scale", [P, BATCH * HEADS, 3])
        diag = sb("diag", [P, 2, P])
        bias_rows = sb("bias_rows", [P, 2, SEQ], BF16)
        bias_sel = sb("bias_sel", [P, 8])

        w_ready = sem("w_ready")
        c_loaded = sem("c_loaded")

        with nc.Block() as block, ExitStack() as own:
            def tmp(name, shape, dt=F32):
                return own.enter_context(nc.sbuf_tensor(name, shape, dt))
            raw_up = tmp("raw_up", [P, ST, DIM])
            raw_w1 = tmp("raw_w1", [P, 4, LATENT])
            raw_w2 = tmp("raw_w2", [LATENT, EXPERTS, INTER])
            raw_fc1 = tmp("raw_fc1", [LATENT, DIM])
            raw_fc2 = tmp("raw_fc2", [P, LATENT])
            raw_down = tmp("raw_down", [P, SHARED])
            raw_gate = tmp("raw_gate", [EXPERTS, DIM])
            raw_qkv = tmp("raw_qkv", [P, 3, DIM])
            raw_proj = tmp("raw_proj", [P, DIM])
            w1_t = tmp("w1_t", [LATENT, EXPERTS * INTER])
            fc2_t = tmp("fc2_t", [LATENT, DIM])
            headsum_f32 = tmp("headsum_f32", [P, HEADS])
            bias_f32 = tmp("bias_f32", [P, 2, SEQ])
            slope8 = tmp("slope8", [P, BATCH * HEADS])
            part_hi = tmp("part_hi", [P, BATCH * HEADS], BF16)
            part_mid = tmp("part_mid", [P, BATCH * HEADS], BF16)
            part_low = tmp("part_low", [P, BATCH * HEADS], BF16)
            rest1 = tmp("rest1", [P, BATCH * HEADS])
            rest2 = tmp("rest2", [P, BATCH * HEADS])
            bank = [own.enter_context(nc.psum_tensor(f"prep{i}", [P, CHUNK], F32)) for i in range(8)]
            prep_mm, prep_cp, prep_v = sem("prep_mm"), sem("prep_cp"), sem("prep_v")
            slopes = io["L0_attn_slopes"].rearrange("(a h) -> a h", a=1)
            br = slice(BIAS_ROW, FULL_K)

            loads = [
                (ident[:, :], consts["ident"]),
                (raw_up[:, :, :], io["L0_ffn_up_w"].rearrange("(t p) c -> p t c", p=P)),
                (raw_w1[:, :, :], io["L0_ffn_w1"].rearrange("(t e) i l -> (e i) t l", e=2)),
                (raw_w2[:, :, :], io["L0_ffn_w2"].rearrange("e l i -> l e i")),
                (raw_fc1[:, :], io["L0_ffn_fc1_w"]),
                (raw_fc2[:, :], io["L0_ffn_fc2_w"]),
                (raw_down[:, :], io["L0_ffn_down_w"]),
                (raw_gate[:, :], io["L0_ffn_gate"]),
                (raw_qkv[:, :, :], io["L0_attn_qkv_w"].rearrange("(s p) c -> p s c", p=P)),
                (raw_proj[:, :], io["L0_attn_proj_w"]),
                (earlier[:, :, :], consts["earlier"].rearrange("p (a b) -> p a b", a=EXPERTS)),
                (corr[:, :], io["L0_ffn_corr_bias"].rearrange("(a h) -> a h", a=1).broadcast_to([P, EXPERTS])),
                (proj_bias[:, :], io["L0_attn_proj_b"].rearrange("(a h) -> a h", a=1).broadcast_to([P, DIM])),
                (slope8[:, :].rearrange("p (b h) -> p b h", b=BATCH), slopes.unsqueeze(1).broadcast_to([P, BATCH, HEADS])),
                (diag[:, :, :], consts["diag"]),
                (headsum_f32[:, :], consts["headsum"]),
                (bias_f32[br, :, :], consts["biasrows"]),
                (bias_sel[br, :], consts["biassel"]),
            ]

            @block.sync
            def _(sp):
                for dst, src in loads:
                    sp.dma_start(dst, src).then_inc(c_loaded, 16)

            @block.tensor
            def _(pe):
                pe.wait_ge(c_loaded, 16 * len(loads))
                tr = nc.tensor.transpose
                for t in range(4):
                    tr(bank[0][:, t * P:(t + 1) * P], raw_up[:, t, :], ident[:, :])
                    tr(bank[1][0:LATENT, t * P:(t + 1) * P], raw_w1[:, t, :], ident[:, :])
                    tr(bank[2][:, t * P:(t + 1) * P], raw_down[:, t * P:(t + 1) * P], ident[:, :])
                tr(bank[3][0:LATENT, 0:P], raw_fc2[:, :], ident[:, :])
                tr(bank[3][:, P:P + EXPERTS], raw_gate[:, :], ident[0:EXPERTS, 0:EXPERTS])
                tr(bank[3][:, 2 * P:3 * P], raw_proj[:, :], ident[:, :])
                for s in range(3):
                    last = tr(bank[4][:, s * P:(s + 1) * P], raw_qkv[:, s, :], ident[:, :])
                last.then_inc(prep_mm, 1)
                pe.wait_ge(prep_cp, 1)
                nc.tensor.matmul(bank[5][:, :], raw_fc1[:, :], w1_t[:, :], start=True, stop=True)
                for t in range(4):
                    last = nc.tensor.matmul(bank[6][:, t * P:(t + 1) * P],
                                            raw_w2[:, 2 * t:2 * t + 2, :].rearrange("l e i -> l (e i)"),
                                            fc2_t[:, :], start=True, stop=True)
                last.then_inc(prep_mm, 1)

            @block.vector
            def _(dve):
                v = nc.vector
                dve.wait_ge(prep_mm, 1)
                v.tensor_copy(w1_t[:, :], bank[1][0:LATENT, :])
                v.tensor_copy(fc2_t[:, :], bank[3][0:LATENT, 0:P]).then_inc(prep_cp, 1)
                v.tensor_copy(w_in[:, 0:SHARED], bank[0][:, :])
                v.tensor_copy(w_out[:, 0:ST, :], bank[2][:, :].rearrange("p (t n) -> p t n", n=DIM))
                v.memset(gate_t[:, EXPERTS:P], 0.0)
                v.tensor_copy(gate_t[:, 0:EXPERTS], bank[3][:, P:P + EXPERTS])
                v.tensor_copy(proj_t[:, :], bank[3][:, 2 * P:3 * P])
                v.tensor_copy(qkv_t[:, :, :], bank[4][:, 0:3 * P].rearrange("p (s n) -> p s n", n=DIM))
                src = bank[4][:, 0:2 * P].rearrange("p (s d) -> p s d", d=HD)
                dst = rot_t[:, :, :].rearrange("p s (h d) -> p (s h) d", d=HD)
                v.tensor_scalar(dst[:, :, 0:HALF], src[:, :, HALF:HD], -1.0, None, ALU.mult)
                v.tensor_copy(dst[:, :, HALF:HD], src[:, :, 0:HALF])
                v.tensor_copy(bias_rows[br, :, :], bias_f32[br, :, :])
                v.tensor_copy(headsum[:, :], headsum_f32[:, :])
                v.tensor_scalar(slope8[:, :], slope8[:, :], 8.0, None, ALU.mult).then_inc(prep_v, 1)
                dve.wait_ge(prep_v, 1)
                v.tensor_copy(part_hi[:, :], slope8[:, :]).then_inc(prep_v, 1)
                dve.wait_ge(prep_v, 2)
                v.tensor_tensor(rest1[:, :], slope8[:, :], part_hi[:, :], ALU.subtract).then_inc(prep_v, 1)
                dve.wait_ge(prep_v, 3)
                v.tensor_copy(part_mid[:, :], rest1[:, :]).then_inc(prep_v, 1)
                dve.wait_ge(prep_v, 4)
                v.tensor_tensor(part_low[:, :], rest1[:, :], part_mid[:, :], ALU.subtract).then_inc(prep_v, 1)
                v.memset(head_scale[:, :, 1:3], 0.0)
                v.tensor_copy(head_scale[:, :, 0], slope8[:, :]).then_inc(prep_v, 1)
                dve.wait_ge(prep_v, 6)
                done = 6
                for side in range(2):
                    col = 4 * side
                    v.tensor_scalar(rest2[br, :], part_hi[br, :], bias_sel[br, col:col + 1],
                                    bias_sel[br, col + 3:col + 4], ALU.mult, ALU.add).then_inc(prep_v, 1)
                    for i, part in enumerate((part_mid, part_low)):
                        done += 1
                        dve.wait_ge(prep_v, done)
                        dst = (rest1, head_scale[:, :, 1 + side])[i]
                        src = (rest2, rest1)[i]
                        v.scalar_tensor_tensor(out=dst[br, :], in0=part[br, :],
                                               scalar=bias_sel[br, col + 1 + i:col + 2 + i],
                                               in1=src[br, :], op0=ALU.mult, op1=ALU.add).then_inc(prep_v, 1)
                    done += 1
                    dve.wait_ge(prep_v, done)
                dve.wait_ge(prep_mm, 2)
                v.tensor_copy(w_in[:, SHARED:HIDDEN], bank[5][:, :])
                v.tensor_copy(w_out[:, ST:HT, :],
                              bank[6][:, :].rearrange("p (t n) -> p t n", n=DIM)).then_inc(w_ready, 1)

        token_pass(nc, sem, 1, locals())
        bound_shift(nc, sem, locals())
        exact_maxima(nc, sem, locals())
        attention(nc, sem, locals())
        token_pass(nc, sem, 2, locals())


def token_pass(nc, sem, number, env):
    first = number == 1
    ident, earlier, corr = env["ident"], env["earlier"], env["corr"]
    w_in, w_out, gate_t = env["w_in"], env["w_out"], env["gate_t"]
    headsum = env["headsum"]
    qkv_t, rot_t, proj_t, proj_bias = env["qkv_t"], env["rot_t"], env["proj_t"], env["proj_bias"]
    RT = HT - ST

    with ExitStack() as own:
        def sb(name, shape, dt=F32):
            return own.enter_context(nc.sbuf_tensor(f"p{number}_{name}", shape, dt))

        def ps(name, shape):
            return own.enter_context(nc.psum_tensor(f"p{number}_{name}", shape, F32))

        def s(name):
            return sem(f"p{number}_{name}")

        x = sb("x", [P, 2, TILES, DIM])
        stats = sb("stats", [P, 2, TILES, 6])
        mean2, mean, apart, apart2, var_n, var_in = (
            sb(name, [P, 2, TILES]) for name in ("mean2", "mean", "apart", "apart2", "var_n", "var_in"))
        veps = sb("veps", [P, 2, TILES])
        rstd = sb("rstd", [P, 2, TILES])
        minus_half = sb("minus_half", [P, TILES])
        xn = sb("xn", [P, TILES, DIM])
        xn_t = sb("xn_t", [P, 2, CHUNK])
        logit_t = sb("logit_t", [P, CHUNK])
        en = sb("en", [P, TILES, EXPERTS])
        en1 = sb("en1", [P, TILES, EXPERTS])
        score = sb("score", [P, TILES, EXPERTS])
        sfc = sb("sfc", [P, TILES, EXPERTS])
        pair_sum = sb("pair_sum", [P, TILES * GROUPS, 6])
        gsum = sb("gsum", [P, TILES, GROUPS])
        gmask = sb("gmask", [P, TILES, GROUPS])
        kept = sb("kept", [P, TILES, EXPERTS])
        above = sb("above", [P, TILES, EXPERTS * EXPERTS])
        equal = sb("equal", [P, TILES, EXPERTS * EXPERTS])
        rank = sb("rank", [P, TILES, EXPERTS])
        chosen = sb("chosen", [P, TILES, EXPERTS])
        csum = sb("csum", [P, TILES])
        csum1 = sb("csum1", [P, TILES])
        crec = sb("crec", [P, TILES])
        coef = sb("coef", [P, TILES, EXPERTS])
        coef_wide = sb("coef_wide", [P, TILES, EXPERTS * INTER])
        relu = sb("relu", [P, HT, CHUNK])
        scaled = sb("scaled", [P, RT, CHUNK])
        hid = sb("hid", [P, HT, CHUNK])
        res = sb("res", [P, TILES, DIM])

        ps_t = ps("ps_t", [P, CHUNK])
        ps_g = ps("ps_g", [P, CHUNK])
        ps_h = ps("ps_h", [P, 2, CHUNK])
        ps_c = ps("ps_c", [P, CHUNK])
        ps_o = ps("ps_o", [P, TILES, DIM])
        ps_q = ps("ps_q", [P, 2, CHUNK])

        x_loaded = [s("x_loaded0"), s("x_loaded1")]
        half_set = s("half_set")
        rstd_ready = [s("rstd_ready"), s("rstd2_ready")]
        norm_step, norm_ready, turned, xt_ready = s("norm_step"), s("norm_ready"), s("turned"), s("xt_ready")
        gate_made, gate_copied, gate_turned, gate_exp = s("gate_made"), s("gate_copied"), s("gate_turned"), s("gate_exp")
        route_step, coef_ready, wide_ready = s("route_step"), s("coef_ready"), s("wide_ready")
        hid_made, relu_ready = s("hid_made"), s("relu_ready")
        spread, scaled_ready = s("spread"), s("scaled_ready")
        sq_pool, sq_dve = s("squared_by_pool"), s("squared_by_dve")
        ffn_made, res_ready, res_stored = s("ffn_made"), s("res_ready"), s("res_stored")
        POOL_N, DVE_N = len(POOL_SQUARES), HT - len(POOL_SQUARES)

        if first:
            xn2 = sb("xn2", [P, TILES, DIM])
            xn2_t = sb("xn2_t", [P, CHUNK])
            rope = sb("rope", [P, 4, SEQ])
            turn_a = sb("turn_a", [P, 2, CHUNK])
            turn_b = sb("turn_b", [P, 2, CHUNK])
            roped = sb("roped", [P, 2, CHUNK])
            left = sb("left", [P, 2, CHUNK])
            squares = sb("squares", [P, 2, CHUNK], BF16)
            parts = sb("parts", [P, 2, PARTS, CHUNK], BF16)
            v_ext = sb("v_ext", [P, HG, TILES, GH * VW])
            rope_loaded, ones_set = s("rope_loaded"), s("ones_set")
            norm2_step, norm2_ready, turned2, xt2_ready = s("norm2_step"), s("norm2_ready"), s("turned2"), s("xt2_ready")
            squares_ready, norms_made, norms_read = s("squares_ready"), s("norms_made"), s("norms_read")
            qk_made, turn_ready, rope_step = s("qk_made"), s("turn_ready"), s("rope_step")
            v_made, v_ready, v_stored = s("v_made"), s("v_ready"), s("v_stored")
            parts_ready, parts_stored = [s("q_parts"), s("k_parts")], [s("q_stored"), s("k_stored")]
        else:
            x_in = sb("x_in", [P, 2, TILES, DIM])
            x_biased = sb("x_biased", [P, TILES, DIM])
            o_in = sb("o_in", [P, 2, CHUNK])
            den_in = sb("den_in", [P, 2, CHUNK])
            rden = sb("rden", [P, CHUNK])
            o_norm = sb("o_norm", [P, CHUNK])
            merge_step, o_ready, proj_made = s("merge_step"), s("o_ready"), s("proj_made")

        block = own.enter_context(nc.Block())

        @block.sync
        def _(sp):
            def load(c):
                half = c.half
                if first:
                    sp.dma_start(x[:, half], env["x_tiles"][c.n]).then_inc(x_loaded[half], 16)
                else:
                    sp.dma_start(x_in[:, half], env["x1_tiles"][c.n]).then_inc(x_loaded[half], 16)
                    heads = env["o_chunk"][c.batch, half]
                    sp.dma_start(o_in[:, half], heads[:, 0:HD, :]).then_inc(x_loaded[half], 16)
                    sp.dma_start(den_in[:, half], heads[:, HD:VW, :].broadcast_to([HEADS, HD, CHUNK])
                                 ).then_inc(x_loaded[half], 16)

            def store_qkv(c):
                sp.wait_ge(v_ready, c.n + 1)
                for g in range(HG):
                    sp.dma_start(env["v_chunk"][c.batch, c.half][:, g], v_ext[:, g].rearrange("p t c -> p (t c)")
                                 ).then_inc(v_stored, 16)
                for side in range(2):
                    sp.wait_ge(parts_ready[side], c.n + 1)
                    sp.dma_start(env["part_chunk"][side][c.batch, c.half], parts[:, side]
                                 ).then_inc(parts_stored[side], 16)

            def lead():
                if first:
                    sp.dma_start(rope[:, :, :], env["consts"]["rope"]).then_inc(rope_loaded, 16)
                load(Chunk(0, 0))

            def body(c, end):
                if not end:
                    if c.at_least >= 1:
                        sp.wait_ge(res_ready, c.n)
                    load(c.next())
                if first and c.at_least >= 1:
                    store_qkv(c.next(-1))
                sp.wait_ge(res_ready, c.n + 1)
                sp.dma_start((env["x1_tiles"] if first else env["out_tiles"])[c.n], res[:, :, :]
                             ).then_inc(res_stored, 16)

            def tail(c):
                if first:
                    store_qkv(c)
                    sp.wait_ge(v_stored, 16 * HG * CHUNKS)
                    for side in range(2):
                        sp.wait_ge(parts_stored[side], 16 * CHUNKS)
                sp.wait_ge(res_stored, 16 * CHUNKS)

            in_chunks(sp, lead, body, tail)

        @block.tensor
        def _(pe):
            def front(c):
                if not first:
                    pe.wait_ge(o_ready, c.n + 1)
                    if c.at_least >= 1:
                        pe.wait_ge(norm_ready, c.n)
                    for t in range(TILES):
                        last = nc.tensor.matmul(ps_q[:, 0, t * P:(t + 1) * P], o_norm[:, t * P:(t + 1) * P],
                                                proj_t[:, :], start=True, stop=True)
                    last.then_inc(proj_made, 1)
                pe.wait_ge(norm_ready, c.n + 1)
                if c.at_least >= 1:
                    pe.wait_ge(xt_ready, c.n)
                if first and c.at_least >= 2:
                    pe.wait_ge(xt2_ready, c.n - 1)
                for t in range(TILES):
                    last = nc.tensor.transpose(ps_t[:, t * P:(t + 1) * P], xn[:, t, :], ident[:, :])
                last.then_inc(turned, 1)
                pe.wait_ge(xt_ready, c.n + 1)
                if c.at_least >= 1:
                    pe.wait_ge(gate_exp, c.n)
                nc.tensor.matmul(ps_g[:, :], gate_t[:, :], xn_t[:, c.half, :],
                                 start=True, stop=True).then_inc(gate_made, 1)
                pe.wait_ge(gate_copied, c.n + 1)
                for t in range(TILES):
                    last = nc.tensor.transpose(ps_g[:, t * P:(t + 1) * P], logit_t[:, t * P:(t + 1) * P],
                                               ident[:, :])
                last.then_inc(gate_turned, 1)

            def hidden(c, m):
                if not (c.at_least == 0 and m < 2):
                    pe.wait_ge(relu_ready, HT * c.n + m - 1)
                nc.tensor.matmul(ps_h[:, m % 2, :], w_in[:, m * P:(m + 1) * P], xn_t[:, c.half, :],
                                 start=True, stop=True).then_inc(hid_made, 1)

            def spread_coef(c, m):
                if m == 0:
                    pe.wait_ge(wide_ready, c.n + 1)
                if not (c.at_least == 0 and m == 0):
                    pe.wait_ge(scaled_ready, RT * c.n + m)
                for t in range(TILES):
                    last = nc.tensor.transpose(ps_c[:, t * P:(t + 1) * P],
                                               coef_wide[:, t, m * P:(m + 1) * P], ident[:, :])
                last.then_inc(spread, 1)

            def outputs(c):
                if c.at_least >= 1:
                    pe.wait_ge(res_ready, c.n)
                for t in range(TILES):
                    for m in range(HT):
                        if t == 0:
                            if m in POOL_SQUARES:
                                pe.wait_ge(sq_pool, POOL_N * c.n + POOL_SQUARES.index(m) + 1)
                            else:
                                pe.wait_ge(sq_dve, DVE_N * c.n + m - POOL_N + 1)
                        last = nc.tensor.matmul(ps_o[:, t, :], hid[:, m, t * P:(t + 1) * P], w_out[:, m, :],
                                                start=(m == 0), stop=(m == HT - 1))
                last.then_inc(ffn_made, 1)

            def qkv(c, fronts):
                pe.wait_ge(norm2_ready, c.n + 1)
                pe.wait_ge(xt_ready, fronts)
                if c.at_least >= 1:
                    pe.wait_ge(xt2_ready, c.n)
                for t in range(TILES):
                    last = nc.tensor.transpose(ps_t[:, t * P:(t + 1) * P], xn2[:, t, :], ident[:, :])
                last.then_inc(turned2, 1)
                pe.wait_ge(xt2_ready, c.n + 1)
                for i, w in enumerate((qkv_t[:, 0, :], rot_t[:, 0, :], qkv_t[:, 1, :], rot_t[:, 1, :])):
                    if i == 0 and c.at_least >= 1:
                        pe.wait_ge(norms_read, c.n)
                    elif i > 1:
                        pe.wait_ge(turn_ready, 4 * c.n + i - 1)
                    nc.tensor.matmul(ps_q[:, i % 2, :], w, xn2_t[:, :], start=True, stop=True).then_inc(qk_made, 1)
                pe.wait_ge(turn_ready, 4 * c.n + 3)
                for t in range(TILES):
                    last = nc.tensor.matmul(ps_q[:, 0, t * P:(t + 1) * P], xn2_t[:, t * P:(t + 1) * P],
                                            qkv_t[:, 2, :], start=True, stop=True)
                last.then_inc(v_made, 1)

            def norms(c):
                pe.wait_ge(squares_ready, c.n + 1)
                pe.wait_ge(v_ready, c.n + 1)
                pe.wait_ge(turn_ready, 4 * c.n + 4)
                for side in range(2):
                    last = nc.tensor.matmul(ps_q[0:HEADS, side, :], headsum[:, :], squares[:, side, :],
                                            start=True, stop=True)
                last.then_inc(norms_made, 1)

            def lead():
                pe.wait_ge(env["w_ready"], 1)
                front(Chunk(0, 0))

            def body(c, end):
                for m in range(ST):
                    hidden(c, m)
                for m in range(RT):
                    hidden(c, ST + m)
                    spread_coef(c, m)
                if first and c.at_least >= 1:
                    qkv(c.next(-1), c.n + 1)
                if not end:
                    front(c.next())
                outputs(c)
                if first and c.at_least >= 1:
                    norms(c.next(-1))

            def tail(c):
                if first:
                    qkv(c, CHUNKS)
                    norms(c)

            in_chunks(pe, lead, body, tail)

        @block.scalar
        def _(act):
            def copy(dst, src):
                return nc.scalar.activation(dst, src, ACT.Copy)

            def front(c):
                act.wait_ge(turned, c.n + 1)
                if c.at_least >= 2:
                    act.wait_ge(hid_made, HT * (c.n - 1))
                copy(xn_t[:, c.half, :], ps_t[:, :]).then_inc(xt_ready, 1)
                act.wait_ge(gate_made, c.n + 1)
                if c.at_least >= 1:
                    act.wait_ge(gate_turned, c.n)
                copy(logit_t[:, :], ps_g[:, :]).then_inc(gate_copied, 1)
                act.wait_ge(gate_turned, c.n + 1)
                if c.at_least >= 1:
                    act.wait_ge(coef_ready, c.n)
                nc.scalar.activation(en[:, :, :], ps_g[:, :].rearrange("p (t e) -> p t e", e=P)[:, :, 0:EXPERTS],
                                     ACT.Exp, scale=-1.0).then_inc(gate_exp, 1)

            def widen(c):
                act.wait_ge(coef_ready, c.n + 1)
                if c.at_least >= 1:
                    act.wait_ge(spread, RT * c.n)
                for t in range(TILES):
                    last = copy(coef_wide[:, t, :].rearrange("p (e i) -> p e i", i=INTER),
                                coef[:, t, :].unsqueeze(2).broadcast_to([P, EXPERTS, INTER]))
                last.then_inc(wide_ready, 1)

            def relus(c, m):
                act.wait_ge(hid_made, HT * c.n + m + 1)
                if c.at_least >= 1:
                    if m in POOL_SQUARES:
                        act.wait_ge(sq_pool, POOL_N * (c.n - 1) + POOL_SQUARES.index(m) + 1)
                    else:
                        act.wait_ge(sq_dve, DVE_N * (c.n - 1) + m - POOL_N + 1)
                nc.scalar.activation(relu[:, m, :], ps_h[:, m % 2, :], ACT.Relu).then_inc(relu_ready, 1)

            def v_of(g):
                return v_ext[:, g, :, :].rearrange("p t (j c) -> p t j c", c=VW)[:, :, :, 0:HD]

            def qkv(c):
                act.wait_ge(turned2, c.n + 1)
                if c.at_least >= 1:
                    act.wait_ge(v_made, c.n)
                copy(xn2_t[:, :], ps_t[:, :]).then_inc(xt2_ready, 1)
                act.wait_ge(v_made, c.n + 1)
                if c.at_least >= 1:
                    act.wait_ge(v_stored, 16 * HG * c.n)
                else:
                    act.wait_ge(ones_set, 1)
                v_ps = ps_q[:, 0, :].rearrange("p (t g j c) -> p g t j c", t=TILES, g=HG, c=HD)
                for g in range(HG):
                    last = copy(v_of(g), v_ps[:, g])
                last.then_inc(v_ready, 1)

            def body(c, end):
                widen(c)
                for m in range(HT):
                    relus(c, m)
                if first and c.at_least >= 1:
                    qkv(c.next(-1))
                if not end:
                    front(c.next())

            in_chunks(act, lambda: front(Chunk(0, 0)), body, lambda c: qkv(c) if first else None)

        def square(eng, ops, c, m, done):
            eng.wait_ge(relu_ready, HT * c.n + m + 1)
            if c.at_least >= 1:
                eng.wait_ge(ffn_made, c.n)
            factor = relu[:, m, :]
            if m >= ST:
                eng.wait_ge(scaled_ready, RT * c.n + m - ST + 1)
                factor = scaled[:, m - ST, :]
            ops.tensor_tensor(hid[:, m, :], factor, relu[:, m, :], ALU.mult).then_inc(done, 1)

        @block.gpsimd
        def _(pool):
            def power(c, which, step):
                pool.wait_ge(step, 4 * c.n + 4)
                nc.gpsimd.tensor_tensor(rstd[:, which, :], veps[:, which, :], minus_half[:, :],
                                        ALU.pow).then_inc(rstd_ready[which], 1)

            def square_qk(c):
                pool.wait_ge(rope_step, 2 * 4 * c.n + 8)
                if c.at_least >= 1:
                    pool.wait_ge(norms_made, c.n)
                nc.gpsimd.tensor_tensor(squares[:, :, :], roped[:, :, :], roped[:, :, :],
                                        ALU.mult).then_inc(squares_ready, 1)

            def lead():
                if first:
                    nc.gpsimd.memset(v_ext[:, :, :, :], 1.0).then_inc(ones_set, 1)
                nc.gpsimd.memset(minus_half[:, :], -0.5).then_inc(half_set, 1)
                pool.wait_ge(half_set, 1)
                power(Chunk(0, 0), 0, norm_step)

            def body(c, end):
                for m in POOL_SQUARES:
                    square(pool, nc.gpsimd, c, m, sq_pool)
                if not end:
                    power(c.next(), 0, norm_step)
                if first:
                    power(c, 1, norm2_step)
                    if c.at_least >= 1:
                        square_qk(c.next(-1))

            in_chunks(pool, lead, body, lambda c: square_qk(c) if first else None)

        @block.vector
        def _(dve):
            v = nc.vector

            def layernorm(src, dst, which, step, n):
                at = 4 * n
                for t in range(TILES):
                    last = v.bn_stats(stats[:, which, t, :], src[:, t, :])
                last.then_inc(step, 1)
                dve.wait_ge(step, at + 1)
                even, odd = stats[:, which, :, 1], stats[:, which, :, 4]
                v.tensor_tensor(mean2[:, which, :], even, odd, ALU.add)
                v.tensor_tensor(apart[:, which, :], even, odd, ALU.subtract)
                v.tensor_tensor(var_n[:, which, :], stats[:, which, :, 2], stats[:, which, :, 5],
                                ALU.add).then_inc(step, 1)
                dve.wait_ge(step, at + 2)
                v.tensor_scalar(mean[:, which, :], mean2[:, which, :], 0.5, None, ALU.mult)
                v.tensor_tensor(apart2[:, which, :], apart[:, which, :], apart[:, which, :], ALU.mult)
                v.tensor_scalar(var_in[:, which, :], var_n[:, which, :], 1.0 / DIM, EPS, ALU.mult,
                                ALU.add).then_inc(step, 1)
                dve.wait_ge(step, at + 3)
                v.scalar_tensor_tensor(out=veps[:, which, :], in0=apart2[:, which, :], scalar=0.25,
                                       in1=var_in[:, which, :], op0=ALU.mult, op1=ALU.add).then_inc(step, 1)
                dve.wait_ge(rstd_ready[which], n + 1)
                for t in range(TILES):
                    last = v.tensor_scalar(dst[:, t, :], src[:, t, :], mean[:, which, t:t + 1],
                                           rstd[:, which, t:t + 1], ALU.subtract, ALU.mult)
                return last

            def front(c):
                if first:
                    dve.wait_ge(x_loaded[c.half], 16 * c.seen)
                else:
                    dve.wait_ge(x_loaded[c.half], 48 * c.seen)
                    v.reciprocal(rden[:, :], den_in[:, c.half, :]).then_inc(merge_step, 1)
                    dve.wait_ge(merge_step, 3 * c.n + 1)
                    if c.at_least >= 1:
                        dve.wait_ge(proj_made, c.n)
                    v.tensor_tensor(o_norm[:, :], o_in[:, c.half, :], rden[:, :], ALU.mult).then_inc(o_ready, 1)
                    v.tensor_tensor(x_biased[:, :, :], x_in[:, c.half],
                                    proj_bias[:, :].unsqueeze(1).broadcast_to([P, TILES, DIM]),
                                    ALU.add).then_inc(merge_step, 1)
                    dve.wait_ge(merge_step, 3 * c.n + 2)
                    dve.wait_ge(proj_made, c.n + 1)
                    v.tensor_tensor(x[:, c.half], x_biased[:, :, :],
                                    ps_q[:, 0, :].rearrange("p (t c) -> p t c", c=DIM),
                                    ALU.add).then_inc(merge_step, 1)
                    dve.wait_ge(merge_step, 3 * c.n + 3)
                if c.at_least >= 1:
                    dve.wait_ge(turned, c.n)
                layernorm(x[:, c.half], xn, 0, norm_step, c.n).then_inc(norm_ready, 1)

            def route(c):
                r = ROUTE_STEPS * c.n
                dve.wait_ge(gate_exp, c.n + 1)
                v.tensor_scalar(en1[:, :, :], en[:, :, :], 1.0, None, ALU.add).then_inc(route_step, 1)
                dve.wait_ge(route_step, r + 1)
                v.reciprocal(score[:, :, :], en1[:, :, :]).then_inc(route_step, 1)
                dve.wait_ge(route_step, r + 2)
                v.tensor_tensor(sfc[:, :, :], score[:, :, :], corr[:, :].unsqueeze(1).broadcast_to(
                    [P, TILES, EXPERTS]), ALU.add).then_inc(route_step, 1)
                dve.wait_ge(route_step, r + 3)
                four = sfc[:, :, :].rearrange("p t (g e) -> p (t g) e", e=PER_GROUP)
                v.tensor_tensor(pair_sum[:, :, 0:3], four[:, :, 0:3], four[:, :, 1:4], ALU.add)
                v.tensor_tensor(pair_sum[:, :, 3:5], four[:, :, 0:2], four[:, :, 2:4], ALU.add)
                v.tensor_tensor(pair_sum[:, :, 5:6], four[:, :, 0:1], four[:, :, 3:4],
                                ALU.add).then_inc(route_step, 1)
                dve.wait_ge(route_step, r + 4)
                v.tensor_reduce(gsum[:, :, :].rearrange("p t g -> p (t g)"), pair_sum[:, :, :],
                                AX.X, ALU.max).then_inc(route_step, 1)
                dve.wait_ge(route_step, r + 5)
                v.tensor_tensor(gmask[:, :, 0:1], gsum[:, :, 0:1], gsum[:, :, 1:2], ALU.is_ge)
                v.tensor_tensor(gmask[:, :, 1:2], gsum[:, :, 1:2], gsum[:, :, 0:1],
                                ALU.is_gt).then_inc(route_step, 1)
                dve.wait_ge(route_step, r + 6)
                v.tensor_tensor(kept[:, :, :].rearrange("p t (g e) -> p (t g) e", e=PER_GROUP), four,
                                gmask[:, :, :].rearrange("p t g -> p (t g)").unsqueeze(2).broadcast_to(
                                    [P, TILES * GROUPS, PER_GROUP]), ALU.mult).then_inc(route_step, 1)
                dve.wait_ge(route_step, r + 7)
                wide = [P, TILES, EXPERTS, EXPERTS]
                mine = kept[:, :, :].unsqueeze(3).broadcast_to(wide)
                other = kept[:, :, :].unsqueeze(2).broadcast_to(wide)
                above4 = above[:, :, :].rearrange("p t (a b) -> p t a b", a=EXPERTS)
                equal4 = equal[:, :, :].rearrange("p t (a b) -> p t a b", a=EXPERTS)
                v.tensor_tensor(above4, other, mine, ALU.is_gt)
                v.tensor_tensor(equal4, other, mine, ALU.is_equal).then_inc(route_step, 1)
                dve.wait_ge(route_step, r + 8)
                v.tensor_tensor(equal[:, :, :], equal[:, :, :],
                                earlier[:, :, :].rearrange("p a b -> p (a b)").unsqueeze(1).broadcast_to(
                                    [P, TILES, EXPERTS * EXPERTS]), ALU.mult).then_inc(route_step, 1)
                dve.wait_ge(route_step, r + 9)
                v.tensor_tensor(above[:, :, :], above[:, :, :], equal[:, :, :], ALU.add).then_inc(route_step, 1)
                dve.wait_ge(route_step, r + 10)
                v.tensor_reduce(rank[:, :, :], above4, AX.X, ALU.add).then_inc(route_step, 1)
                dve.wait_ge(route_step, r + 11)
                v.scalar_tensor_tensor(out=chosen[:, :, :], in0=rank[:, :, :], scalar=2.0, in1=score[:, :, :],
                                       op0=ALU.is_lt, op1=ALU.mult).then_inc(route_step, 1)
                dve.wait_ge(route_step, r + 12)
                v.tensor_reduce(csum[:, :], chosen[:, :, :], AX.X, ALU.add).then_inc(route_step, 1)
                dve.wait_ge(route_step, r + 13)
                v.tensor_scalar(csum1[:, :], csum[:, :], 1e-20, None, ALU.add).then_inc(route_step, 1)
                dve.wait_ge(route_step, r + 14)
                v.reciprocal(crec[:, :], csum1[:, :]).then_inc(route_step, 1)
                dve.wait_ge(route_step, r + 15)
                if c.at_least >= 1:
                    dve.wait_ge(wide_ready, c.n)
                v.tensor_tensor(coef[:, :, :], chosen[:, :, :],
                                crec[:, :].unsqueeze(2).broadcast_to([P, TILES, EXPERTS]),
                                ALU.mult).then_inc(coef_ready, 1)

            def scale(c, m):
                dve.wait_ge(relu_ready, HT * c.n + ST + m + 1)
                dve.wait_ge(spread, RT * c.n + m + 1)
                v.tensor_tensor(scaled[:, m, :], relu[:, ST + m, :], ps_c[:, :], ALU.mult).then_inc(scaled_ready, 1)

            def residual(c):
                dve.wait_ge(ffn_made, c.n + 1)
                if c.at_least >= 1:
                    dve.wait_ge(res_stored, 16 * c.n)
                v.scalar_tensor_tensor(out=res[:, :, :], in0=ps_o[:, :, :], scalar=0.5, in1=x[:, c.half],
                                       op0=ALU.mult, op1=ALU.add).then_inc(res_ready, 1)
                if first:
                    dve.wait_ge(res_ready, c.n + 1)
                    if c.at_least >= 1:
                        dve.wait_ge(turned2, c.n)
                    layernorm(res, xn2, 1, norm2_step, c.n).then_inc(norm2_ready, 1)

            def rotary(c):
                at = slice(c.half * CHUNK, (c.half + 1) * CHUNK)
                for side in range(2):
                    r = 8 * c.n + 4 * side
                    for i, dst in enumerate((turn_a, turn_b)):
                        dve.wait_ge(qk_made, 4 * c.n + 2 * side + i + 1)
                        v.tensor_tensor(dst[:, side, :], ps_q[:, i, :], rope[:, 2 * side + i, at],
                                        ALU.mult).then_inc(turn_ready, 1)
                    dve.wait_ge(turn_ready, 4 * c.n + 2 * side + 2)
                    if c.at_least >= 1:
                        dve.wait_ge(squares_ready, c.n)
                    v.tensor_tensor(roped[:, side, :], turn_a[:, side, :], turn_b[:, side, :],
                                    ALU.add).then_inc(rope_step, 1)
                    dve.wait_ge(rope_step, r + 1)
                    if c.at_least >= 1:
                        dve.wait_ge(parts_stored[side], 16 * c.n)
                    v.tensor_copy(parts[:, side, 0, :], roped[:, side, :]).then_inc(rope_step, 1)
                    dve.wait_ge(rope_step, r + 2)
                    v.tensor_tensor(left[:, side, :], roped[:, side, :], parts[:, side, 0, :],
                                    ALU.subtract).then_inc(rope_step, 1)
                    dve.wait_ge(rope_step, r + 3)
                    v.tensor_copy(parts[:, side, 1, :], left[:, side, :]).then_inc(rope_step, 1)
                    dve.wait_ge(rope_step, r + 4)
                    v.tensor_tensor(parts[:, side, 2, :], left[:, side, :], parts[:, side, 1, :],
                                    ALU.subtract).then_inc(parts_ready[side], 1)

            def largest_norms(c):
                dve.wait_ge(norms_made, c.n + 1)
                v.tensor_reduce(env["norm_max"][:, :, bass.ds(c.n, 1)].rearrange("h s c -> h (s c)"), ps_q[0:HEADS, :, :],
                                AX.X, ALU.max).then_inc(norms_read, 1)

            def lead():
                dve.wait_ge(env["w_ready"], 1)
                front(Chunk(0, 0))
                route(Chunk(0, 0))
                if first:
                    dve.wait_ge(rope_loaded, 16)

            def body(c, end):
                for m in range(HT):
                    if m >= ST:
                        scale(c, m - ST)
                    if m not in POOL_SQUARES:
                        square(dve, v, c, m, sq_dve)
                if first and c.at_least >= 1:
                    rotary(c.next(-1))
                if not end:
                    front(c.next())
                    route(c.next())
                residual(c)
                if first and c.at_least >= 1:
                    largest_norms(c.next(-1))

            def tail(c):
                if first:
                    rotary(c)
                    largest_norms(c)

            in_chunks(dve, lead, body, tail)


def load_parts(sp, env, group, q_op, k_op, loaded):
    for a in range(PARTS):
        for b in range(PARTS):
            at = HD * (PARTS * a + b)
            sp.dma_start(q_op[at:at + HD], env["part_group"][0][group, b]).then_inc(loaded, 16)
            sp.dma_start(k_op[at:at + HD], env["part_group"][1][group, a]).then_inc(loaded, 16)


PART_LOADS = 2 * PARTS * PARTS


def fill_bias_row(nc, env, now, ops, n):
    br = slice(BIAS_ROW, FULL_K)
    j, side = divmod(n, 2)
    return nc.vector.tensor_scalar(ops[side][br, j, :], env["bias_rows"][br, side, :],
                                   now[br, j, 1 + side:2 + side], None, ALU.mult)


def fill_bias_rows(nc, env, now, ops):
    for n in range(2 * GH):
        last = fill_bias_row(nc, env, now, ops, n)
    return last


def pieces(limit):
    cuts = sorted({0, CHUNK, SEQ, limit})
    return [(lo, hi, hi <= limit) for lo, hi in zip(cuts, cuts[1:])]


def bound_shift(nc, sem, env):
    norm_max, bound_ok, ident = env["norm_max"], env["bound_ok"], env["ident"]
    with ExitStack() as own:
        def sb(name, shape, dt=F32):
            return own.enter_context(nc.sbuf_tensor(f"bs_{name}", shape, dt))

        product = sb("product", [HEADS, BATCH])
        both = sb("both", [HEADS, 2, BATCH])
        bound = sb("bound", [HEADS, BATCH])
        half = sb("half", [HEADS, BATCH])
        within = sb("within", [HEADS, BATCH])
        all_within = sb("all_within", [HEADS, 1])
        minus = sb("minus", [HEADS, BATCH])
        left = sb("left", [HEADS, BATCH])
        hi, mid = sb("hi", [HEADS, BATCH], BF16), sb("mid", [HEADS, BATCH], BF16)
        part = sb("part", [HEADS, PARTS, BATCH])
        zeros = sb("zeros", [HEADS, SEQ], BF16)
        shift = sb("shift", [HEADS, PARTS, BATCH, SEQ], BF16)
        ps = own.enter_context(nc.psum_tensor("bs_ps", [P, CHUNK], F32))
        step, rooted, turned, stored = sem("bs_step"), sem("bs_rooted"), sem("bs_turned"), sem("bs_stored")
        half_set, ready, judged = sem("bs_half_set"), sem("bs_ready"), sem("bs_judged")
        block = own.enter_context(nc.Block())

        @block.gpsimd
        def _(pool):
            nc.gpsimd.memset(half[:, :], 0.5).then_inc(half_set, 1)
            pool.wait_ge(half_set, 1)
            pool.wait_ge(step, 2)
            nc.gpsimd.tensor_tensor(bound[:, :], product[:, :], half[:, :], ALU.pow).then_inc(rooted, 1)

        @block.tensor
        def _(pe):
            pe.wait_ge(judged, 1)
            nc.tensor.transpose(ps[0:1, 0:HEADS], all_within[:, :], ident[0:HEADS, 0:HEADS]).then_inc(turned, 1)

        @block.vector
        def _(dve):
            v = nc.vector
            v.memset(zeros[:, :], 0.0)
            v.tensor_reduce(both[:, :, :], norm_max[:, :, :].rearrange("h s (b c) -> h s b c", c=HALVES),
                            AX.X, ALU.max).then_inc(step, 1)
            dve.wait_ge(step, 1)
            v.tensor_tensor(product[:, :], both[:, 0, :], both[:, 1, :], ALU.mult).then_inc(step, 1)
            dve.wait_ge(rooted, 1)
            v.tensor_scalar(within[:, :], bound[:, :], SHIFT_LIMIT, None, ALU.is_le).then_inc(step, 1)
            dve.wait_ge(step, 3)
            v.tensor_reduce(all_within[:, :], within[:, :], AX.X, ALU.min).then_inc(judged, 1)
            v.tensor_scalar(minus[:, :], bound[:, :], -1.0, None, ALU.mult).then_inc(step, 1)
            dve.wait_ge(step, 4)
            v.tensor_copy(hi[:, :], minus[:, :]).then_inc(step, 1)
            dve.wait_ge(step, 5)
            v.tensor_copy(part[:, 0, :], hi[:, :])
            v.tensor_tensor(left[:, :], minus[:, :], hi[:, :], ALU.subtract).then_inc(step, 1)
            dve.wait_ge(step, 6)
            v.tensor_copy(mid[:, :], left[:, :]).then_inc(step, 1)
            dve.wait_ge(step, 7)
            v.tensor_copy(part[:, 1, :], mid[:, :])
            v.tensor_tensor(part[:, 2, :], left[:, :], mid[:, :], ALU.subtract).then_inc(step, 1)
            dve.wait_ge(step, 8)
            for a in range(PARTS):
                for b in range(BATCH):
                    last = v.tensor_scalar(shift[:, a, b, :], zeros[:, :], part[:, a, b:b + 1], None, ALU.add)
            last.then_inc(ready, 1)
            dve.wait_ge(turned, 1)
            v.tensor_reduce(bound_ok[:, :], ps[0:1, 0:HEADS], AX.X, ALU.min).then_inc(step, 1)

        @block.sync
        def _(sp):
            sp.wait_ge(ready, 1)
            for a in range(PARTS):
                sp.dma_start(env["shift_heads"][a], shift[:, a]).then_inc(stored, 16)
            sp.wait_ge(stored, 16 * PARTS)


def exact_maxima(nc, sem, env):
    ident, diag, head_scale, bound_ok = env["ident"], env["diag"], env["head_scale"], env["bound_ok"]
    with ExitStack() as own:
        def sb(name, shape, dt=F32):
            return own.enter_context(nc.sbuf_tensor(f"mx_{name}", shape, dt))

        def s(name):
            return sem(f"mx_{name}")

        q_op, k_op = sb("q_op", [P, GH, SEQ], BF16), sb("k_op", [P, GH, SEQ], BF16)
        now = sb("now", [P, 2, GH, 3])
        largest = sb("largest", [P, UNITS])
        largest_t = sb("largest_t", [UNITS, P])
        rest = sb("rest", [UNITS, P])
        shift = sb("shift", [UNITS, PARTS, P], BF16)
        scores = own.enter_context(nc.psum_tensor("mx_scores", [P, 2, SEQ], F32))
        ps_t = own.enter_context(nc.psum_tensor("mx_ps_t", [P, CHUNK], F32))
        loaded, rows_set, now_set, bias_set = s("loaded"), s("rows_set"), s("now_set"), s("bias_set")
        scores_made, diag_added, reduced = s("scores_made"), s("diag_added"), s("reduced")
        turned, part_step, shift_ready, shift_stored = s("turned"), s("part_step"), s("shift_ready"), s("shift_stored")
        block = own.enter_context(nc.Block())

        @block.sync
        def _(sp):
            with sp.If(sp.value_load(bound_ok[0:1, 0:1], min_val=0, max_val=1) == 0):
                sp.wait_ge(rows_set, 1)
                load_parts(sp, env, 0, q_op, k_op, loaded)
                with sp.Fori(0, NGRP - 1) as g:
                    sp.wait_ge(scores_made, UNITS * (g + 1))
                    load_parts(sp, env, g + 1, q_op, k_op, loaded)
                    sp.wait_ge(shift_ready, g + 1)
                    sp.dma_start(env["shift_rows"][g], shift[:, :, :]).then_inc(shift_stored, 16)
                sp.wait_ge(shift_ready, NGRP)
                sp.dma_start(env["shift_rows"][NGRP - 1], shift[:, :, :]).then_inc(shift_stored, 16)
                sp.wait_ge(shift_stored, 16 * NGRP)

        @block.gpsimd
        def _(pool):
            nc.gpsimd.memset(q_op[64:BIAS_ROW], 0.0)
            nc.gpsimd.memset(k_op[64:BIAS_ROW], 1.0).then_inc(rows_set, 1)

        @block.tensor
        def _(pe):
            with pe.If(pe.value_load(bound_ok[0:1, 0:1], min_val=0, max_val=1) == 0):
                with pe.Fori(0, NGRP) as g:
                    pe.wait_ge(loaded, 16 * PART_LOADS * (g + 1))
                    pe.wait_ge(bias_set, g + 1)
                    for j in range(GH):
                        for qt in range(KT):
                            u = KT * j + qt
                            pe.wait_ge(reduced, UNITS * g + u + 1)
                            for lo, hi, behind in pieces(qt * P):
                                rows = FULL_K if behind else PLAIN_K
                                last = nc.tensor.matmul(scores[:, u % 2, lo:hi], q_op[0:rows, j, qt * P:(qt + 1) * P],
                                                        k_op[0:rows, j, lo:hi], start=True, stop=True)
                            last.then_inc(scores_made, 1)
                    pe.wait_ge(reduced, UNITS * (g + 1) + 2)
                    nc.tensor.transpose(ps_t[0:UNITS, 0:P], largest[:, :], ident[:, :]).then_inc(turned, 1)

        @block.vector
        def _(dve):
            with dve.If(dve.value_load(bound_ok[0:1, 0:1], min_val=0, max_val=1) == 0):
                v = nc.vector
                dve.wait_ge(rows_set, 1)
                v.memset(largest[:, :], 0.0).then_inc(reduced, 2)

                def fill(g, par):
                    v.tensor_copy(now[:, par], head_scale[:, bass.ds(GH * g, GH), :]).then_inc(now_set, 1)
                    dve.wait_ge(now_set, g + 1)
                    fill_bias_rows(nc, env, now[:, par], (q_op, k_op)).then_inc(bias_set, 1)

                def group(g, par, end):
                    for j in range(GH):
                        for qt in range(KT):
                            u = KT * j + qt
                            dve.wait_ge(scores_made, UNITS * g + u + 1)
                            block_at = scores[:, u % 2, qt * P:(qt + 1) * P]
                            v.scalar_tensor_tensor(out=block_at, in0=diag[:, 1, :],
                                                   scalar=now[:, par, j, 0:1], in1=block_at,
                                                   op0=ALU.mult, op1=ALU.add).then_inc(diag_added, 1)
                            dve.wait_ge(diag_added, UNITS * g + u + 1)
                            v.tensor_reduce(largest[:, u:u + 1], scores[:, u % 2, :], AX.X, ALU.max).then_inc(reduced, 1)
                    if not end:
                        fill(g + 1, 1 - par)
                    dve.wait_ge(turned, g + 1)
                    v.tensor_scalar(largest_t[:, :], ps_t[0:UNITS, 0:P], -1.0, None, ALU.mult).then_inc(part_step, 1)
                    dve.wait_ge(part_step, 4 * g + 1)
                    if not isinstance(g, int) or g >= 1:
                        dve.wait_ge(shift_stored, 16 * g)
                    v.tensor_copy(shift[:, 0, :], largest_t[:, :]).then_inc(part_step, 1)
                    dve.wait_ge(part_step, 4 * g + 2)
                    v.tensor_tensor(rest[:, :], largest_t[:, :], shift[:, 0, :], ALU.subtract).then_inc(part_step, 1)
                    dve.wait_ge(part_step, 4 * g + 3)
                    v.tensor_copy(shift[:, 1, :], rest[:, :]).then_inc(part_step, 1)
                    dve.wait_ge(part_step, 4 * g + 4)
                    v.tensor_tensor(shift[:, 2, :], rest[:, :], shift[:, 1, :], ALU.subtract).then_inc(shift_ready, 1)

                fill(0, 0)
                group(0, 0, False)
                with dve.Fori(0, NGRP // 2 - 1) as pair:
                    group(2 * pair + 1, 1, False)
                    group(2 * pair + 2, 0, False)
                group(NGRP - 1, 1, True)


def attention(nc, sem, env):
    diag, head_scale = env["diag"], env["head_scale"]
    with ExitStack() as own:
        def sb(name, shape, dt=F32):
            return own.enter_context(nc.sbuf_tensor(f"at_{name}", shape, dt))

        def s(name):
            return sem(f"at_{name}")

        q_op = [sb(f"q_op{i}", [P, GH, SEQ], BF16) for i in range(2)]
        k_op = [sb(f"k_op{i}", [P, GH, SEQ], BF16) for i in range(2)]
        now = sb("now", [P, 2, GH, 3])
        v_op = [sb(f"v_op{i}", [P, KT, GH * VW]) for i in range(2)]
        weights = sb("weights", [P, PSTEPS, GH, SEQ])
        o_out = sb("o_out", [P, SEQ])
        scores = own.enter_context(nc.psum_tensor("at_scores", [P, SLOTS, SEQ], F32))
        acc = own.enter_context(nc.psum_tensor("at_acc", [P, SEQ], F32))

        qk_loaded, v_loaded = [s("qk_loaded0"), s("qk_loaded1")], [s("v_loaded0"), s("v_loaded1")]
        rows_set, now_set, bias_set = s("rows_set"), s("now_set"), s("bias_set")
        scores_made, diag_added = s("scores_made"), s("diag_added")
        slots_free = s("slots_free")
        steps_free = s("steps_free")
        o_ready, o_stored = s("o_ready"), s("o_stored")
        block = own.enter_context(nc.Block())

        def in_groups(eng, body):
            body(0, 0, 0, False)
            with eng.Fori(0, NGRP // 2 - 1) as pair:
                body(2 * pair + 1, 1, pair, False)
                body(2 * pair + 2, 0, pair + 1, False)
            body(NGRP - 1, 1, NGRP // 2 - 1, True)

        @block.sync
        def _(sp):
            def load(g, par):
                load_parts(sp, env, g, q_op[par], k_op[par], qk_loaded[par])
                sp.dma_start(q_op[par][SHIFT_ROW:PLAIN_K], env["shift_group"][g]).then_inc(qk_loaded[par], 16)

            def load_v(g, par):
                sp.dma_start(v_op[par][:, :, :], env["v_group"][g]).then_inc(v_loaded[par], 16)

            def store(g):
                sp.wait_ge(o_ready, 2 * g + 4)
                for j in range(GH):
                    sp.dma_start(env["o_group"][g, j], o_out[32 * j:32 * j + VW, :]).then_inc(o_stored, 16)

            sp.wait_ge(rows_set, 1)
            for g in range(2):
                load(g, g)
                load_v(g, g)
            with sp.Fori(0, NGRP // 2 - 1) as pair:
                for par in range(2):
                    g = 2 * pair + par
                    sp.wait_ge(scores_made, UNITS * (g + 1))
                    load(g + 2, par)
                    sp.wait_ge(steps_free, KT * (g + 1) + PSTEPS)
                    load_v(g + 2, par)
                    store(g)
            for par in range(2):
                store(NGRP - 2 + par)
            sp.wait_ge(o_stored, 16 * GH * NGRP + 1)

        @block.gpsimd
        def _(pool):
            nc.gpsimd.memset(q_op[0][64:BIAS_ROW], 0.0).then_inc(slots_free, SLOTS)
            nc.gpsimd.memset(q_op[1][64:BIAS_ROW], 0.0).then_inc(steps_free, PSTEPS)
            nc.gpsimd.memset(k_op[0][64:BIAS_ROW], 1.0).then_inc(o_stored, 1)
            nc.gpsimd.memset(k_op[1][64:BIAS_ROW], 1.0).then_inc(rows_set, 1)

        @block.tensor
        def _(pe):
            def score(g, par, seen, u):
                kt, j = divmod(u, GH)
                if u == 0:
                    pe.wait_ge(qk_loaded[par], 16 * (PART_LOADS + 1) * (seen + 1))
                    pe.wait_ge(bias_set, g + 1)
                before = {0: 2, 1: 3, 2: 1}.get(u, u + 1)
                pe.wait_ge(slots_free, UNITS * g + before)
                for lo, hi, ahead in pieces((kt + 1) * P):
                    rows = PLAIN_K if ahead else FULL_K
                    last = nc.tensor.matmul(scores[:, u % SLOTS, lo:hi], k_op[par][0:rows, j, kt * P:(kt + 1) * P],
                                            q_op[par][0:rows, j, lo:hi], start=True, stop=True)
                last.then_inc(scores_made, 1)

            def weigh(g, par, seen, kt, half):
                if half == 0:
                    pe.wait_ge(slots_free, SLOTS + UNITS * g + GH * (kt + 1))
                    if kt == 0:
                        pe.wait_ge(v_loaded[par], 16 * (seen + 1))
                if kt == 0:
                    pe.wait_ge(o_ready, 2 * g + 1 + half)
                cols = slice(half * CHUNK, (half + 1) * CHUNK)
                for j in range(GH):
                    last = nc.tensor.matmul(acc[32 * j:32 * j + VW, cols], v_op[par][:, kt, VW * j:VW * (j + 1)],
                                            weights[:, kt % PSTEPS, j, cols], start=(kt == 0), stop=(kt == KT - 1))
                if half == 1:
                    last.then_inc(steps_free, 1)

            def body(g, par, seen, end):
                def ahead(kt, j):
                    if kt < KT:
                        score(g, par, seen, GH * kt + j)
                    elif not end:
                        score(g + 1, 1 - par, seen + par, GH * (kt - KT) + j)

                for kt in range(KT):
                    ahead(kt + 1, 2)
                    weigh(g, par, seen, kt, 0)
                    ahead(kt + 1, 3)
                    weigh(g, par, seen, kt, 1)
                    ahead(kt + 2, 0)
                    ahead(kt + 2, 1)

            for u in range(GH + 2):
                score(0, 0, 0, u)
            in_groups(pe, body)

        @block.vector
        def _(dve):
            v = nc.vector

            def take_scales(g, par):
                v.tensor_copy(now[:, par], head_scale[:, bass.ds(GH * g, GH), :]).then_inc(now_set, 1)

            def read_acc(g):
                dve.wait_ge(steps_free, KT * (g + 1) + PSTEPS)
                dve.wait_ge(o_stored, 16 * GH * g + 1)
                v.tensor_copy(o_out[:, 0:CHUNK], acc[:, 0:CHUNK]).then_inc(o_ready, 1)
                v.tensor_copy(o_out[:, CHUNK:SEQ], acc[:, CHUNK:SEQ]).then_inc(o_ready, 1)

            def body(g, par, seen, end):
                for u in range(UNITS):
                    kt, j = divmod(u, GH)
                    if u == GH + 2 and (not isinstance(g, int) or g > 0):
                        read_acc(g - 1)
                    dve.wait_ge(scores_made, UNITS * g + u + 1)
                    block_at = scores[:, u % SLOTS, kt * P:(kt + 1) * P]
                    v.scalar_tensor_tensor(out=block_at, in0=diag[:, 0, :], scalar=now[:, par, j, 0:1],
                                           in1=block_at, op0=ALU.mult, op1=ALU.add).then_inc(diag_added, 1)
                    if u == FILL_FROM - 1 and not end:
                        take_scales(g + 1, 1 - par)
                    n = (u - FILL_FROM) // 2
                    if u >= FILL_FROM and u % 2 == 0 and n < 2 * GH and not end:
                        if n == 0:
                            dve.wait_ge(now_set, g + 2)
                        row = fill_bias_row(nc, env, now[:, 1 - par], (q_op[1 - par], k_op[1 - par]), n)
                        if n == 2 * GH - 1:
                            row.then_inc(bias_set, 1)

            v.memset(acc[:, :], 0.0).then_inc(o_ready, 2)
            take_scales(0, 0)
            dve.wait_ge(rows_set, 1)
            dve.wait_ge(now_set, 1)
            fill_bias_rows(nc, env, now[:, 0], (q_op[0], k_op[0])).then_inc(bias_set, 1)
            in_groups(dve, body)
            read_acc(NGRP - 1)

        @block.scalar
        def _(act):
            with act.Fori(0, NGRP) as g:
                for u in range(UNITS):
                    kt, j = divmod(u, GH)
                    if j == 0:
                        act.wait_ge(steps_free, KT * g + kt + 1)
                    act.wait_ge(diag_added, UNITS * g + u + 1)
                    nc.scalar.activation(weights[:, kt % PSTEPS, j, :], scores[:, u % SLOTS, :],
                                         ACT.Exp).then_inc(slots_free, 1)


_INS = ["L0_attn_x", "L0_attn_qkv_w", "L0_attn_proj_w", "L0_attn_proj_b", "L0_attn_slopes", "L0_ffn_gate",
        "L0_ffn_corr_bias", "L0_ffn_w1", "L0_ffn_w2", "L0_ffn_fc1_w", "L0_ffn_fc2_w", "L0_ffn_up_w",
        "L0_ffn_down_w"]


def kernel(**inputs):
    import concourse.bacc as _bacc
    from concourse.bass_utils import run_bass_kernel_spmd as _run

    nc = _bacc.Bacc("TRN2", target_bir_lowering=False, num_devices=1)
    arrays, io, consts = {}, {}, {}
    for name in _INS:
        a = np.ascontiguousarray(inputs[name])
        arrays[f"in_{name}_dram"] = a
        io[name] = nc.dram_tensor(f"in_{name}_dram", a.shape, mybir.dt.from_np(a.dtype), kind="ExternalInput").ap()
    for name, a in shape_constants().items():
        arrays[f"const_{name}"] = a
        consts[name] = nc.dram_tensor(f"const_{name}", a.shape, mybir.dt.from_np(a.dtype), kind="ExternalInput").ap()
    out = nc.dram_tensor("out_0_dram", (BATCH, SEQ, DIM), F32, kind="ExternalOutput").ap()
    program(nc, io, consts, out)
    r = _run(nc, [arrays], core_ids=[0])
    return r.results[0]["out_0_dram"]
```

```python
from contextlib import ExitStack

import numpy as np

import concourse.bass as bass
from concourse import mybir

F32 = mybir.dt.float32
BF16 = mybir.dt.bfloat16
ALU = mybir.AluOpType
ACT = mybir.ActivationFunctionType
AX = mybir.AxisListType

P = 128
BATCH, SEQ, DIM = 4, 1024, 128
HEADS = 16
HD = DIM // HEADS
HALF = HD // 2
EXPERTS, LATENT, INTER, SHARED = 8, 64, 64, 512
GROUPS = 2
PER_GROUP = EXPERTS // GROUPS
HIDDEN = SHARED + EXPERTS * INTER
HT = HIDDEN // P
ST = SHARED // P
CHUNK = 512
TILES = CHUNK // P
CHUNKS = BATCH * SEQ // CHUNK
HALVES = SEQ // CHUNK
GH = 4
HG = HEADS // GH
NGRP = BATCH * HG
KT = SEQ // P
PARTS = 3
VW = HD + 1
EPS = 1e-5
SCALE = HD ** -0.5

QK_ROWS = PARTS * PARTS * HD
SHIFT_ROW = QK_ROWS
PLAIN_K = SHIFT_ROW + PARTS
BIAS_ROW = 96
BIAS_ROWS = PARTS + KT * PARTS + PARTS
FULL_K = BIAS_ROW + BIAS_ROWS
SHIFT_LIMIT = 32.0
SLOTS = 3
PSTEPS = 4
FILL_FROM = 8
UNITS = KT * GH
ROUTE_STEPS = 15


class Chunk:

    def __init__(self, pair, k):
        self.pair, self.k = pair, k
        self.n = 2 * pair + k
        self.batch = pair + k // 2
        self.half = k % 2
        self.seen = self.batch + 1
        self.loads_ahead = not (isinstance(self.n, int) and self.n + 2 >= CHUNKS)
        self.at_least = self.n if isinstance(pair, int) else 2 + k

    def next(self, by=1):
        return Chunk(self.pair, self.k + by)


def in_chunks(eng, lead, body, tail):
    lead()
    for n in range(2):
        body(Chunk(0, n), False)
    with eng.Fori(1, CHUNKS // 2 - 1) as pair:
        body(Chunk(pair, 0), False)
        body(Chunk(pair, 1), False)
    body(Chunk(BATCH - 1, 0), False)
    body(Chunk(BATCH - 1, 1), True)
    tail(Chunk(BATCH - 1, 1))


def shape_constants():
    c = {}
    inv = (1.0 / np.float32(10000.0) ** (np.arange(0, HD, 2, dtype=np.float32) / np.float32(HD))).astype(np.float32)
    ang = (np.arange(SEQ, dtype=np.float32)[None, :] * inv[:, None]).astype(np.float32)
    rows = np.arange(P) % HD % HALF
    cos, sin = np.cos(ang.astype(np.float64))[rows], np.sin(ang.astype(np.float64))[rows]
    c["rope"] = np.stack([cos * SCALE, sin * SCALE, cos, sin], 1).astype(np.float32)
    pos = np.arange(SEQ)
    block, r = pos // P, pos % P
    part = np.arange(BIAS_ROWS) % PARTS
    kside, qside = np.zeros((BIAS_ROWS, SEQ)), np.zeros((BIAS_ROWS, SEQ))
    kside[:PARTS], qside[:PARTS] = r, 1.0
    for j in range(KT):
        at = PARTS * (1 + j)
        kside[at:at + PARTS] = P * (block - j)
        qside[at:at + PARTS] = block == j
    kside[-PARTS:], qside[-PARTS:] = 1.0, -r
    c["biasrows"] = np.stack([qside, kside], 1).astype(np.float32)
    sel = np.zeros((BIAS_ROWS, 2, 4), np.float32)
    for row in range(BIAS_ROWS):
        last = row >= BIAS_ROWS - PARTS
        sel[row, 0, 3 if last else part[row]] = 1.0
        sel[row, 1, part[row] if last else 3] = 1.0
    c["biassel"] = sel.reshape(BIAS_ROWS, 8)
    key, query = np.arange(P)[:, None], np.arange(P)[None, :]
    c["diag"] = np.stack([np.minimum(key - query, 0), np.minimum(query - key, 0)], 1).astype(np.float32)
    tri = np.tril(np.ones((EXPERTS, EXPERTS), np.float32), -1)
    c["earlier"] = np.broadcast_to(tri.reshape(1, -1), (P, EXPERTS * EXPERTS)).copy()
    c["ident"] = np.eye(P, dtype=np.float32)
    c["headsum"] = (np.arange(P)[:, None] // HD == np.arange(HEADS)[None, :]).astype(np.float32)
    return c


def program(nc, io, consts, out):
    ctx = ExitStack()
    with ctx:
        def sb(name, shape, dt=F32):
            return ctx.enter_context(nc.sbuf_tensor(name, shape, dt))

        def sem(name):
            return ctx.enter_context(nc.semaphore(name))

        x1_dram = nc.dram_tensor("x1_scratch", [BATCH * SEQ, DIM], F32)
        part_dram = [nc.dram_tensor(f"{n}_parts", [PARTS, BATCH * DIM, SEQ], BF16) for n in "qk"]
        shift_dram = nc.dram_tensor("shift_parts", [PARTS, BATCH * HEADS, SEQ], BF16)
        v_dram = nc.dram_tensor("v_scratch", [NGRP, P, KT, GH * VW], F32)
        o_dram = nc.dram_tensor("o_scratch", [BATCH * HEADS, VW, SEQ], F32)

        x_tiles = io["L0_attn_x"].rearrange("b (h t p) c -> (b h) p t c", p=P, t=TILES)
        x1_tiles = x1_dram[:, :].rearrange("(n t p) c -> n p t c", p=P, t=TILES)
        out_tiles = out.rearrange("b (h t p) c -> (b h) p t c", p=P, t=TILES)
        part_chunk = [d[:, :].rearrange("a (b c) (h t) -> b h c a t", b=BATCH, h=HALVES) for d in part_dram]
        part_group = [d[:, :].rearrange("a (g j d) t -> g a d j t", j=GH, d=HD) for d in part_dram]
        shift_group = shift_dram[:, :, :].rearrange("a (g j) t -> g a j t", j=GH)
        shift_heads = shift_dram[:, :, :].rearrange("a (b h) t -> a h b t", b=BATCH)
        shift_rows = shift_dram[:, :, :].rearrange("a (g j) (q r) -> g (j q) a r", j=GH, r=P)
        v_chunk = v_dram[:, :, :, :].rearrange("(b g) p (h k) c -> b h p g (k c)", b=BATCH, h=HALVES)
        v_group = v_dram[:, :, :, :]
        o_group = o_dram[:, :, :].rearrange("(g j) r t -> g j r t", j=GH)
        rden_dram = nc.dram_tensor("rden_scratch", [BATCH * HEADS, SEQ], F32)
        den_half = o_dram[:, :, :].rearrange("n r (h t) -> h n r t", h=HALVES)[:, :, HD, :]
        rden_half = rden_dram[:, :].rearrange("n (h t) -> h n t", h=HALVES)
        rden_chunk = rden_dram[:, :].rearrange("(b j) (h t) -> b h j t", b=BATCH, h=HALVES)
        o_chunk = o_dram[:, :, :].rearrange("(b j) r (h t) -> b h j r t", b=BATCH, h=HALVES)

        ident = sb("ident", [P, P])
        earlier = sb("earlier", [P, EXPERTS, EXPERTS])
        corr = sb("corr", [P, EXPERTS])
        proj_bias = sb("proj_bias", [P, DIM])
        w_in = sb("w_in", [P, HIDDEN])
        w_out = sb("w_out", [P, HT, DIM])
        gate_t = sb("gate_t", [P, P])
        qkv_t = sb("qkv_t", [P, 3, DIM])
        rot_t = sb("rot_t", [P, 2, DIM])
        proj_t = sb("proj_t", [P, DIM])
        headsum = sb("headsum", [P, HEADS], BF16)
        norm_max = sb("norm_max", [HEADS, 2, CHUNKS])
        bound_ok = sb("bound_ok", [1, 1], mybir.dt.int32)
        head_scale = sb("head_scale", [P, BATCH * HEADS, 3])
        diag = sb("diag", [P, 2, P])
        bias_rows = sb("bias_rows", [P, 2, SEQ], BF16)
        bias_sel = sb("bias_sel", [P, 8])

        w_ready = sem("w_ready")
        c_loaded = sem("c_loaded")

        with nc.Block() as block, ExitStack() as own:
            def tmp(name, shape, dt=F32):
                return own.enter_context(nc.sbuf_tensor(name, shape, dt))
            raw_up = tmp("raw_up", [P, ST, DIM])
            raw_w1 = tmp("raw_w1", [P, 4, LATENT])
            raw_w2 = tmp("raw_w2", [LATENT, EXPERTS, INTER])
            raw_fc1 = tmp("raw_fc1", [LATENT, DIM])
            raw_fc2 = tmp("raw_fc2", [P, LATENT])
            raw_down = tmp("raw_down", [P, SHARED])
            raw_gate = tmp("raw_gate", [EXPERTS, DIM])
            raw_qkv = tmp("raw_qkv", [P, 3, DIM])
            raw_proj = tmp("raw_proj", [P, DIM])
            w1_t = tmp("w1_t", [LATENT, EXPERTS * INTER])
            fc2_t = tmp("fc2_t", [LATENT, DIM])
            headsum_f32 = tmp("headsum_f32", [P, HEADS])
            bias_f32 = tmp("bias_f32", [P, 2, SEQ])
            slope8 = tmp("slope8", [P, BATCH * HEADS])
            part_hi = tmp("part_hi", [P, BATCH * HEADS], BF16)
            part_mid = tmp("part_mid", [P, BATCH * HEADS], BF16)
            part_low = tmp("part_low", [P, BATCH * HEADS], BF16)
            rest1 = tmp("rest1", [P, BATCH * HEADS])
            rest2 = tmp("rest2", [P, BATCH * HEADS])
            bank = [own.enter_context(nc.psum_tensor(f"prep{i}", [P, CHUNK], F32)) for i in range(8)]
            prep_mm, prep_cp, prep_v = sem("prep_mm"), sem("prep_cp"), sem("prep_v")
            slopes = io["L0_attn_slopes"].rearrange("(a h) -> a h", a=1)
            br = slice(BIAS_ROW, FULL_K)

            loads = [
                (ident[:, :], consts["ident"]),
                (raw_up[:, :, :], io["L0_ffn_up_w"].rearrange("(t p) c -> p t c", p=P)),
                (raw_w1[:, :, :], io["L0_ffn_w1"].rearrange("(t e) i l -> (e i) t l", e=2)),
                (raw_w2[:, :, :], io["L0_ffn_w2"].rearrange("e l i -> l e i")),
                (raw_fc1[:, :], io["L0_ffn_fc1_w"]),
                (raw_fc2[:, :], io["L0_ffn_fc2_w"]),
                (raw_down[:, :], io["L0_ffn_down_w"]),
                (raw_gate[:, :], io["L0_ffn_gate"]),
                (raw_qkv[:, :, :], io["L0_attn_qkv_w"].rearrange("(s p) c -> p s c", p=P)),
                (raw_proj[:, :], io["L0_attn_proj_w"]),
                (earlier[:, :, :], consts["earlier"].rearrange("p (a b) -> p a b", a=EXPERTS)),
                (corr[:, :], io["L0_ffn_corr_bias"].rearrange("(a h) -> a h", a=1).broadcast_to([P, EXPERTS])),
                (proj_bias[:, :], io["L0_attn_proj_b"].rearrange("(a h) -> a h", a=1).broadcast_to([P, DIM])),
                (slope8[:, :].rearrange("p (b h) -> p b h", b=BATCH), slopes.unsqueeze(1).broadcast_to([P, BATCH, HEADS])),
                (diag[:, :, :], consts["diag"]),
                (headsum_f32[:, :], consts["headsum"]),
                (bias_f32[br, :, :], consts["biasrows"]),
                (bias_sel[br, :], consts["biassel"]),
            ]

            @block.sync
            def _(sp):
                for dst, src in loads:
                    sp.dma_start(dst, src).then_inc(c_loaded, 16)

            @block.tensor
            def _(pe):
                pe.wait_ge(c_loaded, 16 * len(loads))
                tr = nc.tensor.transpose
                for t in range(4):
                    tr(bank[0][:, t * P:(t + 1) * P], raw_up[:, t, :], ident[:, :])
                    tr(bank[1][0:LATENT, t * P:(t + 1) * P], raw_w1[:, t, :], ident[:, :])
                    tr(bank[2][:, t * P:(t + 1) * P], raw_down[:, t * P:(t + 1) * P], ident[:, :])
                tr(bank[3][0:LATENT, 0:P], raw_fc2[:, :], ident[:, :])
                tr(bank[3][:, P:P + EXPERTS], raw_gate[:, :], ident[0:EXPERTS, 0:EXPERTS])
                tr(bank[3][:, 2 * P:3 * P], raw_proj[:, :], ident[:, :])
                for s in range(3):
                    last = tr(bank[4][:, s * P:(s + 1) * P], raw_qkv[:, s, :], ident[:, :])
                last.then_inc(prep_mm, 1)
                pe.wait_ge(prep_cp, 1)
                nc.tensor.matmul(bank[5][:, :], raw_fc1[:, :], w1_t[:, :], start=True, stop=True)
                for t in range(4):
                    last = nc.tensor.matmul(bank[6][:, t * P:(t + 1) * P],
                                            raw_w2[:, 2 * t:2 * t + 2, :].rearrange("l e i -> l (e i)"),
                                            fc2_t[:, :], start=True, stop=True)
                last.then_inc(prep_mm, 1)

            @block.vector
            def _(dve):
                v = nc.vector
                dve.wait_ge(prep_mm, 1)
                v.tensor_copy(w1_t[:, :], bank[1][0:LATENT, :])
                v.tensor_copy(fc2_t[:, :], bank[3][0:LATENT, 0:P]).then_inc(prep_cp, 1)
                v.tensor_copy(w_in[:, 0:SHARED], bank[0][:, :])
                v.tensor_copy(w_out[:, 0:ST, :], bank[2][:, :].rearrange("p (t n) -> p t n", n=DIM))
                v.memset(gate_t[:, EXPERTS:P], 0.0)
                v.tensor_copy(gate_t[:, 0:EXPERTS], bank[3][:, P:P + EXPERTS])
                v.tensor_copy(proj_t[:, :], bank[3][:, 2 * P:3 * P])
                v.tensor_copy(qkv_t[:, :, :], bank[4][:, 0:3 * P].rearrange("p (s n) -> p s n", n=DIM))
                src = bank[4][:, 0:2 * P].rearrange("p (s d) -> p s d", d=HD)
                dst = rot_t[:, :, :].rearrange("p s (h d) -> p (s h) d", d=HD)
                v.tensor_scalar(dst[:, :, 0:HALF], src[:, :, HALF:HD], -1.0, None, ALU.mult)
                v.tensor_copy(dst[:, :, HALF:HD], src[:, :, 0:HALF])
                v.tensor_copy(bias_rows[br, :, :], bias_f32[br, :, :])
                v.tensor_copy(headsum[:, :], headsum_f32[:, :])
                v.tensor_scalar(slope8[:, :], slope8[:, :], 8.0, None, ALU.mult).then_inc(prep_v, 1)
                dve.wait_ge(prep_v, 1)
                v.tensor_copy(part_hi[:, :], slope8[:, :]).then_inc(prep_v, 1)
                dve.wait_ge(prep_v, 2)
                v.tensor_tensor(rest1[:, :], slope8[:, :], part_hi[:, :], ALU.subtract).then_inc(prep_v, 1)
                dve.wait_ge(prep_v, 3)
                v.tensor_copy(part_mid[:, :], rest1[:, :]).then_inc(prep_v, 1)
                dve.wait_ge(prep_v, 4)
                v.tensor_tensor(part_low[:, :], rest1[:, :], part_mid[:, :], ALU.subtract).then_inc(prep_v, 1)
                v.memset(head_scale[:, :, 1:3], 0.0)
                v.tensor_copy(head_scale[:, :, 0], slope8[:, :]).then_inc(prep_v, 1)
                dve.wait_ge(prep_v, 6)
                done = 6
                for side in range(2):
                    col = 4 * side
                    v.tensor_scalar(rest2[br, :], part_hi[br, :], bias_sel[br, col:col + 1],
                                    bias_sel[br, col + 3:col + 4], ALU.mult, ALU.add).then_inc(prep_v, 1)
                    for i, part in enumerate((part_mid, part_low)):
                        done += 1
                        dve.wait_ge(prep_v, done)
                        dst = (rest1, head_scale[:, :, 1 + side])[i]
                        src = (rest2, rest1)[i]
                        v.scalar_tensor_tensor(out=dst[br, :], in0=part[br, :],
                                               scalar=bias_sel[br, col + 1 + i:col + 2 + i],
                                               in1=src[br, :], op0=ALU.mult, op1=ALU.add).then_inc(prep_v, 1)
                    done += 1
                    dve.wait_ge(prep_v, done)
                dve.wait_ge(prep_mm, 2)
                v.tensor_copy(w_in[:, SHARED:HIDDEN], bank[5][:, :])
                v.tensor_copy(w_out[:, ST:HT, :],
                              bank[6][:, :].rearrange("p (t n) -> p t n", n=DIM)).then_inc(w_ready, 1)

        token_pass(nc, sem, 1, locals())
        bound_shift(nc, sem, locals())
        exact_maxima(nc, sem, locals())
        attention(nc, sem, locals())
        token_pass(nc, sem, 2, locals())


def token_pass(nc, sem, number, env):
    first = number == 1
    ident, earlier, corr = env["ident"], env["earlier"], env["corr"]
    w_in, w_out, gate_t = env["w_in"], env["w_out"], env["gate_t"]
    headsum = env["headsum"]
    qkv_t, rot_t, proj_t, proj_bias = env["qkv_t"], env["rot_t"], env["proj_t"], env["proj_bias"]
    RT = HT - ST

    with ExitStack() as own:
        def sb(name, shape, dt=F32):
            return own.enter_context(nc.sbuf_tensor(f"p{number}_{name}", shape, dt))

        def ps(name, shape):
            return own.enter_context(nc.psum_tensor(f"p{number}_{name}", shape, F32))

        def s(name):
            return sem(f"p{number}_{name}")

        x = sb("x", [P, 2, TILES, DIM])
        stats = sb("stats", [P, 2, TILES, 6])
        mean2, mean, apart, apart2, var_n, var_in = (
            sb(name, [P, 2, TILES]) for name in ("mean2", "mean", "apart", "apart2", "var_n", "var_in"))
        veps = sb("veps", [P, 2, TILES])
        rstd = sb("rstd", [P, 2, TILES])
        minus_half = sb("minus_half", [P, TILES])
        xn = sb("xn", [P, TILES, DIM])
        xn_t = sb("xn_t", [P, 2, CHUNK])
        logit_t = sb("logit_t", [P, CHUNK])
        en = sb("en", [P, TILES, EXPERTS])
        en1 = sb("en1", [P, TILES, EXPERTS])
        score = sb("score", [P, TILES, EXPERTS])
        sfc = sb("sfc", [P, TILES, EXPERTS])
        pair_sum = sb("pair_sum", [P, TILES * GROUPS, 6])
        gsum = sb("gsum", [P, TILES, GROUPS])
        gmask = sb("gmask", [P, TILES, GROUPS])
        kept = sb("kept", [P, TILES, EXPERTS])
        above = sb("above", [P, TILES, EXPERTS * EXPERTS])
        equal = sb("equal", [P, TILES, EXPERTS * EXPERTS])
        rank = sb("rank", [P, TILES, EXPERTS])
        chosen = sb("chosen", [P, TILES, EXPERTS])
        csum = sb("csum", [P, TILES])
        csum1 = sb("csum1", [P, TILES])
        crec = sb("crec", [P, TILES])
        coef = sb("coef", [P, TILES, EXPERTS])
        half = sb("half", [P, TILES, EXPERTS])
        coef_root = sb("coef_root", [P, TILES, EXPERTS])
        coef_wide = sb("coef_wide", [P, TILES, EXPERTS * INTER])
        relu = sb("relu", [P, HT, CHUNK])
        scaled = sb("scaled", [P, RT, CHUNK])
        hid = sb("hid", [P, HT, CHUNK])
        res = sb("res", [P, TILES, DIM])

        ps_t = ps("ps_t", [P, CHUNK])
        ps_g = ps("ps_g", [P, CHUNK])
        ps_h = ps("ps_h", [P, 2, CHUNK])
        ps_c = ps("ps_c", [P, CHUNK])
        ps_o = ps("ps_o", [P, TILES, DIM])
        ps_q = ps("ps_q", [P, 2, CHUNK])

        x_loaded = [s("x_loaded0"), s("x_loaded1")]
        half_set = s("half_set")
        rstd_ready = [s("rstd_ready"), s("rstd2_ready")]
        norm_step, norm_ready, turned, xt_ready = s("norm_step"), s("norm_ready"), s("turned"), s("xt_ready")
        gate_made, gate_copied, gate_turned, gate_exp = s("gate_made"), s("gate_copied"), s("gate_turned"), s("gate_exp")
        route_step, coef_ready, root_ready, wide_ready = (
            s("route_step"), s("coef_ready"), s("root_ready"), s("wide_ready"))
        hid_made, relu_ready = s("hid_made"), s("relu_ready")
        spread, scaled_ready = s("spread"), s("scaled_ready")
        sq_pool, sq_act = s("squared_by_pool"), s("squared_by_act")
        ffn_made, res_ready, res_stored = s("ffn_made"), s("res_ready"), s("res_stored")

        if first:
            xn2 = sb("xn2", [P, TILES, DIM])
            xn2_t = sb("xn2_t", [P, CHUNK])
            rope = sb("rope", [P, 4, SEQ])
            turn_a = sb("turn_a", [P, 2, CHUNK])
            turn_b = sb("turn_b", [P, 2, CHUNK])
            roped = sb("roped", [P, 2, CHUNK])
            left = sb("left", [P, 2, CHUNK])
            x_ln = sb("x_ln", [P, 2, TILES, DIM])
            squares = sb("squares", [P, 2, CHUNK], BF16)
            parts = sb("parts", [P, 2, PARTS, CHUNK], BF16)
            v_ext = sb("v_ext", [P, HG, TILES, GH * VW])
            rope_loaded, ones_set = s("rope_loaded"), s("ones_set")
            norm2_step, norm2_ready, turned2, xt2_ready = s("norm2_step"), s("norm2_ready"), s("turned2"), s("xt2_ready")
            squares_ready, norms_made, norms_read = s("squares_ready"), s("norms_made"), s("norms_read")
            qk_made, turn_ready, rope_step = s("qk_made"), s("turn_ready"), s("rope_step")
            v_made, v_ready, v_stored = s("v_made"), s("v_ready"), s("v_stored")
            ln_loaded = [s("ln_loaded0"), s("ln_loaded1")]
            k_sum, k_hi, k_rest, k_mid = s("k_sum"), s("k_hi"), s("k_rest"), s("k_mid")
            parts_ready, parts_stored = [s("q_parts"), s("k_parts")], [s("q_stored"), s("k_stored")]
        else:
            x_in = sb("x_in", [P, 2, TILES, DIM])
            x_biased = sb("x_biased", [P, TILES, DIM])
            o_in = sb("o_in", [P, 2, CHUNK])
            den_all = sb("den_all", [P, CHUNK])
            den_rec = sb("den_rec", [P, CHUNK])
            rden = sb("rden", [P, 2, CHUNK])
            o_norm = sb("o_norm", [P, CHUNK])
            den_loaded, den_turned, den_stored = s("den_loaded"), s("den_turned"), s("den_stored")
            merged = s("merged")
            merge_step, o_ready, proj_made = s("merge_step"), s("o_ready"), s("proj_made")

        block = own.enter_context(nc.Block())

        @block.sync
        def _(sp):
            def load(c):
                half = c.half
                if first:
                    sp.dma_start(x_ln[:, half], env["x_tiles"][c.n]).then_inc(ln_loaded[half], 16)
                else:
                    sp.dma_start(x_in[:, half], env["x1_tiles"][c.n]).then_inc(x_loaded[half], 16)
                    sp.dma_start(o_in[:, half], env["o_chunk"][c.batch, half][:, 0:HD, :]).then_inc(x_loaded[half], 16)
                    sp.dma_start(rden[:, half], env["rden_chunk"][c.batch, half].unsqueeze(1)
                                 .broadcast_to([HEADS, HD, CHUNK])).then_inc(x_loaded[half], 16)

            def load_residual(c):
                sp.dma_start(x[:, c.half], env["x_tiles"][c.n]).then_inc(x_loaded[c.half], 16)

            def store_qkv(c):
                sp.wait_ge(v_ready, c.n + 1)
                for g in range(HG):
                    sp.dma_start(env["v_chunk"][c.batch, c.half][:, g], v_ext[:, g].rearrange("p t c -> p (t c)")
                                 ).then_inc(v_stored, 16)
                for side in range(2):
                    sp.wait_ge(parts_ready[side], c.n + 1)
                    sp.dma_start(env["part_chunk"][side][c.batch, c.half], parts[:, side]
                                 ).then_inc(parts_stored[side], 16)

            def lead():
                if first:
                    sp.dma_start(rope[:, :, :], env["consts"]["rope"]).then_inc(rope_loaded, 16)
                else:
                    for h in range(HALVES):
                        sp.dma_start(den_all[64 * h:64 * h + 64, :], env["den_half"][h]).then_inc(den_loaded, 16)
                    sp.wait_ge(den_turned, 1)
                    for h in range(HALVES):
                        sp.dma_start(env["rden_half"][h], den_rec[64 * h:64 * h + 64, :]).then_inc(den_stored, 16)
                    sp.wait_ge(den_stored, 16 * HALVES)
                load(Chunk(0, 0))
                load(Chunk(0, 1))
                if first:
                    load_residual(Chunk(0, 0))
                    load_residual(Chunk(0, 1))

            def body(c, end):
                if not end and c.loads_ahead:
                    sp.wait_ge(norm_ready if first else merged, c.n + 1)
                    load(c.next(2))
                if first and c.at_least >= 1:
                    store_qkv(c.next(-1))
                sp.wait_ge(res_ready, c.n + 1)
                sp.dma_start((env["x1_tiles"] if first else env["out_tiles"])[c.n], res[:, :, :]
                             ).then_inc(res_stored, 16)
                if first and not end and c.loads_ahead:
                    load_residual(c.next(2))

            def tail(c):
                if first:
                    store_qkv(c)
                    sp.wait_ge(v_stored, 16 * HG * CHUNKS)
                    for side in range(2):
                        sp.wait_ge(parts_stored[side], 16 * CHUNKS)
                sp.wait_ge(res_stored, 16 * CHUNKS)

            in_chunks(sp, lead, body, tail)

        @block.tensor
        def _(pe):
            def project(c):
                pe.wait_ge(o_ready, c.n + 1)
                if c.at_least >= 1:
                    pe.wait_ge(merge_step, c.n)
                for t in range(TILES):
                    last = nc.tensor.matmul(ps_q[:, 0, t * P:(t + 1) * P], o_norm[:, t * P:(t + 1) * P],
                                            proj_t[:, :], start=True, stop=True)
                last.then_inc(proj_made, 1)

            def turn(c):
                pe.wait_ge(norm_ready, c.n + 1)
                if c.at_least >= 1:
                    pe.wait_ge(xt_ready, c.n)
                if first and c.at_least >= 3:
                    pe.wait_ge(xt2_ready, c.n - 2)
                for t in range(TILES):
                    last = nc.tensor.transpose(ps_t[:, t * P:(t + 1) * P], xn[:, t, :], ident[:, :])
                last.then_inc(turned, 1)

            def gate(c):
                pe.wait_ge(xt_ready, c.n + 1)
                if c.at_least >= 1:
                    pe.wait_ge(gate_exp, c.n)
                nc.tensor.matmul(ps_g[:, :], gate_t[:, :], xn_t[:, c.half, :],
                                 start=True, stop=True).then_inc(gate_made, 1)

            def turn_gate(c):
                pe.wait_ge(gate_copied, c.n + 1)
                for t in range(TILES):
                    last = nc.tensor.transpose(ps_g[:, t * P:(t + 1) * P], logit_t[:, t * P:(t + 1) * P],
                                               ident[:, :])
                last.then_inc(gate_turned, 1)

            def hidden(c, m):
                if not (c.at_least == 0 and m < 2):
                    pe.wait_ge(relu_ready, HT * c.n + m - 1)
                nc.tensor.matmul(ps_h[:, m % 2, :], w_in[:, m * P:(m + 1) * P], xn_t[:, c.half, :],
                                 start=True, stop=True).then_inc(hid_made, 1)

            def spread_coef(c, m):
                if not (c.at_least == 0 and m == 0):
                    pe.wait_ge(scaled_ready, RT * c.n + m)
                for t in range(TILES):
                    last = nc.tensor.transpose(ps_c[:, t * P:(t + 1) * P],
                                               coef_wide[:, t, m * P:(m + 1) * P], ident[:, :])
                last.then_inc(spread, 1)

            def outputs(c):
                if c.at_least >= 1:
                    pe.wait_ge(res_ready, c.n)
                for t in range(TILES):
                    for m in range(HT):
                        if t == 0:
                            if m < ST:
                                pe.wait_ge(sq_pool, ST * c.n + m + 1)
                            else:
                                pe.wait_ge(sq_act, RT * c.n + m - ST + 1)
                        last = nc.tensor.matmul(ps_o[:, t, :], hid[:, m, t * P:(t + 1) * P], w_out[:, m, :],
                                                start=(m == 0), stop=(m == HT - 1))
                last.then_inc(ffn_made, 1)

            def qkv(c, turns):
                pe.wait_ge(norm2_ready, c.n + 1)
                pe.wait_ge(xt_ready, turns)
                if c.at_least >= 1:
                    pe.wait_ge(xt2_ready, c.n)
                for t in range(TILES):
                    last = nc.tensor.transpose(ps_t[:, t * P:(t + 1) * P], xn2[:, t, :], ident[:, :])
                last.then_inc(turned2, 1)
                pe.wait_ge(xt2_ready, c.n + 1)
                for i, w in enumerate((qkv_t[:, 0, :], rot_t[:, 0, :], qkv_t[:, 1, :], rot_t[:, 1, :])):
                    if i == 0 and c.at_least >= 1:
                        pe.wait_ge(norms_read, c.n)
                    elif i > 1:
                        pe.wait_ge(turn_ready, 4 * c.n + i - 1)
                    nc.tensor.matmul(ps_q[:, i % 2, :], w, xn2_t[:, :], start=True, stop=True).then_inc(qk_made, 1)
                pe.wait_ge(turn_ready, 4 * c.n + 3)
                for t in range(TILES):
                    last = nc.tensor.matmul(ps_q[:, 0, t * P:(t + 1) * P], xn2_t[:, t * P:(t + 1) * P],
                                            qkv_t[:, 2, :], start=True, stop=True)
                last.then_inc(v_made, 1)

            def norms(c):
                pe.wait_ge(squares_ready, c.n + 1)
                pe.wait_ge(v_ready, c.n + 1)
                pe.wait_ge(turn_ready, 4 * c.n + 4)
                for side in range(2):
                    last = nc.tensor.matmul(ps_q[0:HEADS, side, :], headsum[:, :], squares[:, side, :],
                                            start=True, stop=True)
                last.then_inc(norms_made, 1)

            def lead():
                pe.wait_ge(env["w_ready"], 1)
                if not first:
                    project(Chunk(0, 0))
                turn(Chunk(0, 0))
                gate(Chunk(0, 0))
                turn_gate(Chunk(0, 0))

            def body(c, end):
                if not first and not end:
                    project(c.next())
                for m in range(ST):
                    hidden(c, m)
                if not end:
                    turn(c.next())
                for m in range(RT):
                    hidden(c, ST + m)
                    if m == 0:
                        pe.wait_ge(wide_ready, c.n + 1)
                    spread_coef(c, m)
                if not end:
                    gate(c.next())
                if first and c.at_least >= 1:
                    qkv(c.next(-1), c.n + (1 if end else 2))
                if not end:
                    turn_gate(c.next())
                outputs(c)
                if first and c.at_least >= 1:
                    norms(c.next(-1))

            def tail(c):
                if first:
                    qkv(c, CHUNKS)
                    norms(c)

            in_chunks(pe, lead, body, tail)

        @block.scalar
        def _(act):
            def copy(dst, src):
                return nc.scalar.activation(dst, src, ACT.Copy)

            def take_xt(c):
                act.wait_ge(turned, c.n + 1)
                if c.at_least >= 2:
                    act.wait_ge(hid_made, HT * (c.n - 1))
                copy(xn_t[:, c.half, :], ps_t[:, :]).then_inc(xt_ready, 1)

            def take_logits(c):
                act.wait_ge(gate_made, c.n + 1)
                if c.at_least >= 1:
                    act.wait_ge(gate_turned, c.n)
                copy(logit_t[:, :], ps_g[:, :]).then_inc(gate_copied, 1)

            def exp_logits(c):
                act.wait_ge(gate_turned, c.n + 1)
                if c.at_least >= 1:
                    act.wait_ge(coef_ready, c.n)
                nc.scalar.activation(en[:, :, :], ps_g[:, :].rearrange("p (t e) -> p t e", e=P)[:, :, 0:EXPERTS],
                                     ACT.Exp, scale=-1.0).then_inc(gate_exp, 1)

            def widen(c):
                act.wait_ge(root_ready, c.n + 1)
                if c.at_least >= 1:
                    act.wait_ge(spread, RT * c.n)
                for t in range(TILES):
                    last = copy(coef_wide[:, t, :].rearrange("p (e i) -> p e i", i=INTER),
                                coef_root[:, t, :].unsqueeze(2).broadcast_to([P, EXPERTS, INTER]))
                last.then_inc(wide_ready, 1)

            def relus(c, m):
                act.wait_ge(hid_made, HT * c.n + m + 1)
                if c.at_least >= 1:
                    if m < ST:
                        act.wait_ge(sq_pool, ST * (c.n - 1) + m + 1)
                    else:
                        act.wait_ge(scaled_ready, RT * (c.n - 1) + m - ST + 1)
                nc.scalar.activation(relu[:, m, :], ps_h[:, m % 2, :], ACT.Relu).then_inc(relu_ready, 1)

            def squares_of(c, m):
                act.wait_ge(scaled_ready, RT * c.n + m + 1)
                if c.at_least >= 1:
                    act.wait_ge(ffn_made, c.n)
                nc.scalar.activation(hid[:, ST + m, :], scaled[:, m, :], ACT.Square).then_inc(sq_act, 1)

            def v_of(g):
                return v_ext[:, g, :, :].rearrange("p t (j c) -> p t j c", c=VW)[:, :, :, 0:HD]

            def take_xt2(c):
                act.wait_ge(turned2, c.n + 1)
                if c.at_least >= 1:
                    act.wait_ge(v_made, c.n)
                copy(xn2_t[:, :], ps_t[:, :]).then_inc(xt2_ready, 1)

            def take_v(c):
                act.wait_ge(v_made, c.n + 1)
                if c.at_least >= 1:
                    act.wait_ge(v_stored, 16 * HG * c.n)
                else:
                    act.wait_ge(ones_set, 1)
                v_ps = ps_q[:, 0, :].rearrange("p (t g j c) -> p g t j c", t=TILES, g=HG, c=HD)
                for g in range(HG):
                    last = copy(v_of(g), v_ps[:, g])
                last.then_inc(v_ready, 1)

            def k_parts(c):
                act.wait_ge(k_sum, c.n + 1)
                if c.at_least >= 1:
                    act.wait_ge(parts_stored[1], 16 * c.n)
                copy(parts[:, 1, 0, :], roped[:, 1, :]).then_inc(k_hi, 1)
                act.wait_ge(k_rest, c.n + 1)
                copy(parts[:, 1, 1, :], left[:, 1, :]).then_inc(k_mid, 1)

            def body(c, end):
                for m in range(ST):
                    relus(c, m)
                if not end:
                    take_xt(c.next())
                for m in range(RT):
                    relus(c, ST + m)
                    if m >= 1:
                        squares_of(c, m - 1)
                squares_of(c, RT - 1)
                if not end:
                    take_logits(c.next())
                if first and c.at_least >= 1:
                    take_xt2(c.next(-1))
                    take_v(c.next(-1))
                if not end:
                    exp_logits(c.next())
                if first and c.at_least >= 1:
                    k_parts(c.next(-1))
                if not end:
                    widen(c.next())

            def lead():
                take_xt(Chunk(0, 0))
                take_logits(Chunk(0, 0))
                exp_logits(Chunk(0, 0))
                widen(Chunk(0, 0))

            def tail(c):
                if first:
                    take_xt2(c)
                    take_v(c)
                    k_parts(c)

            in_chunks(act, lead, body, tail)

        @block.gpsimd
        def _(pool):
            def power(c, which, step):
                pool.wait_ge(step, 4 * c.n + 4)
                nc.gpsimd.tensor_tensor(rstd[:, which, :], veps[:, which, :], minus_half[:, :],
                                        ALU.pow).then_inc(rstd_ready[which], 1)

            def root(c):
                pool.wait_ge(coef_ready, c.n + 1)
                if c.at_least >= 1:
                    pool.wait_ge(wide_ready, c.n)
                nc.gpsimd.tensor_tensor(coef_root[:, :, :], coef[:, :, :], half[:, :, :],
                                        ALU.pow).then_inc(root_ready, 1)

            def square(c, m):
                pool.wait_ge(relu_ready, HT * c.n + m + 1)
                if c.at_least >= 1:
                    pool.wait_ge(ffn_made, c.n)
                nc.gpsimd.tensor_tensor(hid[:, m, :], relu[:, m, :], relu[:, m, :], ALU.mult).then_inc(sq_pool, 1)

            def k_side(c):
                pool.wait_ge(turn_ready, 4 * c.n + 4)
                nc.gpsimd.tensor_tensor(roped[:, 1, :], turn_a[:, 1, :], turn_b[:, 1, :], ALU.add).then_inc(k_sum, 1)
                pool.wait_ge(k_hi, c.n + 1)
                nc.gpsimd.tensor_tensor(left[:, 1, :], roped[:, 1, :], parts[:, 1, 0, :],
                                        ALU.subtract).then_inc(k_rest, 1)
                pool.wait_ge(k_mid, c.n + 1)
                nc.gpsimd.tensor_tensor(parts[:, 1, 2, :], left[:, 1, :], parts[:, 1, 1, :],
                                        ALU.subtract).then_inc(parts_ready[1], 1)

            def square_qk(c):
                pool.wait_ge(rope_step, 4 * c.n + 1)
                pool.wait_ge(k_sum, c.n + 1)
                if c.at_least >= 1:
                    pool.wait_ge(norms_made, c.n)
                nc.gpsimd.tensor_tensor(squares[:, :, :], roped[:, :, :], roped[:, :, :],
                                        ALU.mult).then_inc(squares_ready, 1)

            def lead():
                if first:
                    nc.gpsimd.memset(v_ext[:, :, :, :], 1.0).then_inc(ones_set, 1)
                nc.gpsimd.memset(minus_half[:, :], -0.5).then_inc(half_set, 1)
                nc.gpsimd.memset(half[:, :, :], 0.5).then_inc(half_set, 1)
                pool.wait_ge(half_set, 2)
                power(Chunk(0, 0), 0, norm_step)
                root(Chunk(0, 0))

            def body(c, end):
                if not end:
                    power(c.next(), 0, norm_step)
                for m in range(ST):
                    square(c, m)
                if first and c.at_least >= 1:
                    k_side(c.next(-1))
                if not end:
                    root(c.next())
                if first and c.at_least >= 1:
                    square_qk(c.next(-1))
                if first:
                    power(c, 1, norm2_step)

            def tail(c):
                if first:
                    k_side(c)
                    square_qk(c)

            in_chunks(pool, lead, body, tail)

        @block.vector
        def _(dve):
            v = nc.vector

            def layernorm(src, dst, which, step, n):
                at = 4 * n
                for t in range(TILES):
                    last = v.bn_stats(stats[:, which, t, :], src[:, t, :])
                last.then_inc(step, 1)
                dve.wait_ge(step, at + 1)
                even, odd = stats[:, which, :, 1], stats[:, which, :, 4]
                v.tensor_tensor(mean2[:, which, :], even, odd, ALU.add)
                v.tensor_tensor(apart[:, which, :], even, odd, ALU.subtract)
                v.tensor_tensor(var_n[:, which, :], stats[:, which, :, 2], stats[:, which, :, 5],
                                ALU.add).then_inc(step, 1)
                dve.wait_ge(step, at + 2)
                v.tensor_scalar(mean[:, which, :], mean2[:, which, :], 0.5, None, ALU.mult)
                v.tensor_tensor(apart2[:, which, :], apart[:, which, :], apart[:, which, :], ALU.mult)
                v.tensor_scalar(var_in[:, which, :], var_n[:, which, :], 1.0 / DIM, EPS, ALU.mult,
                                ALU.add).then_inc(step, 1)
                dve.wait_ge(step, at + 3)
                v.scalar_tensor_tensor(out=veps[:, which, :], in0=apart2[:, which, :], scalar=0.25,
                                       in1=var_in[:, which, :], op0=ALU.mult, op1=ALU.add).then_inc(step, 1)
                dve.wait_ge(rstd_ready[which], n + 1)
                for t in range(TILES):
                    last = v.tensor_scalar(dst[:, t, :], src[:, t, :], mean[:, which, t:t + 1],
                                           rstd[:, which, t:t + 1], ALU.subtract, ALU.mult)
                return last

            def normalise_o(c):
                dve.wait_ge(x_loaded[c.half], 48 * c.seen)
                if c.at_least >= 1:
                    dve.wait_ge(proj_made, c.n)
                    dve.wait_ge(merge_step, c.n)
                v.tensor_tensor(o_norm[:, :], o_in[:, c.half, :], rden[:, c.half, :], ALU.mult).then_inc(o_ready, 1)
                v.tensor_tensor(x_biased[:, :, :], x_in[:, c.half],
                                proj_bias[:, :].unsqueeze(1).broadcast_to([P, TILES, DIM]),
                                ALU.add).then_inc(merged, 1)

            def merge(c):
                dve.wait_ge(merged, c.n + 1)
                dve.wait_ge(proj_made, c.n + 1)
                if c.at_least >= 2:
                    dve.wait_ge(res_ready, c.n - 1)
                v.tensor_tensor(x[:, c.half], x_biased[:, :, :], ps_q[:, 0, :].rearrange("p (t c) -> p t c", c=DIM),
                                ALU.add).then_inc(merge_step, 1)
                dve.wait_ge(merge_step, c.n + 1)

            def norm(c):
                if first:
                    dve.wait_ge(ln_loaded[c.half], 16 * c.seen)
                if c.at_least >= 1:
                    dve.wait_ge(turned, c.n)
                layernorm(x_ln[:, c.half] if first else x[:, c.half], xn, 0, norm_step, c.n).then_inc(norm_ready, 1)

            def route(c):
                r = ROUTE_STEPS * c.n
                dve.wait_ge(gate_exp, c.n + 1)
                v.tensor_scalar(en1[:, :, :], en[:, :, :], 1.0, None, ALU.add).then_inc(route_step, 1)
                dve.wait_ge(route_step, r + 1)
                v.reciprocal(score[:, :, :], en1[:, :, :]).then_inc(route_step, 1)
                dve.wait_ge(route_step, r + 2)
                v.tensor_tensor(sfc[:, :, :], score[:, :, :], corr[:, :].unsqueeze(1).broadcast_to(
                    [P, TILES, EXPERTS]), ALU.add).then_inc(route_step, 1)
                dve.wait_ge(route_step, r + 3)
                four = sfc[:, :, :].rearrange("p t (g e) -> p (t g) e", e=PER_GROUP)
                v.tensor_tensor(pair_sum[:, :, 0:3], four[:, :, 0:3], four[:, :, 1:4], ALU.add)
                v.tensor_tensor(pair_sum[:, :, 3:5], four[:, :, 0:2], four[:, :, 2:4], ALU.add)
                v.tensor_tensor(pair_sum[:, :, 5:6], four[:, :, 0:1], four[:, :, 3:4],
                                ALU.add).then_inc(route_step, 1)
                dve.wait_ge(route_step, r + 4)
                v.tensor_reduce(gsum[:, :, :].rearrange("p t g -> p (t g)"), pair_sum[:, :, :],
                                AX.X, ALU.max).then_inc(route_step, 1)
                dve.wait_ge(route_step, r + 5)
                v.tensor_tensor(gmask[:, :, 0:1], gsum[:, :, 0:1], gsum[:, :, 1:2], ALU.is_ge)
                v.tensor_tensor(gmask[:, :, 1:2], gsum[:, :, 1:2], gsum[:, :, 0:1],
                                ALU.is_gt).then_inc(route_step, 1)
                dve.wait_ge(route_step, r + 6)
                v.tensor_tensor(kept[:, :, :].rearrange("p t (g e) -> p (t g) e", e=PER_GROUP), four,
                                gmask[:, :, :].rearrange("p t g -> p (t g)").unsqueeze(2).broadcast_to(
                                    [P, TILES * GROUPS, PER_GROUP]), ALU.mult).then_inc(route_step, 1)
                dve.wait_ge(route_step, r + 7)
                wide = [P, TILES, EXPERTS, EXPERTS]
                mine = kept[:, :, :].unsqueeze(3).broadcast_to(wide)
                other = kept[:, :, :].unsqueeze(2).broadcast_to(wide)
                above4 = above[:, :, :].rearrange("p t (a b) -> p t a b", a=EXPERTS)
                equal4 = equal[:, :, :].rearrange("p t (a b) -> p t a b", a=EXPERTS)
                v.tensor_tensor(above4, other, mine, ALU.is_gt)
                v.tensor_tensor(equal4, other, mine, ALU.is_equal).then_inc(route_step, 1)
                dve.wait_ge(route_step, r + 8)
                v.tensor_tensor(equal[:, :, :], equal[:, :, :],
                                earlier[:, :, :].rearrange("p a b -> p (a b)").unsqueeze(1).broadcast_to(
                                    [P, TILES, EXPERTS * EXPERTS]), ALU.mult).then_inc(route_step, 1)
                dve.wait_ge(route_step, r + 9)
                v.tensor_tensor(above[:, :, :], above[:, :, :], equal[:, :, :], ALU.add).then_inc(route_step, 1)
                dve.wait_ge(route_step, r + 10)
                v.tensor_reduce(rank[:, :, :], above4, AX.X, ALU.add).then_inc(route_step, 1)
                dve.wait_ge(route_step, r + 11)
                v.scalar_tensor_tensor(out=chosen[:, :, :], in0=rank[:, :, :], scalar=2.0, in1=score[:, :, :],
                                       op0=ALU.is_lt, op1=ALU.mult).then_inc(route_step, 1)
                dve.wait_ge(route_step, r + 12)
                v.tensor_reduce(csum[:, :], chosen[:, :, :], AX.X, ALU.add).then_inc(route_step, 1)
                dve.wait_ge(route_step, r + 13)
                v.tensor_scalar(csum1[:, :], csum[:, :], 1e-20, None, ALU.add).then_inc(route_step, 1)
                dve.wait_ge(route_step, r + 14)
                v.reciprocal(crec[:, :], csum1[:, :]).then_inc(route_step, 1)
                dve.wait_ge(route_step, r + 15)
                if c.at_least >= 1:
                    dve.wait_ge(root_ready, c.n)
                v.tensor_tensor(coef[:, :, :], chosen[:, :, :],
                                crec[:, :].unsqueeze(2).broadcast_to([P, TILES, EXPERTS]),
                                ALU.mult).then_inc(coef_ready, 1)

            def scale(c, m):
                if c.at_least >= 1:
                    dve.wait_ge(sq_act, RT * (c.n - 1) + m + 1)
                dve.wait_ge(relu_ready, HT * c.n + ST + m + 1)
                dve.wait_ge(spread, RT * c.n + m + 1)
                v.tensor_tensor(scaled[:, m, :], relu[:, ST + m, :], ps_c[:, :], ALU.mult).then_inc(scaled_ready, 1)

            def residual(c):
                dve.wait_ge(ffn_made, c.n + 1)
                if first:
                    dve.wait_ge(x_loaded[c.half], 16 * c.seen)
                if c.at_least >= 1:
                    dve.wait_ge(res_stored, 16 * c.n)
                v.scalar_tensor_tensor(out=res[:, :, :], in0=ps_o[:, :, :], scalar=0.5, in1=x[:, c.half],
                                       op0=ALU.mult, op1=ALU.add).then_inc(res_ready, 1)
                if first:
                    dve.wait_ge(res_ready, c.n + 1)
                    if c.at_least >= 1:
                        dve.wait_ge(turned2, c.n)
                    layernorm(res, xn2, 1, norm2_step, c.n).then_inc(norm2_ready, 1)

            def rotary(c):
                at = slice(c.half * CHUNK, (c.half + 1) * CHUNK)
                for side in range(2):
                    if side == 1 and c.at_least >= 1:
                        dve.wait_ge(k_sum, c.n)
                    for i, dst in enumerate((turn_a, turn_b)):
                        dve.wait_ge(qk_made, 4 * c.n + 2 * side + i + 1)
                        v.tensor_tensor(dst[:, side, :], ps_q[:, i, :], rope[:, 2 * side + i, at],
                                        ALU.mult).then_inc(turn_ready, 1)
                dve.wait_ge(turn_ready, 4 * c.n + 2)
                if c.at_least >= 1:
                    dve.wait_ge(squares_ready, c.n)
                v.tensor_tensor(roped[:, 0, :], turn_a[:, 0, :], turn_b[:, 0, :], ALU.add).then_inc(rope_step, 1)
                dve.wait_ge(rope_step, 4 * c.n + 1)
                if c.at_least >= 1:
                    dve.wait_ge(parts_stored[0], 16 * c.n)
                v.tensor_copy(parts[:, 0, 0, :], roped[:, 0, :]).then_inc(rope_step, 1)
                dve.wait_ge(rope_step, 4 * c.n + 2)
                v.tensor_tensor(left[:, 0, :], roped[:, 0, :], parts[:, 0, 0, :], ALU.subtract).then_inc(rope_step, 1)
                dve.wait_ge(rope_step, 4 * c.n + 3)
                v.tensor_copy(parts[:, 0, 1, :], left[:, 0, :]).then_inc(rope_step, 1)
                dve.wait_ge(rope_step, 4 * c.n + 4)
                v.tensor_tensor(parts[:, 0, 2, :], left[:, 0, :], parts[:, 0, 1, :],
                                ALU.subtract).then_inc(parts_ready[0], 1)

            def largest_norms(c):
                dve.wait_ge(norms_made, c.n + 1)
                v.tensor_reduce(env["norm_max"][:, :, bass.ds(c.n, 1)].rearrange("h s c -> h (s c)"), ps_q[0:HEADS, :, :],
                                AX.X, ALU.max).then_inc(norms_read, 1)

            def lead():
                dve.wait_ge(env["w_ready"], 1)
                if not first:
                    dve.wait_ge(den_loaded, 16 * HALVES)
                    v.reciprocal(den_rec[:, :], den_all[:, :]).then_inc(den_turned, 1)
                    normalise_o(Chunk(0, 0))
                    merge(Chunk(0, 0))
                norm(Chunk(0, 0))
                if not first:
                    normalise_o(Chunk(0, 1))
                route(Chunk(0, 0))
                if first:
                    dve.wait_ge(rope_loaded, 16)

            def body(c, end):
                if not end:
                    if not first:
                        merge(c.next())
                    norm(c.next())
                for m in range(RT):
                    scale(c, m)
                if first and c.at_least >= 1:
                    rotary(c.next(-1))
                if not end:
                    route(c.next())
                    if not first and c.loads_ahead:
                        normalise_o(c.next(2))
                residual(c)
                if first and c.at_least >= 1:
                    largest_norms(c.next(-1))

            def tail(c):
                if first:
                    rotary(c)
                    largest_norms(c)

            in_chunks(dve, lead, body, tail)


def load_parts(sp, env, group, q_op, k_op, loaded):
    for a in range(PARTS):
        for b in range(PARTS):
            at = HD * (PARTS * a + b)
            sp.dma_start(q_op[at:at + HD], env["part_group"][0][group, b]).then_inc(loaded, 16)
            sp.dma_start(k_op[at:at + HD], env["part_group"][1][group, a]).then_inc(loaded, 16)


PART_LOADS = 2 * PARTS * PARTS


def fill_bias_row(nc, env, now, ops, n):
    br = slice(BIAS_ROW, FULL_K)
    j, side = divmod(n, 2)
    return nc.vector.tensor_scalar(ops[side][br, j, :], env["bias_rows"][br, side, :],
                                   now[br, j, 1 + side:2 + side], None, ALU.mult)


def fill_bias_rows(nc, env, now, ops):
    for n in range(2 * GH):
        last = fill_bias_row(nc, env, now, ops, n)
    return last


def pieces(limit):
    cuts = sorted({0, CHUNK, SEQ, limit})
    return [(lo, hi, hi <= limit) for lo, hi in zip(cuts, cuts[1:])]


def bound_shift(nc, sem, env):
    norm_max, bound_ok, ident = env["norm_max"], env["bound_ok"], env["ident"]
    with ExitStack() as own:
        def sb(name, shape, dt=F32):
            return own.enter_context(nc.sbuf_tensor(f"bs_{name}", shape, dt))

        product = sb("product", [HEADS, BATCH])
        both = sb("both", [HEADS, 2, BATCH])
        bound = sb("bound", [HEADS, BATCH])
        half = sb("half", [HEADS, BATCH])
        within = sb("within", [HEADS, BATCH])
        all_within = sb("all_within", [HEADS, 1])
        minus = sb("minus", [HEADS, BATCH])
        left = sb("left", [HEADS, BATCH])
        hi, mid = sb("hi", [HEADS, BATCH], BF16), sb("mid", [HEADS, BATCH], BF16)
        part = sb("part", [HEADS, PARTS, BATCH])
        zeros = sb("zeros", [HEADS, SEQ], BF16)
        shift = sb("shift", [HEADS, PARTS, BATCH, SEQ], BF16)
        ps = own.enter_context(nc.psum_tensor("bs_ps", [P, CHUNK], F32))
        step, rooted, turned, stored = sem("bs_step"), sem("bs_rooted"), sem("bs_turned"), sem("bs_stored")
        half_set, ready, judged = sem("bs_half_set"), sem("bs_ready"), sem("bs_judged")
        block = own.enter_context(nc.Block())

        @block.gpsimd
        def _(pool):
            nc.gpsimd.memset(half[:, :], 0.5).then_inc(half_set, 1)
            pool.wait_ge(half_set, 1)
            pool.wait_ge(step, 2)
            nc.gpsimd.tensor_tensor(bound[:, :], product[:, :], half[:, :], ALU.pow).then_inc(rooted, 1)

        @block.tensor
        def _(pe):
            pe.wait_ge(judged, 1)
            nc.tensor.transpose(ps[0:1, 0:HEADS], all_within[:, :], ident[0:HEADS, 0:HEADS]).then_inc(turned, 1)

        @block.vector
        def _(dve):
            v = nc.vector
            v.memset(zeros[:, :], 0.0)
            v.tensor_reduce(both[:, :, :], norm_max[:, :, :].rearrange("h s (b c) -> h s b c", c=HALVES),
                            AX.X, ALU.max).then_inc(step, 1)
            dve.wait_ge(step, 1)
            v.tensor_tensor(product[:, :], both[:, 0, :], both[:, 1, :], ALU.mult).then_inc(step, 1)
            dve.wait_ge(rooted, 1)
            v.tensor_scalar(within[:, :], bound[:, :], SHIFT_LIMIT, None, ALU.is_le).then_inc(step, 1)
            dve.wait_ge(step, 3)
            v.tensor_reduce(all_within[:, :], within[:, :], AX.X, ALU.min).then_inc(judged, 1)
            v.tensor_scalar(minus[:, :], bound[:, :], -1.0, None, ALU.mult).then_inc(step, 1)
            dve.wait_ge(step, 4)
            v.tensor_copy(hi[:, :], minus[:, :]).then_inc(step, 1)
            dve.wait_ge(step, 5)
            v.tensor_copy(part[:, 0, :], hi[:, :])
            v.tensor_tensor(left[:, :], minus[:, :], hi[:, :], ALU.subtract).then_inc(step, 1)
            dve.wait_ge(step, 6)
            v.tensor_copy(mid[:, :], left[:, :]).then_inc(step, 1)
            dve.wait_ge(step, 7)
            v.tensor_copy(part[:, 1, :], mid[:, :])
            v.tensor_tensor(part[:, 2, :], left[:, :], mid[:, :], ALU.subtract).then_inc(step, 1)
            dve.wait_ge(step, 8)
            for a in range(PARTS):
                for b in range(BATCH):
                    last = v.tensor_scalar(shift[:, a, b, :], zeros[:, :], part[:, a, b:b + 1], None, ALU.add)
            last.then_inc(ready, 1)
            dve.wait_ge(turned, 1)
            v.tensor_reduce(bound_ok[:, :], ps[0:1, 0:HEADS], AX.X, ALU.min).then_inc(step, 1)

        @block.sync
        def _(sp):
            sp.wait_ge(ready, 1)
            for a in range(PARTS):
                sp.dma_start(env["shift_heads"][a], shift[:, a]).then_inc(stored, 16)
            sp.wait_ge(stored, 16 * PARTS)


def exact_maxima(nc, sem, env):
    ident, diag, head_scale, bound_ok = env["ident"], env["diag"], env["head_scale"], env["bound_ok"]
    with ExitStack() as own:
        def sb(name, shape, dt=F32):
            return own.enter_context(nc.sbuf_tensor(f"mx_{name}", shape, dt))

        def s(name):
            return sem(f"mx_{name}")

        q_op, k_op = sb("q_op", [P, GH, SEQ], BF16), sb("k_op", [P, GH, SEQ], BF16)
        now = sb("now", [P, 2, GH, 3])
        largest = sb("largest", [P, UNITS])
        largest_t = sb("largest_t", [UNITS, P])
        rest = sb("rest", [UNITS, P])
        shift = sb("shift", [UNITS, PARTS, P], BF16)
        scores = own.enter_context(nc.psum_tensor("mx_scores", [P, 2, SEQ], F32))
        ps_t = own.enter_context(nc.psum_tensor("mx_ps_t", [P, CHUNK], F32))
        loaded, rows_set, now_set, bias_set = s("loaded"), s("rows_set"), s("now_set"), s("bias_set")
        scores_made, diag_added, reduced = s("scores_made"), s("diag_added"), s("reduced")
        turned, part_step, shift_ready, shift_stored = s("turned"), s("part_step"), s("shift_ready"), s("shift_stored")
        block = own.enter_context(nc.Block())

        @block.sync
        def _(sp):
            with sp.If(sp.value_load(bound_ok[0:1, 0:1], min_val=0, max_val=1) == 0):
                sp.wait_ge(rows_set, 1)
                load_parts(sp, env, 0, q_op, k_op, loaded)
                with sp.Fori(0, NGRP - 1) as g:
                    sp.wait_ge(scores_made, UNITS * (g + 1))
                    load_parts(sp, env, g + 1, q_op, k_op, loaded)
                    sp.wait_ge(shift_ready, g + 1)
                    sp.dma_start(env["shift_rows"][g], shift[:, :, :]).then_inc(shift_stored, 16)
                sp.wait_ge(shift_ready, NGRP)
                sp.dma_start(env["shift_rows"][NGRP - 1], shift[:, :, :]).then_inc(shift_stored, 16)
                sp.wait_ge(shift_stored, 16 * NGRP)

        @block.gpsimd
        def _(pool):
            nc.gpsimd.memset(q_op[64:BIAS_ROW], 0.0)
            nc.gpsimd.memset(k_op[64:BIAS_ROW], 1.0).then_inc(rows_set, 1)

        @block.tensor
        def _(pe):
            with pe.If(pe.value_load(bound_ok[0:1, 0:1], min_val=0, max_val=1) == 0):
                with pe.Fori(0, NGRP) as g:
                    pe.wait_ge(loaded, 16 * PART_LOADS * (g + 1))
                    pe.wait_ge(bias_set, g + 1)
                    for j in range(GH):
                        for qt in range(KT):
                            u = KT * j + qt
                            pe.wait_ge(reduced, UNITS * g + u + 1)
                            for lo, hi, behind in pieces(qt * P):
                                rows = FULL_K if behind else PLAIN_K
                                last = nc.tensor.matmul(scores[:, u % 2, lo:hi], q_op[0:rows, j, qt * P:(qt + 1) * P],
                                                        k_op[0:rows, j, lo:hi], start=True, stop=True)
                            last.then_inc(scores_made, 1)
                    pe.wait_ge(reduced, UNITS * (g + 1) + 2)
                    nc.tensor.transpose(ps_t[0:UNITS, 0:P], largest[:, :], ident[:, :]).then_inc(turned, 1)

        @block.vector
        def _(dve):
            with dve.If(dve.value_load(bound_ok[0:1, 0:1], min_val=0, max_val=1) == 0):
                v = nc.vector
                dve.wait_ge(rows_set, 1)
                v.memset(largest[:, :], 0.0).then_inc(reduced, 2)

                def fill(g, par):
                    v.tensor_copy(now[:, par], head_scale[:, bass.ds(GH * g, GH), :]).then_inc(now_set, 1)
                    dve.wait_ge(now_set, g + 1)
                    fill_bias_rows(nc, env, now[:, par], (q_op, k_op)).then_inc(bias_set, 1)

                def group(g, par, end):
                    for j in range(GH):
                        for qt in range(KT):
                            u = KT * j + qt
                            dve.wait_ge(scores_made, UNITS * g + u + 1)
                            block_at = scores[:, u % 2, qt * P:(qt + 1) * P]
                            v.scalar_tensor_tensor(out=block_at, in0=diag[:, 1, :],
                                                   scalar=now[:, par, j, 0:1], in1=block_at,
                                                   op0=ALU.mult, op1=ALU.add).then_inc(diag_added, 1)
                            dve.wait_ge(diag_added, UNITS * g + u + 1)
                            v.tensor_reduce(largest[:, u:u + 1], scores[:, u % 2, :], AX.X, ALU.max).then_inc(reduced, 1)
                    if not end:
                        fill(g + 1, 1 - par)
                    dve.wait_ge(turned, g + 1)
                    v.tensor_scalar(largest_t[:, :], ps_t[0:UNITS, 0:P], -1.0, None, ALU.mult).then_inc(part_step, 1)
                    dve.wait_ge(part_step, 4 * g + 1)
                    if not isinstance(g, int) or g >= 1:
                        dve.wait_ge(shift_stored, 16 * g)
                    v.tensor_copy(shift[:, 0, :], largest_t[:, :]).then_inc(part_step, 1)
                    dve.wait_ge(part_step, 4 * g + 2)
                    v.tensor_tensor(rest[:, :], largest_t[:, :], shift[:, 0, :], ALU.subtract).then_inc(part_step, 1)
                    dve.wait_ge(part_step, 4 * g + 3)
                    v.tensor_copy(shift[:, 1, :], rest[:, :]).then_inc(part_step, 1)
                    dve.wait_ge(part_step, 4 * g + 4)
                    v.tensor_tensor(shift[:, 2, :], rest[:, :], shift[:, 1, :], ALU.subtract).then_inc(shift_ready, 1)

                fill(0, 0)
                group(0, 0, False)
                with dve.Fori(0, NGRP // 2 - 1) as pair:
                    group(2 * pair + 1, 1, False)
                    group(2 * pair + 2, 0, False)
                group(NGRP - 1, 1, True)


def attention(nc, sem, env):
    diag, head_scale = env["diag"], env["head_scale"]
    with ExitStack() as own:
        def sb(name, shape, dt=F32):
            return own.enter_context(nc.sbuf_tensor(f"at_{name}", shape, dt))

        def s(name):
            return sem(f"at_{name}")

        q_op = [sb(f"q_op{i}", [P, GH, SEQ], BF16) for i in range(2)]
        k_op = [sb(f"k_op{i}", [P, GH, SEQ], BF16) for i in range(2)]
        now = sb("now", [P, 2, GH, 3])
        v_op = [sb(f"v_op{i}", [P, KT, GH * VW]) for i in range(2)]
        weights = sb("weights", [P, PSTEPS, GH, SEQ])
        o_out = sb("o_out", [P, SEQ])
        scores = own.enter_context(nc.psum_tensor("at_scores", [P, SLOTS, SEQ], F32))
        acc = own.enter_context(nc.psum_tensor("at_acc", [P, SEQ], F32))

        qk_loaded, v_loaded = [s("qk_loaded0"), s("qk_loaded1")], [s("v_loaded0"), s("v_loaded1")]
        rows_set, now_set, bias_set = s("rows_set"), s("now_set"), s("bias_set")
        scores_made, diag_added = s("scores_made"), s("diag_added")
        slots_free = s("slots_free")
        steps_free = s("steps_free")
        o_ready, o_stored = s("o_ready"), s("o_stored")
        block = own.enter_context(nc.Block())

        def in_groups(eng, body):
            body(0, 0, 0, False)
            with eng.Fori(0, NGRP // 2 - 1) as pair:
                body(2 * pair + 1, 1, pair, False)
                body(2 * pair + 2, 0, pair + 1, False)
            body(NGRP - 1, 1, NGRP // 2 - 1, True)

        @block.sync
        def _(sp):
            def load(g, par):
                load_parts(sp, env, g, q_op[par], k_op[par], qk_loaded[par])
                sp.dma_start(q_op[par][SHIFT_ROW:PLAIN_K], env["shift_group"][g]).then_inc(qk_loaded[par], 16)

            def load_v(g, par):
                sp.dma_start(v_op[par][:, :, :], env["v_group"][g]).then_inc(v_loaded[par], 16)

            def store(g):
                sp.wait_ge(o_ready, 2 * g + 4)
                for j in range(GH):
                    sp.dma_start(env["o_group"][g, j], o_out[32 * j:32 * j + VW, :]).then_inc(o_stored, 16)

            sp.wait_ge(rows_set, 1)
            for g in range(2):
                load(g, g)
                load_v(g, g)
            with sp.Fori(0, NGRP // 2 - 1) as pair:
                for par in range(2):
                    g = 2 * pair + par
                    sp.wait_ge(scores_made, UNITS * (g + 1))
                    load(g + 2, par)
                    sp.wait_ge(steps_free, KT * (g + 1) + PSTEPS)
                    load_v(g + 2, par)
                    store(g)
            for par in range(2):
                store(NGRP - 2 + par)
            sp.wait_ge(o_stored, 16 * GH * NGRP + 1)

        @block.gpsimd
        def _(pool):
            nc.gpsimd.memset(q_op[0][64:BIAS_ROW], 0.0).then_inc(slots_free, SLOTS)
            nc.gpsimd.memset(q_op[1][64:BIAS_ROW], 0.0).then_inc(steps_free, PSTEPS)
            nc.gpsimd.memset(k_op[0][64:BIAS_ROW], 1.0).then_inc(o_stored, 1)
            nc.gpsimd.memset(k_op[1][64:BIAS_ROW], 1.0).then_inc(rows_set, 1)

        @block.tensor
        def _(pe):
            def score(g, par, seen, u):
                kt, j = divmod(u, GH)
                if u == 0:
                    pe.wait_ge(qk_loaded[par], 16 * (PART_LOADS + 1) * (seen + 1))
                    pe.wait_ge(bias_set, g + 1)
                before = {0: 2, 1: 3, 2: 1}.get(u, u + 1)
                pe.wait_ge(slots_free, UNITS * g + before)
                for lo, hi, ahead in pieces((kt + 1) * P):
                    rows = PLAIN_K if ahead else FULL_K
                    last = nc.tensor.matmul(scores[:, u % SLOTS, lo:hi], k_op[par][0:rows, j, kt * P:(kt + 1) * P],
                                            q_op[par][0:rows, j, lo:hi], start=True, stop=True)
                last.then_inc(scores_made, 1)

            def weigh(g, par, seen, kt, half):
                if half == 0:
                    pe.wait_ge(slots_free, SLOTS + UNITS * g + GH * (kt + 1))
                    if kt == 0:
                        pe.wait_ge(v_loaded[par], 16 * (seen + 1))
                if kt == 0:
                    pe.wait_ge(o_ready, 2 * g + 1 + half)
                cols = slice(half * CHUNK, (half + 1) * CHUNK)
                for j in range(GH):
                    last = nc.tensor.matmul(acc[32 * j:32 * j + VW, cols], v_op[par][:, kt, VW * j:VW * (j + 1)],
                                            weights[:, kt % PSTEPS, j, cols], start=(kt == 0), stop=(kt == KT - 1))
                if half == 1:
                    last.then_inc(steps_free, 1)

            def body(g, par, seen, end):
                def ahead(kt, j):
                    if kt < KT:
                        score(g, par, seen, GH * kt + j)
                    elif not end:
                        score(g + 1, 1 - par, seen + par, GH * (kt - KT) + j)

                for kt in range(KT):
                    ahead(kt + 1, 2)
                    weigh(g, par, seen, kt, 0)
                    ahead(kt + 1, 3)
                    weigh(g, par, seen, kt, 1)
                    ahead(kt + 2, 0)
                    ahead(kt + 2, 1)

            for u in range(GH + 2):
                score(0, 0, 0, u)
            in_groups(pe, body)

        @block.vector
        def _(dve):
            v = nc.vector

            def take_scales(g, par):
                v.tensor_copy(now[:, par], head_scale[:, bass.ds(GH * g, GH), :]).then_inc(now_set, 1)

            def read_acc(g):
                dve.wait_ge(steps_free, KT * (g + 1) + PSTEPS)
                dve.wait_ge(o_stored, 16 * GH * g + 1)
                v.tensor_copy(o_out[:, 0:CHUNK], acc[:, 0:CHUNK]).then_inc(o_ready, 1)
                v.tensor_copy(o_out[:, CHUNK:SEQ], acc[:, CHUNK:SEQ]).then_inc(o_ready, 1)

            def body(g, par, seen, end):
                for u in range(UNITS):
                    kt, j = divmod(u, GH)
                    if u == GH + 2 and (not isinstance(g, int) or g > 0):
                        read_acc(g - 1)
                    dve.wait_ge(scores_made, UNITS * g + u + 1)
                    block_at = scores[:, u % SLOTS, kt * P:(kt + 1) * P]
                    v.scalar_tensor_tensor(out=block_at, in0=diag[:, 0, :], scalar=now[:, par, j, 0:1],
                                           in1=block_at, op0=ALU.mult, op1=ALU.add).then_inc(diag_added, 1)
                    if u == FILL_FROM - 1 and not end:
                        take_scales(g + 1, 1 - par)
                    n = (u - FILL_FROM) // 2
                    if u >= FILL_FROM and u % 2 == 0 and n < 2 * GH and not end:
                        if n == 0:
                            dve.wait_ge(now_set, g + 2)
                        row = fill_bias_row(nc, env, now[:, 1 - par], (q_op[1 - par], k_op[1 - par]), n)
                        if n == 2 * GH - 1:
                            row.then_inc(bias_set, 1)

            v.memset(acc[:, :], 0.0).then_inc(o_ready, 2)
            take_scales(0, 0)
            dve.wait_ge(rows_set, 1)
            dve.wait_ge(now_set, 1)
            fill_bias_rows(nc, env, now[:, 0], (q_op[0], k_op[0])).then_inc(bias_set, 1)
            in_groups(dve, body)
            read_acc(NGRP - 1)

        @block.scalar
        def _(act):
            with act.Fori(0, NGRP) as g:
                for u in range(UNITS):
                    kt, j = divmod(u, GH)
                    if j == 0:
                        act.wait_ge(steps_free, KT * g + kt + 1)
                    act.wait_ge(diag_added, UNITS * g + u + 1)
                    nc.scalar.activation(weights[:, kt % PSTEPS, j, :], scores[:, u % SLOTS, :],
                                         ACT.Exp).then_inc(slots_free, 1)


_INS = ["L0_attn_x", "L0_attn_qkv_w", "L0_attn_proj_w", "L0_attn_proj_b", "L0_attn_slopes", "L0_ffn_gate",
        "L0_ffn_corr_bias", "L0_ffn_w1", "L0_ffn_w2", "L0_ffn_fc1_w", "L0_ffn_fc2_w", "L0_ffn_up_w",
        "L0_ffn_down_w"]


def kernel(**inputs):
    import concourse.bacc as _bacc
    from concourse.bass_utils import run_bass_kernel_spmd as _run

    nc = _bacc.Bacc("TRN2", target_bir_lowering=False, num_devices=1)
    arrays, io, consts = {}, {}, {}
    for name in _INS:
        a = np.ascontiguousarray(inputs[name])
        arrays[f"in_{name}_dram"] = a
        io[name] = nc.dram_tensor(f"in_{name}_dram", a.shape, mybir.dt.from_np(a.dtype), kind="ExternalInput").ap()
    for name, a in shape_constants().items():
        arrays[f"const_{name}"] = a
        consts[name] = nc.dram_tensor(f"const_{name}", a.shape, mybir.dt.from_np(a.dtype), kind="ExternalInput").ap()
    out = nc.dram_tensor("out_0_dram", (BATCH, SEQ, DIM), F32, kind="ExternalOutput").ap()
    program(nc, io, consts, out)
    r = _run(nc, [arrays], core_ids=[0])
    return r.results[0]["out_0_dram"]
```

```python
from contextlib import ExitStack

import numpy as np

import concourse.bass as bass
from concourse import mybir

F32 = mybir.dt.float32
F32R = mybir.dt.float32r
BF16 = mybir.dt.bfloat16
ALU = mybir.AluOpType
ACT = mybir.ActivationFunctionType
AX = mybir.AxisListType

P = 128
BATCH, SEQ, DIM = 4, 1024, 128
HEADS = 16
HD = DIM // HEADS
HALF = HD // 2
EXPERTS, LATENT, INTER, SHARED = 8, 64, 64, 512
GROUPS = 2
PER_GROUP = EXPERTS // GROUPS
HIDDEN = SHARED + EXPERTS * INTER
HT = HIDDEN // P
ST = SHARED // P
CHUNK = 512
TILES = CHUNK // P
CHUNKS = BATCH * SEQ // CHUNK
HALVES = SEQ // CHUNK
GH = 4
HG = HEADS // GH
NGRP = BATCH * HG
KT = SEQ // P
PARTS = 3
VW = HD + 1
EPS = 1e-5
SCALE = HD ** -0.5

QK_ROWS = PARTS * PARTS * HD
SHIFT_ROW = QK_ROWS
PLAIN_K = SHIFT_ROW + PARTS
BIAS_ROW = 96
BIAS_ROWS = PARTS + KT * PARTS + PARTS
FULL_K = BIAS_ROW + BIAS_ROWS
SHIFT_LIMIT = 32.0
SLOTS = 3
PSTEPS = 4
FILL_FROM = 8
UNITS = KT * GH
ROUTE_STEPS = 15

QKV_COL = P
ROT_COL = QKV_COL + 3 * DIM
IN_COL = ROT_COL + 2 * DIM
W_COLS = IN_COL + HIDDEN


class Chunk:

    def __init__(self, pair, k):
        self.pair, self.k = pair, k
        self.n = 2 * pair + k
        self.batch = pair + k // 2
        self.half = k % 2
        self.seen = self.batch + 1
        self.loads_ahead = not (isinstance(self.n, int) and self.n + 2 >= CHUNKS)
        self.at_least = self.n if isinstance(pair, int) else 2 + k

    def next(self, by=1):
        return Chunk(self.pair, self.k + by)


def in_chunks(eng, lead, body, tail):
    lead()
    for n in range(2):
        body(Chunk(0, n), False)
    with eng.Fori(1, CHUNKS // 2 - 1) as pair:
        body(Chunk(pair, 0), False)
        body(Chunk(pair, 1), False)
    body(Chunk(BATCH - 1, 0), False)
    body(Chunk(BATCH - 1, 1), True)
    tail(Chunk(BATCH - 1, 1))


def shape_constants():
    c = {}
    inv = (1.0 / np.float32(10000.0) ** (np.arange(0, HD, 2, dtype=np.float32) / np.float32(HD))).astype(np.float32)
    ang = (np.arange(SEQ, dtype=np.float32)[None, :] * inv[:, None]).astype(np.float32)
    rows = np.arange(P) % HD % HALF
    cos, sin = np.cos(ang.astype(np.float64))[rows], np.sin(ang.astype(np.float64))[rows]
    c["rope"] = np.stack([cos * SCALE, sin * SCALE, cos, sin], 1).astype(np.float32)
    pos = np.arange(SEQ)
    block, r = pos // P, pos % P
    part = np.arange(BIAS_ROWS) % PARTS
    kside, qside = np.zeros((BIAS_ROWS, SEQ)), np.zeros((BIAS_ROWS, SEQ))
    kside[:PARTS], qside[:PARTS] = r, 1.0
    for j in range(KT):
        at = PARTS * (1 + j)
        kside[at:at + PARTS] = P * (block - j)
        qside[at:at + PARTS] = block == j
    kside[-PARTS:], qside[-PARTS:] = 1.0, -r
    c["biasrows"] = np.stack([qside, kside], 1).astype(np.float32)
    sel = np.zeros((BIAS_ROWS, 2, 4), np.float32)
    for row in range(BIAS_ROWS):
        last = row >= BIAS_ROWS - PARTS
        sel[row, 0, 3 if last else part[row]] = 1.0
        sel[row, 1, part[row] if last else 3] = 1.0
    c["biassel"] = sel.reshape(BIAS_ROWS, 8)
    key, query = np.arange(P)[:, None], np.arange(P)[None, :]
    c["diag"] = np.stack([np.minimum(key - query, 0), np.minimum(query - key, 0)], 1).astype(np.float32)
    tri = np.tril(np.ones((EXPERTS, EXPERTS), np.float32), -1)
    c["earlier"] = np.broadcast_to(tri.reshape(1, -1), (P, EXPERTS * EXPERTS)).copy()
    c["ident"] = np.eye(P, dtype=np.float32)
    c["headsum"] = (np.arange(P)[:, None] // HD == np.arange(HEADS)[None, :]).astype(np.float32)
    return c


def program(nc, io, consts, out):
    ctx = ExitStack()
    with ctx:
        def sb(name, shape, dt=F32):
            return ctx.enter_context(nc.sbuf_tensor(name, shape, dt))

        def sem(name):
            return ctx.enter_context(nc.semaphore(name))

        x1_dram = nc.dram_tensor("x1_scratch", [BATCH * SEQ, DIM], F32)
        part_dram = [nc.dram_tensor(f"{n}_parts", [PARTS, BATCH * DIM, SEQ], BF16) for n in "qk"]
        shift_dram = nc.dram_tensor("shift_parts", [PARTS, BATCH * HEADS, SEQ], BF16)
        v_dram = nc.dram_tensor("v_scratch", [NGRP, P, KT, GH * VW], F32)
        o_dram = nc.dram_tensor("o_scratch", [BATCH * HEADS, VW, SEQ], F32)

        x_tiles = io["L0_attn_x"].rearrange("b (h t p) c -> (b h) p t c", p=P, t=TILES)
        x1_tiles = x1_dram[:, :].rearrange("(n t p) c -> n p t c", p=P, t=TILES)
        out_tiles = out.rearrange("b (h t p) c -> (b h) p t c", p=P, t=TILES)
        part_chunk = [d[:, :].rearrange("a (b c) (h t) -> b h c a t", b=BATCH, h=HALVES) for d in part_dram]
        part_group = [d[:, :].rearrange("a (g j d) t -> g a d j t", j=GH, d=HD) for d in part_dram]
        shift_group = shift_dram[:, :, :].rearrange("a (g j) t -> g a j t", j=GH)
        shift_heads = shift_dram[:, :, :].rearrange("a (b h) t -> a h b t", b=BATCH)
        shift_rows = shift_dram[:, :, :].rearrange("a (g j) (q r) -> g (j q) a r", j=GH, r=P)
        v_chunk = v_dram[:, :, :, :].rearrange("(b g) p (h k) c -> b h p g (k c)", b=BATCH, h=HALVES)
        v_group = v_dram[:, :, :, :]
        o_group = o_dram[:, :, :].rearrange("(g j) r t -> g j r t", j=GH)
        rden_dram = nc.dram_tensor("rden_scratch", [BATCH * HEADS, SEQ], F32)
        den_batch = o_dram[:, :, :].rearrange("(b j) r (e t) -> b j e r t", b=BATCH, t=P)[:, :, :, HD, :]
        rden_batch = rden_dram[:, :].rearrange("(b j) (e t) -> b j e t", b=BATCH, t=P)
        rden_chunk = rden_dram[:, :].rearrange("(b j) (h t) -> b h j t", b=BATCH, h=HALVES)
        o_chunk = o_dram[:, :, :].rearrange("(b j) r (h t) -> b h j r t", b=BATCH, h=HALVES)

        ident = sb("ident", [P, P])
        earlier = sb("earlier", [P, EXPERTS, EXPERTS])
        corr = sb("corr", [P, EXPERTS])
        proj_bias = sb("proj_bias", [P, DIM])
        w_hi = sb("w_hi", [P, W_COLS], F32R)
        w_lo = sb("w_lo", [P, W_COLS], F32R)
        w_out = sb("w_out", [P, HT, DIM])
        proj_t = sb("proj_t", [P, DIM])
        headsum = sb("headsum", [P, HEADS], BF16)
        norm_max = sb("norm_max", [HEADS, 2, CHUNKS])
        bound_ok = sb("bound_ok", [1, 1], mybir.dt.int32)
        head_scale = sb("head_scale", [P, BATCH * HEADS, 3])
        diag = sb("diag", [P, 2, P])
        bias_rows = sb("bias_rows", [P, 2, SEQ], BF16)
        bias_sel = sb("bias_sel", [P, 8])
        x_ln = sb("x_ln", [P, 2, TILES, DIM])
        rope = sb("rope", [P, 4, SEQ])
        q_op = [sb(f"q_op{i}", [P, GH, SEQ], BF16) for i in range(2)]
        k_op = [sb(f"k_op{i}", [P, GH, SEQ], BF16) for i in range(2)]
        ones = sb("ones", [HEADS, SEQ], BF16)
        bound_rows = sb("bound_rows", [HEADS, PARTS, BATCH, SEQ], BF16)
        x_in = x_ln
        o_in, rden = (rope[:, i, :].rearrange("p (h t) -> p h t", h=HALVES) for i in range(2))
        den_all, den_rec = (rope[:, 2 + i, 0:BATCH * P].rearrange("p (b t) -> p b t", b=BATCH) for i in range(2))
        ln_loaded, rope_loaded = [sem("ln_loaded0"), sem("ln_loaded1")], sem("rope_loaded")
        qk_loaded = [sem("qk_loaded0"), sem("qk_loaded1")]
        in_loaded = [sem("in_loaded0"), sem("in_loaded1")]
        den_loaded, den_turned, den_stored = sem("den_loaded"), sem("den_turned"), sem("den_stored")
        shift_stored, first_shift = sem("shift_stored"), sem("first_shift")

        w_ready = sem("w_ready")
        f_loaded, c_loaded, t_loaded = sem("f_loaded"), sem("c_loaded"), sem("t_loaded")

        with nc.Block() as block, ExitStack() as own:
            def tmp(name, shape, dt=F32):
                return own.enter_context(nc.sbuf_tensor(name, shape, dt))
            raw_up = tmp("raw_up", [P, ST, DIM])
            raw_w1 = tmp("raw_w1", [P, 4, LATENT])
            raw_w2 = tmp("raw_w2", [LATENT, EXPERTS, INTER])
            raw_fc1 = tmp("raw_fc1", [LATENT, DIM])
            raw_fc2 = tmp("raw_fc2", [P, LATENT])
            raw_down = tmp("raw_down", [P, SHARED])
            raw_gate = tmp("raw_gate", [EXPERTS, DIM])
            raw_qkv = tmp("raw_qkv", [P, 3, DIM])
            raw_proj = tmp("raw_proj", [P, DIM])
            w_all = tmp("w_all", [P, W_COLS])
            w1_t = tmp("w1_t", [LATENT, EXPERTS * INTER])
            fc2_t = tmp("fc2_t", [LATENT, DIM])
            headsum_f32 = tmp("headsum_f32", [P, HEADS])
            bias_f32 = tmp("bias_f32", [P, 2, SEQ])
            slope8 = tmp("slope8", [P, BATCH * HEADS])
            part_hi = tmp("part_hi", [P, BATCH * HEADS], BF16)
            part_mid = tmp("part_mid", [P, BATCH * HEADS], BF16)
            part_low = tmp("part_low", [P, BATCH * HEADS], BF16)
            rest1 = tmp("rest1", [P, BATCH * HEADS])
            rest2 = tmp("rest2", [P, BATCH * HEADS])
            bank = [own.enter_context(nc.psum_tensor(f"prep{i}", [P, CHUNK], F32)) for i in range(8)]
            prep_mm, prep_cp, prep_v = sem("prep_mm"), sem("prep_cp"), sem("prep_v")
            shared_in, w_whole, hi_ready = sem("shared_in"), sem("w_whole"), sem("hi_ready")
            known = IN_COL + SHARED
            gate_cols, qkv_cols, rot_cols = w_all[:, 0:P], w_all[:, QKV_COL:ROT_COL], w_all[:, ROT_COL:IN_COL]
            slopes = io["L0_attn_slopes"].rearrange("(a h) -> a h", a=1)
            br = slice(BIAS_ROW, FULL_K)

            fold_loads = [
                (ident[:, :], consts["ident"]),
                (raw_w1[:, :, :], io["L0_ffn_w1"].rearrange("(t e) i l -> (e i) t l", e=2)),
                (raw_w2[:, :, :], io["L0_ffn_w2"].rearrange("e l i -> l e i")),
                (raw_fc1[:, :], io["L0_ffn_fc1_w"]),
                (raw_fc2[:, :], io["L0_ffn_fc2_w"]),
            ]
            loads = [
                (raw_up[:, :, :], io["L0_ffn_up_w"].rearrange("(t p) c -> p t c", p=P)),
                (raw_down[:, :], io["L0_ffn_down_w"]),
                (raw_gate[:, :], io["L0_ffn_gate"]),
                (raw_qkv[:, :, :], io["L0_attn_qkv_w"].rearrange("(s p) c -> p s c", p=P)),
                (raw_proj[:, :], io["L0_attn_proj_w"]),
            ]
            table_loads = [
                (earlier[:, :, :], consts["earlier"].rearrange("p (a b) -> p a b", a=EXPERTS)),
                (corr[:, :], io["L0_ffn_corr_bias"].rearrange("(a h) -> a h", a=1).broadcast_to([P, EXPERTS])),
                (proj_bias[:, :], io["L0_attn_proj_b"].rearrange("(a h) -> a h", a=1).broadcast_to([P, DIM])),
                (slope8[:, :].rearrange("p (b h) -> p b h", b=BATCH), slopes.unsqueeze(1).broadcast_to([P, BATCH, HEADS])),
                (diag[:, :, :], consts["diag"]),
                (headsum_f32[:, :], consts["headsum"]),
                (bias_f32[br, :, :], consts["biasrows"]),
                (bias_sel[br, :], consts["biassel"]),
            ]

            @block.sync
            def _(sp):
                for dst, src in fold_loads:
                    sp.dma_start(dst, src).then_inc(f_loaded, 16)
                for dst, src in loads:
                    sp.dma_start(dst, src).then_inc(c_loaded, 16)
                for dst, src in table_loads:
                    sp.dma_start(dst, src).then_inc(t_loaded, 16)
                for n in range(2):
                    sp.dma_start(x_ln[:, n], x_tiles[n]).then_inc(ln_loaded[n], 16)
                sp.dma_start(rope[:, :, :], consts["rope"]).then_inc(rope_loaded, 16)

            @block.gpsimd
            def _(pool):
                for i in range(2):
                    nc.gpsimd.memset(q_op[i][64:BIAS_ROW], 0.0)
                    nc.gpsimd.memset(k_op[i][64:BIAS_ROW], 1.0)
                nc.gpsimd.memset(ones[:, :], 1.0)

            @block.scalar
            def _(act):
                act.wait_ge(prep_mm, 2)
                def copy(dst, src):
                    return nc.scalar.activation(dst, src, ACT.Copy)
                copy(w_all[:, IN_COL:known], bank[0][:, :]).then_inc(shared_in, 1)
                copy(w_out[:, 0:ST, :], bank[2][:, :].rearrange("p (t n) -> p t n", n=DIM))
                copy(proj_t[:, :], bank[7][:, 0:P])
                act.wait_ge(shared_in, 1)
                act.wait_ge(w_whole, 1)
                copy(w_hi[:, 0:known], w_all[:, 0:known]).then_inc(hi_ready, 1)
                act.wait_ge(w_whole, 2)
                copy(w_hi[:, known:W_COLS], w_all[:, known:W_COLS]).then_inc(w_ready, 1)

            @block.tensor
            def _(pe):
                pe.wait_ge(f_loaded, 16 * len(fold_loads))
                tr = nc.tensor.transpose
                for t in range(4):
                    tr(bank[1][0:LATENT, t * P:(t + 1) * P], raw_w1[:, t, :], ident[:, :])
                tr(bank[5][0:LATENT, 0:P], raw_fc2[:, :], ident[:, :]).then_inc(prep_mm, 1)
                pe.wait_ge(c_loaded, 16 * len(loads))
                for t in range(4):
                    tr(bank[0][:, t * P:(t + 1) * P], raw_up[:, t, :], ident[:, :])
                    tr(bank[2][:, t * P:(t + 1) * P], raw_down[:, t * P:(t + 1) * P], ident[:, :])
                tr(bank[3][:, P:P + EXPERTS], raw_gate[:, :], ident[0:EXPERTS, 0:EXPERTS])
                tr(bank[7][:, 0:P], raw_proj[:, :], ident[:, :])
                for s in range(3):
                    last = tr(bank[4][:, s * P:(s + 1) * P], raw_qkv[:, s, :], ident[:, :])
                last.then_inc(prep_mm, 1)
                pe.wait_ge(prep_cp, 1)
                nc.tensor.matmul(bank[5][:, :], raw_fc1[:, :], w1_t[:, :], start=True, stop=True)
                for t in range(4):
                    last = nc.tensor.matmul(bank[6][:, t * P:(t + 1) * P],
                                            raw_w2[:, 2 * t:2 * t + 2, :].rearrange("l e i -> l (e i)"),
                                            fc2_t[:, :], start=True, stop=True)
                last.then_inc(prep_mm, 1)

            @block.vector
            def _(dve):
                v = nc.vector
                dve.wait_ge(prep_mm, 1)
                v.tensor_copy(w1_t[:, :], bank[1][0:LATENT, :])
                v.tensor_copy(fc2_t[:, :], bank[5][0:LATENT, 0:P]).then_inc(prep_cp, 1)
                dve.wait_ge(prep_mm, 2)
                v.memset(gate_cols[:, EXPERTS:P], 0.0)
                v.tensor_copy(gate_cols[:, 0:EXPERTS], bank[3][:, P:P + EXPERTS])
                v.tensor_copy(qkv_cols, bank[4][:, 0:3 * P])
                src = bank[4][:, 0:2 * P].rearrange("p (s d) -> p s d", d=HD)
                dst = rot_cols.rearrange("p (s d) -> p s d", d=HD)
                v.tensor_scalar(dst[:, :, 0:HALF], src[:, :, HALF:HD], -1.0, None, ALU.mult)
                v.tensor_copy(dst[:, :, HALF:HD], src[:, :, 0:HALF]).then_inc(w_whole, 1)
                dve.wait_ge(t_loaded, 16 * len(table_loads))
                v.tensor_copy(bias_rows[br, :, :], bias_f32[br, :, :])
                v.tensor_copy(headsum[:, :], headsum_f32[:, :])
                v.tensor_scalar(slope8[:, :], slope8[:, :], 8.0, None, ALU.mult).then_inc(prep_v, 1)
                dve.wait_ge(prep_v, 1)
                v.tensor_copy(part_hi[:, :], slope8[:, :]).then_inc(prep_v, 1)
                dve.wait_ge(prep_v, 2)
                v.tensor_tensor(rest1[:, :], slope8[:, :], part_hi[:, :], ALU.subtract).then_inc(prep_v, 1)
                dve.wait_ge(prep_v, 3)
                v.tensor_copy(part_mid[:, :], rest1[:, :]).then_inc(prep_v, 1)
                dve.wait_ge(prep_v, 4)
                v.tensor_tensor(part_low[:, :], rest1[:, :], part_mid[:, :], ALU.subtract).then_inc(prep_v, 1)
                v.memset(head_scale[:, :, 1:3], 0.0)
                v.tensor_copy(head_scale[:, :, 0], slope8[:, :]).then_inc(prep_v, 1)
                dve.wait_ge(prep_v, 6)
                done = 6
                for side in range(2):
                    col = 4 * side
                    v.tensor_scalar(rest2[br, :], part_hi[br, :], bias_sel[br, col:col + 1],
                                    bias_sel[br, col + 3:col + 4], ALU.mult, ALU.add).then_inc(prep_v, 1)
                    for i, part in enumerate((part_mid, part_low)):
                        done += 1
                        dve.wait_ge(prep_v, done)
                        dst = (rest1, head_scale[:, :, 1 + side])[i]
                        src = (rest2, rest1)[i]
                        v.scalar_tensor_tensor(out=dst[br, :], in0=part[br, :],
                                               scalar=bias_sel[br, col + 1 + i:col + 2 + i],
                                               in1=src[br, :], op0=ALU.mult, op1=ALU.add).then_inc(prep_v, 1)
                    done += 1
                    dve.wait_ge(prep_v, done)
                dve.wait_ge(prep_mm, 3)
                v.tensor_copy(w_all[:, known:W_COLS], bank[5][:, :]).then_inc(w_whole, 1)
                v.tensor_copy(w_out[:, ST:HT, :], bank[6][:, :].rearrange("p (t n) -> p t n", n=DIM))
                dve.wait_ge(hi_ready, 1)
                v.tensor_tensor(w_lo[:, 0:known], w_all[:, 0:known], w_hi[:, 0:known], ALU.subtract)
                dve.wait_ge(w_whole, 2)
                dve.wait_ge(w_ready, 1)
                v.tensor_tensor(w_lo[:, known:W_COLS], w_all[:, known:W_COLS], w_hi[:, known:W_COLS],
                                ALU.subtract).then_inc(w_ready, 1)

        token_pass(nc, sem, 1, locals())
        bound_shift(nc, sem, locals())
        exact_maxima(nc, sem, locals())
        attention(nc, sem, locals())
        token_pass(nc, sem, 2, locals())


def token_pass(nc, sem, number, env):
    first = number == 1
    ident, earlier, corr = env["ident"], env["earlier"], env["corr"]
    w_hi, w_lo, w_out = env["w_hi"], env["w_lo"], env["w_out"]
    headsum = env["headsum"]
    proj_t, proj_bias = env["proj_t"], env["proj_bias"]
    RT = HT - ST

    with ExitStack() as own:
        def sb(name, shape, dt=F32):
            return own.enter_context(nc.sbuf_tensor(f"p{number}_{name}", shape, dt))

        def ps(name, shape):
            return own.enter_context(nc.psum_tensor(f"p{number}_{name}", shape, F32))

        def s(name):
            return sem(f"p{number}_{name}")

        x = sb("x", [P, 2, TILES, DIM])
        stats = sb("stats", [P, 2, TILES, 6])
        mean2, mean, apart, apart2, var_n, var_in = (
            sb(name, [P, 2, TILES]) for name in ("mean2", "mean", "apart", "apart2", "var_n", "var_in"))
        veps = sb("veps", [P, 2, TILES])
        rstd = sb("rstd", [P, 2, TILES])
        minus_half = sb("minus_half", [P, TILES])
        xn = sb("xn", [P, TILES, DIM])
        xn_t = sb("xn_t", [P, 2, 2, CHUNK], F32R)
        logit_t = sb("logit_t", [P, CHUNK])
        en = sb("en", [P, TILES, EXPERTS])
        en1 = sb("en1", [P, TILES, EXPERTS])
        score = sb("score", [P, TILES, EXPERTS])
        sfc = sb("sfc", [P, TILES, EXPERTS])
        pair_sum = sb("pair_sum", [P, TILES * GROUPS, 6])
        gsum = sb("gsum", [P, TILES, GROUPS])
        gmask = sb("gmask", [P, TILES, GROUPS])
        kept = sb("kept", [P, TILES, EXPERTS])
        above = sb("above", [P, TILES, EXPERTS * EXPERTS])
        equal = sb("equal", [P, TILES, EXPERTS * EXPERTS])
        rank = sb("rank", [P, TILES, EXPERTS])
        chosen = sb("chosen", [P, TILES, EXPERTS])
        csum = sb("csum", [P, TILES])
        csum1 = sb("csum1", [P, TILES])
        crec = sb("crec", [P, TILES])
        coef = sb("coef", [P, TILES, EXPERTS])
        coef_wide = sb("coef_wide", [P, TILES, EXPERTS * INTER])
        relu = sb("relu", [P, HT, CHUNK])
        squared = sb("squared", [P, RT, CHUNK])
        hid = sb("hid", [P, HT, CHUNK])
        res = sb("res", [P, TILES, DIM])

        ps_t = ps("ps_t", [P, CHUNK])
        ps_g = ps("ps_g", [P, CHUNK])
        ps_h = ps("ps_h", [P, 2, CHUNK])
        ps_c = ps("ps_c", [P, CHUNK])
        ps_o = ps("ps_o", [P, TILES, DIM])
        ps_q = ps("ps_q", [P, 2, CHUNK])
        wide_bank = [ps_c[:, :], ps_q[:, 1, :]]

        x_loaded = [s("x_loaded0"), s("x_loaded1")]
        half_set, xt_high = s("half_set"), s("xt_high")
        rstd_ready = [s("rstd_ready"), s("rstd2_ready")]
        norm_step, norm_ready, turned, xt_ready = s("norm_step"), s("norm_ready"), s("turned"), s("xt_ready")
        gate_made, gate_copied, gate_turned, gate_exp = s("gate_made"), s("gate_copied"), s("gate_turned"), s("gate_exp")
        route_step, coef_ready, wide_ready = s("route_step"), s("coef_ready"), s("wide_ready")
        hid_made, relu_ready = s("hid_made"), s("relu_ready")
        spread, scaled_ready = s("spread"), s("scaled_ready")
        sq_pool, sq_act = s("squared_by_pool"), s("squared_by_act")
        ffn_made, res_ready, res_stored = s("ffn_made"), s("res_ready"), s("res_stored")

        if first:
            xn2 = sb("xn2", [P, TILES, DIM])
            xn2_t = sb("xn2_t", [P, 2, CHUNK], F32R)
            x_ln, ln_loaded, rope, rope_loaded = env["x_ln"], env["ln_loaded"], env["rope"], env["rope_loaded"]
            turn_a = sb("turn_a", [P, 2, CHUNK])
            turn_b = sb("turn_b", [P, 2, CHUNK])
            roped = sb("roped", [P, 2, CHUNK])
            left = sb("left", [P, 2, CHUNK])
            squares = sb("squares", [P, 2, CHUNK], BF16)
            parts = sb("parts", [P, 2, PARTS, CHUNK], BF16)
            v_ext = sb("v_ext", [P, HG, TILES, GH * VW])
            ones_set, xt2_high = s("ones_set"), s("xt2_high")
            norm2_step, norm2_ready, turned2, xt2_ready = s("norm2_step"), s("norm2_ready"), s("turned2"), s("xt2_ready")
            squares_ready, norms_made, norms_read = s("squares_ready"), s("norms_made"), s("norms_read")
            qk_made, turn_ready, rope_step = s("qk_made"), s("turn_ready"), s("rope_step")
            v_made, v_ready, v_stored = s("v_made"), s("v_ready"), s("v_stored")
            k_sum, k_hi, k_rest, k_mid = s("k_sum"), s("k_hi"), s("k_rest"), s("k_mid")
            parts_ready, parts_stored = [s("q_parts"), s("k_parts")], [s("q_stored"), s("k_stored")]
        else:
            x_in, o_in, rden, in_loaded = env["x_in"], env["o_in"], env["rden"], env["in_loaded"]
            x_biased = sb("x_biased", [P, TILES, DIM])
            o_norm = sb("o_norm", [P, CHUNK])
            merged = s("merged")
            merge_step, o_ready, proj_made = s("merge_step"), s("o_ready"), s("proj_made")

        block = own.enter_context(nc.Block())

        @block.sync
        def _(sp):
            def load(c):
                if first:
                    sp.dma_start(x_ln[:, c.half], env["x_tiles"][c.n]).then_inc(ln_loaded[c.half], 16)
                else:
                    load_merge(sp, env, c)

            def load_residual(c):
                sp.dma_start(x[:, c.half], env["x_tiles"][c.n]).then_inc(x_loaded[c.half], 16)

            def store_qkv(c):
                sp.wait_ge(v_ready, c.n + 1)
                for g in range(HG):
                    sp.dma_start(env["v_chunk"][c.batch, c.half][:, g], v_ext[:, g].rearrange("p t c -> p (t c)")
                                 ).then_inc(v_stored, 16)
                for side in range(2):
                    sp.wait_ge(parts_ready[side], c.n + 1)
                    sp.dma_start(env["part_chunk"][side][c.batch, c.half], parts[:, side]
                                 ).then_inc(parts_stored[side], 16)

            def lead():
                if first:
                    load_residual(Chunk(0, 0))
                    load_residual(Chunk(0, 1))
                else:
                    load_sums(sp, env, BATCH - 1)
                    store_reciprocals(sp, env, BATCH - 1)
                    sp.wait_ge(env["den_stored"], 16 * BATCH)

            def body(c, end):
                if not end and c.loads_ahead:
                    sp.wait_ge(norm_ready if first else merged, c.n + 1)
                    load(c.next(2))
                if first and c.at_least >= 1:
                    store_qkv(c.next(-1))
                sp.wait_ge(res_ready, c.n + 1)
                sp.dma_start((env["x1_tiles"] if first else env["out_tiles"])[c.n], res[:, :, :]
                             ).then_inc(res_stored, 16)
                if first and not end and c.loads_ahead:
                    load_residual(c.next(2))

            def tail(c):
                if first:
                    store_qkv(c)
                    sp.wait_ge(v_stored, 16 * HG * CHUNKS)
                    for side in range(2):
                        sp.wait_ge(parts_stored[side], 16 * CHUNKS)
                sp.wait_ge(res_stored, 16 * CHUNKS)

            in_chunks(sp, lead, body, tail)

        @block.tensor
        def _(pe):
            def times_weights(out, col, x_t):
                for i, (w, part) in enumerate(((w_hi, 0), (w_hi, 1), (w_lo, 0))):
                    last = nc.tensor.matmul(out, w[:, col:col + P], x_t[:, part, :], start=(i == 0), stop=(i == 2))
                return last

            def project(c):
                pe.wait_ge(o_ready, c.n + 1)
                if c.at_least >= 1:
                    pe.wait_ge(merge_step, c.n)
                for t in range(TILES):
                    last = nc.tensor.matmul(ps_q[:, 0, t * P:(t + 1) * P], o_norm[:, t * P:(t + 1) * P],
                                            proj_t[:, :], start=True, stop=True)
                last.then_inc(proj_made, 1)

            def turn(c):
                pe.wait_ge(norm_ready, c.n + 1)
                if c.at_least >= 1:
                    pe.wait_ge(xt_ready, c.n)
                if first and c.at_least >= 3:
                    pe.wait_ge(xt2_ready, c.n - 2)
                for t in range(TILES):
                    last = nc.tensor.transpose(ps_t[:, t * P:(t + 1) * P], xn[:, t, :], ident[:, :])
                last.then_inc(turned, 1)

            def gate(c):
                pe.wait_ge(xt_ready, c.n + 1)
                if c.at_least >= 1:
                    pe.wait_ge(gate_exp, c.n)
                times_weights(ps_g[:, :], 0, xn_t[:, c.half]).then_inc(gate_made, 1)

            def turn_gate(c):
                pe.wait_ge(gate_copied, c.n + 1)
                for t in range(TILES):
                    last = nc.tensor.transpose(ps_g[:, t * P:(t + 1) * P], logit_t[:, t * P:(t + 1) * P],
                                               ident[:, :])
                last.then_inc(gate_turned, 1)

            def hidden(c, m):
                if not (c.at_least == 0 and m < 2):
                    pe.wait_ge(relu_ready, HT * c.n + m - 1)
                times_weights(ps_h[:, m % 2, :], IN_COL + m * P, xn_t[:, c.half]).then_inc(hid_made, 1)

            def spread_coef(c, m):
                if m == 1 and first and c.at_least >= 2:
                    pe.wait_ge(turn_ready, 4 * (c.n - 1))
                    pe.wait_ge(norms_read, c.n - 1)
                if not (c.at_least == 0 and m <= 1):
                    pe.wait_ge(scaled_ready, RT * c.n + m - 1)
                for t in range(TILES):
                    last = nc.tensor.transpose(wide_bank[m % 2][:, t * P:(t + 1) * P],
                                               coef_wide[:, t, m * P:(m + 1) * P], ident[:, :])
                last.then_inc(spread, 1)

            def outputs(c, tiles):
                if tiles[0] == 0 and c.at_least >= 1:
                    pe.wait_ge(res_ready, c.n)
                for t in tiles:
                    for m in range(HT):
                        if t == 0:
                            if m < ST:
                                pe.wait_ge(sq_pool, ST * c.n + m + 1)
                            else:
                                pe.wait_ge(scaled_ready, RT * c.n + m - ST + 1)
                        last = nc.tensor.matmul(ps_o[:, t, :], hid[:, m, t * P:(t + 1) * P], w_out[:, m, :],
                                                start=(m == 0), stop=(m == HT - 1))
                if tiles[-1] == TILES - 1:
                    last.then_inc(ffn_made, 1)

            def turn2(c, turns):
                pe.wait_ge(norm2_ready, c.n + 1)
                pe.wait_ge(xt_ready, turns)
                if c.at_least >= 1:
                    pe.wait_ge(xt2_ready, c.n)
                for t in range(TILES):
                    last = nc.tensor.transpose(ps_t[:, t * P:(t + 1) * P], xn2[:, t, :], ident[:, :])
                last.then_inc(turned2, 1)

            def qkv(c):
                pe.wait_ge(xt2_ready, c.n + 1)
                for i, col in enumerate((QKV_COL, ROT_COL, QKV_COL + DIM, ROT_COL + DIM)):
                    if i == 0 and c.at_least >= 1:
                        pe.wait_ge(norms_read, c.n)
                    elif i > 1:
                        pe.wait_ge(turn_ready, 4 * c.n + i - 1)
                    times_weights(ps_q[:, i % 2, :], col, xn2_t).then_inc(qk_made, 1)
                pe.wait_ge(turn_ready, 4 * c.n + 3)
                for t in range(TILES):
                    col = QKV_COL + 2 * DIM
                    for i, (part, w) in enumerate(((0, w_hi), (1, w_hi), (0, w_lo))):
                        last = nc.tensor.matmul(ps_q[:, 0, t * P:(t + 1) * P], xn2_t[:, part, t * P:(t + 1) * P],
                                                w[:, col:col + DIM], start=(i == 0), stop=(i == 2))
                last.then_inc(v_made, 1)

            def norms(c):
                pe.wait_ge(squares_ready, c.n + 1)
                pe.wait_ge(v_ready, c.n + 1)
                pe.wait_ge(turn_ready, 4 * c.n + 4)
                for side in range(2):
                    last = nc.tensor.matmul(ps_q[0:HEADS, side, :], headsum[:, :], squares[:, side, :],
                                            start=True, stop=True)
                last.then_inc(norms_made, 1)

            def lead():
                pe.wait_ge(env["w_ready"], 2)
                if not first:
                    project(Chunk(0, 0))
                turn(Chunk(0, 0))
                gate(Chunk(0, 0))
                turn_gate(Chunk(0, 0))

            def body(c, end):
                if not first and not end:
                    project(c.next())
                for m in range(ST):
                    hidden(c, m)
                if first and c.at_least >= 2:
                    norms(c.next(-2))
                hidden(c, ST)
                pe.wait_ge(wide_ready, c.n + 1)
                for m in range(RT):
                    if m + 1 < RT:
                        hidden(c, ST + m + 1)
                    spread_coef(c, m)
                    if m == 0 and not end:
                        turn(c.next())
                    if m == 2 and not end:
                        gate(c.next())
                if first and c.at_least >= 1:
                    turn2(c.next(-1), c.n + (1 if end else 2))
                if not end:
                    turn_gate(c.next())
                outputs(c, [0])
                if first and c.at_least >= 1:
                    qkv(c.next(-1))
                outputs(c, range(1, TILES))

            def tail(c):
                if first:
                    norms(c.next(-1))
                    turn2(c, CHUNKS)
                    qkv(c)
                    norms(c)

            in_chunks(pe, lead, body, tail)

        @block.scalar
        def _(act):
            def copy(dst, src):
                return nc.scalar.activation(dst, src, ACT.Copy)

            def take_xt(c):
                act.wait_ge(turned, c.n + 1)
                if c.at_least >= 2:
                    act.wait_ge(hid_made, HT * (c.n - 1))
                copy(xn_t[:, c.half, 0, :], ps_t[:, :]).then_inc(xt_high, 1)

            def take_logits(c):
                act.wait_ge(gate_made, c.n + 1)
                if c.at_least >= 1:
                    act.wait_ge(gate_turned, c.n)
                copy(logit_t[:, :], ps_g[:, :]).then_inc(gate_copied, 1)

            def exp_logits(c):
                act.wait_ge(gate_turned, c.n + 1)
                if c.at_least >= 1:
                    act.wait_ge(coef_ready, c.n)
                nc.scalar.activation(en[:, :, :], ps_g[:, :].rearrange("p (t e) -> p t e", e=P)[:, :, 0:EXPERTS],
                                     ACT.Exp, scale=-1.0).then_inc(gate_exp, 1)

            def widen(c):
                act.wait_ge(coef_ready, c.n + 1)
                if c.at_least >= 1:
                    act.wait_ge(spread, RT * c.n)
                for t in range(TILES):
                    last = copy(coef_wide[:, t, :].rearrange("p (e i) -> p e i", i=INTER),
                                coef[:, t, :].unsqueeze(2).broadcast_to([P, EXPERTS, INTER]))
                last.then_inc(wide_ready, 1)

            def relus(c, m):
                act.wait_ge(hid_made, HT * c.n + m + 1)
                if c.at_least >= 1:
                    if m < ST:
                        act.wait_ge(sq_pool, ST * (c.n - 1) + m + 1)
                    else:
                        act.wait_ge(sq_act, RT * (c.n - 1) + m - ST + 1)
                nc.scalar.activation(relu[:, m, :], ps_h[:, m % 2, :], ACT.Relu).then_inc(relu_ready, 1)

            def squares_of(c, m):
                act.wait_ge(relu_ready, HT * c.n + ST + m + 1)
                if c.at_least >= 1:
                    act.wait_ge(scaled_ready, RT * (c.n - 1) + m + 1)
                nc.scalar.activation(squared[:, m, :], relu[:, ST + m, :], ACT.Square).then_inc(sq_act, 1)

            def v_of(g):
                return v_ext[:, g, :, :].rearrange("p t (j c) -> p t j c", c=VW)[:, :, :, 0:HD]

            def take_xt2(c):
                act.wait_ge(turned2, c.n + 1)
                if c.at_least >= 1:
                    act.wait_ge(v_made, c.n)
                copy(xn2_t[:, 0, :], ps_t[:, :]).then_inc(xt2_high, 1)

            def take_v(c):
                act.wait_ge(v_made, c.n + 1)
                if c.at_least >= 1:
                    act.wait_ge(v_stored, 16 * HG * c.n)
                else:
                    act.wait_ge(ones_set, 1)
                v_ps = ps_q[:, 0, :].rearrange("p (t g j c) -> p g t j c", t=TILES, g=HG, c=HD)
                for g in range(HG):
                    last = copy(v_of(g), v_ps[:, g])
                last.then_inc(v_ready, 1)

            def k_parts(c):
                act.wait_ge(k_sum, c.n + 1)
                if c.at_least >= 1:
                    act.wait_ge(parts_stored[1], 16 * c.n)
                copy(parts[:, 1, 0, :], roped[:, 1, :]).then_inc(k_hi, 1)
                act.wait_ge(k_rest, c.n + 1)
                copy(parts[:, 1, 1, :], left[:, 1, :]).then_inc(k_mid, 1)

            def body(c, end):
                for m in range(ST):
                    relus(c, m)
                for m in range(RT):
                    relus(c, ST + m)
                    squares_of(c, m)
                    if m == 1 and not end:
                        take_xt(c.next())
                if not end:
                    take_logits(c.next())
                if first and c.at_least >= 1:
                    take_xt2(c.next(-1))
                if not end:
                    exp_logits(c.next())
                if first and c.at_least >= 1:
                    take_v(c.next(-1))
                    k_parts(c.next(-1))
                if not end:
                    widen(c.next())

            def lead():
                take_xt(Chunk(0, 0))
                take_logits(Chunk(0, 0))
                exp_logits(Chunk(0, 0))
                widen(Chunk(0, 0))

            def tail(c):
                if first:
                    fill_bias_rows(on_scalar(nc), env, env["head_scale"], (env["q_op"][0], env["k_op"][0]))
                    take_xt2(c)
                    take_v(c)
                    act.wait_ge(rope_step, 4 * c.n + 1)
                    act.wait_ge(k_sum, c.n + 1)
                    act.wait_ge(norms_made, c.n)
                    nc.scalar.activation(squares[:, :, :], roped[:, :, :], ACT.Square).then_inc(squares_ready, 1)
                    k_parts(c)

            in_chunks(act, lead, body, tail)

        @block.gpsimd
        def _(pool):
            def power(c, which, step):
                pool.wait_ge(step, 4 * c.n + 4)
                nc.gpsimd.tensor_tensor(rstd[:, which, :], veps[:, which, :], minus_half[:, :],
                                        ALU.pow).then_inc(rstd_ready[which], 1)

            def square(c, m):
                pool.wait_ge(relu_ready, HT * c.n + m + 1)
                if c.at_least >= 1:
                    pool.wait_ge(ffn_made, c.n)
                nc.gpsimd.tensor_tensor(hid[:, m, :], relu[:, m, :], relu[:, m, :], ALU.mult).then_inc(sq_pool, 1)

            def k_side(c):
                pool.wait_ge(turn_ready, 4 * c.n + 4)
                nc.gpsimd.tensor_tensor(roped[:, 1, :], turn_a[:, 1, :], turn_b[:, 1, :], ALU.add).then_inc(k_sum, 1)
                pool.wait_ge(k_hi, c.n + 1)
                nc.gpsimd.tensor_tensor(left[:, 1, :], roped[:, 1, :], parts[:, 1, 0, :],
                                        ALU.subtract).then_inc(k_rest, 1)
                pool.wait_ge(k_mid, c.n + 1)
                nc.gpsimd.tensor_tensor(parts[:, 1, 2, :], left[:, 1, :], parts[:, 1, 1, :],
                                        ALU.subtract).then_inc(parts_ready[1], 1)

            def square_qk(c):
                pool.wait_ge(rope_step, 4 * c.n + 1)
                pool.wait_ge(k_sum, c.n + 1)
                if c.at_least >= 1:
                    pool.wait_ge(norms_made, c.n)
                nc.gpsimd.tensor_tensor(squares[:, :, :], roped[:, :, :], roped[:, :, :],
                                        ALU.mult).then_inc(squares_ready, 1)

            def lead():
                if first:
                    nc.gpsimd.memset(v_ext[:, :, :, :], 1.0).then_inc(ones_set, 1)
                nc.gpsimd.memset(minus_half[:, :], -0.5).then_inc(half_set, 1)
                pool.wait_ge(half_set, 1)
                power(Chunk(0, 0), 0, norm_step)
                if first:
                    power(Chunk(0, 1), 0, norm_step)

            def body(c, end):
                if not first and not end:
                    power(c.next(), 0, norm_step)
                for m in range(ST):
                    square(c, m)
                if first and c.loads_ahead:
                    power(c.next(2), 0, norm_step)
                if first and c.at_least >= 1:
                    k_side(c.next(-1))
                    square_qk(c.next(-1))
                if first:
                    power(c, 1, norm2_step)

            def tail(c):
                if first:
                    k_side(c)

            in_chunks(pool, lead, body, tail)

        @block.vector
        def _(dve):
            v = nc.vector

            def moments(src, which, step, n):
                at = 4 * n
                for t in range(TILES):
                    last = v.bn_stats(stats[:, which, t, :], src[:, t, :])
                last.then_inc(step, 1)
                dve.wait_ge(step, at + 1)
                even, odd = stats[:, which, :, 1], stats[:, which, :, 4]
                v.tensor_tensor(mean2[:, which, :], even, odd, ALU.add)
                v.tensor_tensor(apart[:, which, :], even, odd, ALU.subtract)
                v.tensor_tensor(var_n[:, which, :], stats[:, which, :, 2], stats[:, which, :, 5],
                                ALU.add).then_inc(step, 1)
                dve.wait_ge(step, at + 2)
                v.tensor_scalar(mean[:, which, :], mean2[:, which, :], 0.5, None, ALU.mult)
                v.tensor_tensor(apart2[:, which, :], apart[:, which, :], apart[:, which, :], ALU.mult)
                v.tensor_scalar(var_in[:, which, :], var_n[:, which, :], 1.0 / DIM, EPS, ALU.mult,
                                ALU.add).then_inc(step, 1)
                dve.wait_ge(step, at + 3)
                v.scalar_tensor_tensor(out=veps[:, which, :], in0=apart2[:, which, :], scalar=0.25,
                                       in1=var_in[:, which, :], op0=ALU.mult, op1=ALU.add).then_inc(step, 1)

            def centre(src, dst, which, n, t):
                if t == 0:
                    dve.wait_ge(rstd_ready[which], n + 1)
                return v.tensor_scalar(dst[:, t, :], src[:, t, :], mean[:, which, t:t + 1],
                                       rstd[:, which, t:t + 1], ALU.subtract, ALU.mult)

            def normalise_o(c):
                dve.wait_ge(in_loaded[c.half], 48 * c.seen)
                if c.at_least >= 1:
                    dve.wait_ge(proj_made, c.n)
                    dve.wait_ge(merge_step, c.n)
                v.tensor_tensor(o_norm[:, :], o_in[:, c.half, :], rden[:, c.half, :], ALU.mult).then_inc(o_ready, 1)
                v.tensor_tensor(x_biased[:, :, :], x_in[:, c.half],
                                proj_bias[:, :].unsqueeze(1).broadcast_to([P, TILES, DIM]),
                                ALU.add).then_inc(merged, 1)

            def merge(c):
                dve.wait_ge(merged, c.n + 1)
                dve.wait_ge(proj_made, c.n + 1)
                if c.at_least >= 2:
                    dve.wait_ge(res_ready, c.n - 1)
                v.tensor_tensor(x[:, c.half], x_biased[:, :, :], ps_q[:, 0, :].rearrange("p (t c) -> p t c", c=DIM),
                                ALU.add).then_inc(merge_step, 1)
                dve.wait_ge(merge_step, c.n + 1)

            def take_low(c):
                dve.wait_ge(xt_high, c.n + 1)
                if c.at_least >= 2:
                    dve.wait_ge(hid_made, HT * (c.n - 1))
                v.tensor_tensor(xn_t[:, c.half, 1, :], ps_t[:, :], xn_t[:, c.half, 0, :],
                                ALU.subtract).then_inc(xt_ready, 1)

            def take_low2(c):
                dve.wait_ge(xt2_high, c.n + 1)
                if c.at_least >= 1:
                    dve.wait_ge(v_made, c.n)
                v.tensor_tensor(xn2_t[:, 1, :], ps_t[:, :], xn2_t[:, 0, :], ALU.subtract).then_inc(xt2_ready, 1)

            def norm_source(c):
                return x_ln[:, c.half] if first else x[:, c.half]

            def norm_moments(c):
                if first:
                    dve.wait_ge(ln_loaded[c.half], 16 * c.seen)
                moments(norm_source(c), 0, norm_step, c.n)

            def norm_centre(c):
                if c.at_least >= 1:
                    dve.wait_ge(turned, c.n)
                for t in range(TILES):
                    last = centre(norm_source(c), xn, 0, c.n, t)
                last.then_inc(norm_ready, 1)

            def norm2(c, t):
                if t == 0 and c.at_least >= 1:
                    dve.wait_ge(turned2, c.n)
                last = centre(res, xn2, 1, c.n, t)
                if t == TILES - 1:
                    last.then_inc(norm2_ready, 1)

            def route(c):
                r = ROUTE_STEPS * c.n
                dve.wait_ge(gate_exp, c.n + 1)
                v.tensor_scalar(en1[:, :, :], en[:, :, :], 1.0, None, ALU.add).then_inc(route_step, 1)
                dve.wait_ge(route_step, r + 1)
                v.reciprocal(score[:, :, :], en1[:, :, :]).then_inc(route_step, 1)
                dve.wait_ge(route_step, r + 2)
                v.tensor_tensor(sfc[:, :, :], score[:, :, :], corr[:, :].unsqueeze(1).broadcast_to(
                    [P, TILES, EXPERTS]), ALU.add).then_inc(route_step, 1)
                dve.wait_ge(route_step, r + 3)
                four = sfc[:, :, :].rearrange("p t (g e) -> p (t g) e", e=PER_GROUP)
                v.tensor_tensor(pair_sum[:, :, 0:3], four[:, :, 0:3], four[:, :, 1:4], ALU.add)
                v.tensor_tensor(pair_sum[:, :, 3:5], four[:, :, 0:2], four[:, :, 2:4], ALU.add)
                v.tensor_tensor(pair_sum[:, :, 5:6], four[:, :, 0:1], four[:, :, 3:4],
                                ALU.add).then_inc(route_step, 1)
                dve.wait_ge(route_step, r + 4)
                v.tensor_reduce(gsum[:, :, :].rearrange("p t g -> p (t g)"), pair_sum[:, :, :],
                                AX.X, ALU.max).then_inc(route_step, 1)
                dve.wait_ge(route_step, r + 5)
                v.tensor_tensor(gmask[:, :, 0:1], gsum[:, :, 0:1], gsum[:, :, 1:2], ALU.is_ge)
                v.tensor_tensor(gmask[:, :, 1:2], gsum[:, :, 1:2], gsum[:, :, 0:1],
                                ALU.is_gt).then_inc(route_step, 1)
                dve.wait_ge(route_step, r + 6)
                v.tensor_tensor(kept[:, :, :].rearrange("p t (g e) -> p (t g) e", e=PER_GROUP), four,
                                gmask[:, :, :].rearrange("p t g -> p (t g)").unsqueeze(2).broadcast_to(
                                    [P, TILES * GROUPS, PER_GROUP]), ALU.mult).then_inc(route_step, 1)
                dve.wait_ge(route_step, r + 7)
                wide = [P, TILES, EXPERTS, EXPERTS]
                mine = kept[:, :, :].unsqueeze(3).broadcast_to(wide)
                other = kept[:, :, :].unsqueeze(2).broadcast_to(wide)
                above4 = above[:, :, :].rearrange("p t (a b) -> p t a b", a=EXPERTS)
                equal4 = equal[:, :, :].rearrange("p t (a b) -> p t a b", a=EXPERTS)
                v.tensor_tensor(above4, other, mine, ALU.is_gt)
                v.tensor_tensor(equal4, other, mine, ALU.is_equal).then_inc(route_step, 1)
                dve.wait_ge(route_step, r + 8)
                v.tensor_tensor(equal[:, :, :], equal[:, :, :],
                                earlier[:, :, :].rearrange("p a b -> p (a b)").unsqueeze(1).broadcast_to(
                                    [P, TILES, EXPERTS * EXPERTS]), ALU.mult).then_inc(route_step, 1)
                dve.wait_ge(route_step, r + 9)
                v.tensor_tensor(above[:, :, :], above[:, :, :], equal[:, :, :], ALU.add).then_inc(route_step, 1)
                dve.wait_ge(route_step, r + 10)
                v.tensor_reduce(rank[:, :, :], above4, AX.X, ALU.add).then_inc(route_step, 1)
                dve.wait_ge(route_step, r + 11)
                v.scalar_tensor_tensor(out=chosen[:, :, :], in0=rank[:, :, :], scalar=2.0, in1=score[:, :, :],
                                       op0=ALU.is_lt, op1=ALU.mult).then_inc(route_step, 1)
                dve.wait_ge(route_step, r + 12)
                v.tensor_reduce(csum[:, :], chosen[:, :, :], AX.X, ALU.add).then_inc(route_step, 1)
                dve.wait_ge(route_step, r + 13)
                v.tensor_scalar(csum1[:, :], csum[:, :], 1e-20, None, ALU.add).then_inc(route_step, 1)
                dve.wait_ge(route_step, r + 14)
                v.reciprocal(crec[:, :], csum1[:, :]).then_inc(route_step, 1)
                dve.wait_ge(route_step, r + 15)
                if c.at_least >= 1:
                    dve.wait_ge(wide_ready, c.n)
                v.tensor_tensor(coef[:, :, :], chosen[:, :, :],
                                crec[:, :].unsqueeze(2).broadcast_to([P, TILES, EXPERTS]),
                                ALU.mult).then_inc(coef_ready, 1)

            def scale(c, m):
                if c.at_least >= 1:
                    dve.wait_ge(ffn_made, c.n)
                dve.wait_ge(sq_act, RT * c.n + m + 1)
                dve.wait_ge(spread, RT * c.n + m + 1)
                v.tensor_tensor(hid[:, ST + m, :], squared[:, m, :], wide_bank[m % 2], ALU.mult).then_inc(scaled_ready, 1)

            def residual(c):
                dve.wait_ge(ffn_made, c.n + 1)
                if first:
                    dve.wait_ge(x_loaded[c.half], 16 * c.seen)
                if c.at_least >= 1:
                    dve.wait_ge(res_stored, 16 * c.n)
                v.scalar_tensor_tensor(out=res[:, :, :], in0=ps_o[:, :, :], scalar=0.5, in1=x[:, c.half],
                                       op0=ALU.mult, op1=ALU.add).then_inc(res_ready, 1)
                if first:
                    dve.wait_ge(res_ready, c.n + 1)
                    moments(res, 1, norm2_step, c.n)

            def rotary_products(c):
                at = slice(c.half * CHUNK, (c.half + 1) * CHUNK)
                for side in range(2):
                    if side == 1 and c.at_least >= 1:
                        dve.wait_ge(k_sum, c.n)
                    for i, dst in enumerate((turn_a, turn_b)):
                        dve.wait_ge(qk_made, 4 * c.n + 2 * side + i + 1)
                        v.tensor_tensor(dst[:, side, :], ps_q[:, i, :], rope[:, 2 * side + i, at],
                                        ALU.mult).then_inc(turn_ready, 1)

            def rotary_q(c):
                dve.wait_ge(turn_ready, 4 * c.n + 2)
                if c.at_least >= 1:
                    dve.wait_ge(squares_ready, c.n)
                v.tensor_tensor(roped[:, 0, :], turn_a[:, 0, :], turn_b[:, 0, :], ALU.add).then_inc(rope_step, 1)
                dve.wait_ge(rope_step, 4 * c.n + 1)
                if c.at_least >= 1:
                    dve.wait_ge(parts_stored[0], 16 * c.n)
                v.tensor_copy(parts[:, 0, 0, :], roped[:, 0, :]).then_inc(rope_step, 1)
                dve.wait_ge(rope_step, 4 * c.n + 2)
                v.tensor_tensor(left[:, 0, :], roped[:, 0, :], parts[:, 0, 0, :], ALU.subtract).then_inc(rope_step, 1)
                dve.wait_ge(rope_step, 4 * c.n + 3)
                v.tensor_copy(parts[:, 0, 1, :], left[:, 0, :]).then_inc(rope_step, 1)
                dve.wait_ge(rope_step, 4 * c.n + 4)
                v.tensor_tensor(parts[:, 0, 2, :], left[:, 0, :], parts[:, 0, 1, :],
                                ALU.subtract).then_inc(parts_ready[0], 1)

            def largest_norms(c):
                dve.wait_ge(norms_made, c.n + 1)
                v.tensor_reduce(env["norm_max"][:, :, bass.ds(c.n, 1)].rearrange("h s c -> h (s c)"), ps_q[0:HEADS, :, :],
                                AX.X, ALU.max).then_inc(norms_read, 1)

            def lead():
                dve.wait_ge(env["w_ready"], 2)
                if not first:
                    normalise_o(Chunk(0, 0))
                    merge(Chunk(0, 0))
                norm_moments(Chunk(0, 0))
                norm_centre(Chunk(0, 0))
                if first:
                    norm_moments(Chunk(0, 1))
                take_low(Chunk(0, 0))
                if first:
                    norm_centre(Chunk(0, 1))
                else:
                    normalise_o(Chunk(0, 1))
                    reciprocals(nc, dve, env, BATCH - 1)
                route(Chunk(0, 0))
                if first:
                    dve.wait_ge(rope_loaded, 16)

            def body(c, end):
                if not first and not end:
                    merge(c.next())
                    norm_moments(c.next())
                    norm_centre(c.next())
                if first and c.at_least >= 2:
                    largest_norms(c.next(-2))
                for m in range(RT):
                    scale(c, m)
                    if first and c.at_least >= 1:
                        for t in ((0, 1), (2,), (3,), ())[m]:
                            norm2(c.next(-1), t)
                    if m == 1 and not end:
                        take_low(c.next())
                if first and c.loads_ahead:
                    norm_moments(c.next(2))
                if first and c.at_least >= 1:
                    take_low2(c.next(-1))
                    rotary_products(c.next(-1))
                if not first and c.loads_ahead:
                    normalise_o(c.next(2))
                if not end:
                    route(c.next())
                if first and c.loads_ahead:
                    norm_centre(c.next(2))
                if first and c.at_least >= 1:
                    rotary_q(c.next(-1))
                residual(c)

            def tail(c):
                if first:
                    largest_norms(c.next(-1))
                    for t in range(TILES):
                        norm2(c, t)
                    take_low2(c)
                    rotary_products(c)
                    rotary_q(c)
                    largest_norms(c)

            in_chunks(dve, lead, body, tail)


def load_merge(sp, env, c):
    half, loaded = c.half, env["in_loaded"][c.half]
    sp.dma_start(env["x_in"][:, half], env["x1_tiles"][c.n]).then_inc(loaded, 16)
    sp.dma_start(env["o_in"][:, half], env["o_chunk"][c.batch, half][:, 0:HD, :]).then_inc(loaded, 16)
    sp.dma_start(env["rden"][:, half], env["rden_chunk"][c.batch, half].unsqueeze(1)
                 .broadcast_to([HEADS, HD, CHUNK])).then_inc(loaded, 16)


def load_sums(sp, env, batch):
    sp.dma_start(env["den_all"][:, batch], env["den_batch"][batch]).then_inc(env["den_loaded"], 16)


def reciprocals(nc, dve, env, batch):
    dve.wait_ge(env["den_loaded"], 16 * max(batch + 1, BATCH - 1))
    nc.vector.reciprocal(env["den_rec"][:, batch], env["den_all"][:, batch]).then_inc(env["den_turned"], 1)


def store_reciprocals(sp, env, batch):
    sp.wait_ge(env["den_turned"], batch + 1)
    sp.dma_start(env["rden_batch"][batch], env["den_rec"][:, batch]).then_inc(env["den_stored"], 16)


def load_parts(sp, env, group, q_op, k_op, loaded):
    for a in range(PARTS):
        for b in range(PARTS):
            at = HD * (PARTS * a + b)
            sp.dma_start(q_op[at:at + HD], env["part_group"][0][group, b]).then_inc(loaded, 16)
            sp.dma_start(k_op[at:at + HD], env["part_group"][1][group, a]).then_inc(loaded, 16)


PART_LOADS = 2 * PARTS * PARTS


def on_vector(nc):
    return lambda out, in_, factor: nc.vector.tensor_scalar(out, in_, factor, None, ALU.mult)


def on_scalar(nc):
    return lambda out, in_, factor: nc.scalar.activation(out, in_, ACT.Copy, scale=factor)


def fill_bias_row(multiply, env, now, ops, n):
    br = slice(BIAS_ROW, FULL_K)
    j, side = divmod(n, 2)
    return multiply(ops[side][br, j, :], env["bias_rows"][br, side, :], now[br, j, 1 + side:2 + side])


def fill_bias_rows(multiply, env, now, ops):
    for n in range(2 * GH):
        last = fill_bias_row(multiply, env, now, ops, n)
    return last


def pieces(limit):
    cuts = sorted({0, CHUNK, SEQ, limit})
    return [(lo, hi, hi <= limit) for lo, hi in zip(cuts, cuts[1:])]


def bound_shift(nc, sem, env):
    norm_max, bound_ok, ident = env["norm_max"], env["bound_ok"], env["ident"]
    ones = env["ones"]
    with ExitStack() as own:
        def sb(name, shape, dt=F32):
            return own.enter_context(nc.sbuf_tensor(f"bs_{name}", shape, dt))

        product = sb("product", [HEADS, BATCH])
        both = sb("both", [HEADS, 2, BATCH])
        bound = sb("bound", [HEADS, BATCH])
        half = sb("half", [HEADS, BATCH])
        within = sb("within", [HEADS, BATCH])
        all_within = sb("all_within", [HEADS, 1])
        minus = sb("minus", [HEADS, BATCH])
        left = sb("left", [HEADS, BATCH])
        hi, mid = sb("hi", [HEADS, BATCH], BF16), sb("mid", [HEADS, BATCH], BF16)
        part = sb("part", [HEADS, PARTS, BATCH])
        shift = env["bound_rows"]
        ps = own.enter_context(nc.psum_tensor("bs_ps", [P, CHUNK], F32))
        step, rooted, turned = sem("bs_step"), sem("bs_rooted"), sem("bs_turned")
        half_set, ready, judged = sem("bs_half_set"), sem("bs_ready"), sem("bs_judged")
        rows = [(a, b) for a in range(PARTS) for b in range(BATCH)]

        def widen(multiply, a, b):
            return multiply(shift[:, a, b, :], ones[:, :], part[:, a, b:b + 1])

        block = own.enter_context(nc.Block())

        @block.gpsimd
        def _(pool):
            nc.gpsimd.memset(half[:, :], 0.5).then_inc(half_set, 1)
            pool.wait_ge(half_set, 1)
            pool.wait_ge(step, 2)
            nc.gpsimd.tensor_tensor(bound[:, :], product[:, :], half[:, :], ALU.pow).then_inc(rooted, 1)

        @block.tensor
        def _(pe):
            pe.wait_ge(judged, 1)
            nc.tensor.transpose(ps[0:1, 0:HEADS], all_within[:, :], ident[0:HEADS, 0:HEADS]).then_inc(turned, 1)

        @block.vector
        def _(dve):
            v = nc.vector
            v.tensor_reduce(both[:, :, :], norm_max[:, :, :].rearrange("h s (b c) -> h s b c", c=HALVES),
                            AX.X, ALU.max).then_inc(step, 1)
            dve.wait_ge(step, 1)
            v.tensor_tensor(product[:, :], both[:, 0, :], both[:, 1, :], ALU.mult).then_inc(step, 1)
            dve.wait_ge(rooted, 1)
            v.tensor_scalar(within[:, :], bound[:, :], SHIFT_LIMIT, None, ALU.is_le).then_inc(step, 1)
            dve.wait_ge(step, 3)
            v.tensor_reduce(all_within[:, :], within[:, :], AX.X, ALU.min).then_inc(judged, 1)
            v.tensor_scalar(minus[:, :], bound[:, :], -1.0, None, ALU.mult).then_inc(step, 1)
            dve.wait_ge(step, 4)
            v.tensor_copy(hi[:, :], minus[:, :]).then_inc(step, 1)
            dve.wait_ge(step, 5)
            v.tensor_copy(part[:, 0, :], hi[:, :])
            v.tensor_tensor(left[:, :], minus[:, :], hi[:, :], ALU.subtract).then_inc(step, 1)
            dve.wait_ge(step, 6)
            v.tensor_copy(mid[:, :], left[:, :]).then_inc(step, 1)
            dve.wait_ge(step, 7)
            v.tensor_copy(part[:, 1, :], mid[:, :])
            v.tensor_tensor(part[:, 2, :], left[:, :], mid[:, :], ALU.subtract).then_inc(step, 1)
            dve.wait_ge(step, 8)
            for a, b in rows[3:]:
                last = widen(on_vector(nc), a, b)
            last.then_inc(ready, 1)
            dve.wait_ge(turned, 1)
            v.tensor_reduce(bound_ok[:, :], ps[0:1, 0:HEADS], AX.X, ALU.min).then_inc(step, 1)

        @block.scalar
        def _(act):
            act.wait_ge(step, 8)
            for a, b in rows[:3]:
                last = widen(on_scalar(nc), a, b)
            last.then_inc(ready, 1)

        @block.sync
        def _(sp):
            load_parts(sp, env, 0, env["q_op"][0], env["k_op"][0], env["qk_loaded"][0])
            sp.wait_ge(ready, 2)
            for a in range(PARTS):
                row = env["q_op"][0][SHIFT_ROW + a:SHIFT_ROW + a + 1]
                sp.dma_start(row, shift[0:GH, a, 0, :]).then_inc(env["first_shift"], 16)
            for a in range(PARTS):
                sp.dma_start(env["shift_heads"][a], shift[:, a]).then_inc(env["shift_stored"], 16)


def exact_maxima(nc, sem, env):
    ident, diag, head_scale, bound_ok = env["ident"], env["diag"], env["head_scale"], env["bound_ok"]
    with ExitStack() as own:
        def sb(name, shape, dt=F32):
            return own.enter_context(nc.sbuf_tensor(f"mx_{name}", shape, dt))

        def s(name):
            return sem(f"mx_{name}")

        q_op, k_op = env["q_op"][1], env["k_op"][1]
        now = sb("now", [P, 2, GH, 3])
        largest = sb("largest", [P, UNITS])
        largest_t = sb("largest_t", [UNITS, P])
        rest = sb("rest", [UNITS, P])
        shift = sb("shift", [UNITS, PARTS, P], BF16)
        scores = own.enter_context(nc.psum_tensor("mx_scores", [P, 2, SEQ], F32))
        ps_t = own.enter_context(nc.psum_tensor("mx_ps_t", [P, CHUNK], F32))
        loaded, now_set, bias_set = s("loaded"), s("now_set"), s("bias_set")
        scores_made, diag_added, reduced = s("scores_made"), s("diag_added"), s("reduced")
        turned, part_step, shift_ready, shift_stored = s("turned"), s("part_step"), s("shift_ready"), s("shift_stored")
        replaced = s("replaced")
        block = own.enter_context(nc.Block())

        @block.sync
        def _(sp):
            with sp.If(sp.value_load(bound_ok[0:1, 0:1], min_val=0, max_val=1) == 0):
                sp.wait_ge(env["shift_stored"], 16 * PARTS)
                load_parts(sp, env, 0, q_op, k_op, loaded)
                with sp.Fori(0, NGRP - 1) as g:
                    sp.wait_ge(scores_made, UNITS * (g + 1))
                    load_parts(sp, env, g + 1, q_op, k_op, loaded)
                    sp.wait_ge(shift_ready, g + 1)
                    sp.dma_start(env["shift_rows"][g], shift[:, :, :]).then_inc(shift_stored, 16)
                sp.wait_ge(shift_ready, NGRP)
                sp.dma_start(env["shift_rows"][NGRP - 1], shift[:, :, :]).then_inc(shift_stored, 16)
                sp.wait_ge(shift_stored, 16 * NGRP)
                sp.wait_ge(env["first_shift"], 16 * PARTS)
                sp.dma_start(env["q_op"][0][SHIFT_ROW:PLAIN_K], env["shift_group"][0]).then_inc(replaced, 16)
                sp.wait_ge(replaced, 16)

        @block.tensor
        def _(pe):
            with pe.If(pe.value_load(bound_ok[0:1, 0:1], min_val=0, max_val=1) == 0):
                with pe.Fori(0, NGRP) as g:
                    pe.wait_ge(loaded, 16 * PART_LOADS * (g + 1))
                    pe.wait_ge(bias_set, g + 1)
                    for j in range(GH):
                        for qt in range(KT):
                            u = KT * j + qt
                            pe.wait_ge(reduced, UNITS * g + u + 1)
                            for lo, hi, behind in pieces(qt * P):
                                rows = FULL_K if behind else PLAIN_K
                                last = nc.tensor.matmul(scores[:, u % 2, lo:hi], q_op[0:rows, j, qt * P:(qt + 1) * P],
                                                        k_op[0:rows, j, lo:hi], start=True, stop=True)
                            last.then_inc(scores_made, 1)
                    pe.wait_ge(reduced, UNITS * (g + 1) + 2)
                    nc.tensor.transpose(ps_t[0:UNITS, 0:P], largest[:, :], ident[:, :]).then_inc(turned, 1)

        @block.vector
        def _(dve):
            with dve.If(dve.value_load(bound_ok[0:1, 0:1], min_val=0, max_val=1) == 0):
                v = nc.vector
                v.memset(largest[:, :], 0.0).then_inc(reduced, 2)

                def fill(g, par):
                    v.tensor_copy(now[:, par], head_scale[:, bass.ds(GH * g, GH), :]).then_inc(now_set, 1)
                    dve.wait_ge(now_set, g + 1)
                    fill_bias_rows(on_vector(nc), env, now[:, par], (q_op, k_op)).then_inc(bias_set, 1)

                def group(g, par, end):
                    for j in range(GH):
                        for qt in range(KT):
                            u = KT * j + qt
                            dve.wait_ge(scores_made, UNITS * g + u + 1)
                            block_at = scores[:, u % 2, qt * P:(qt + 1) * P]
                            v.scalar_tensor_tensor(out=block_at, in0=diag[:, 1, :],
                                                   scalar=now[:, par, j, 0:1], in1=block_at,
                                                   op0=ALU.mult, op1=ALU.add).then_inc(diag_added, 1)
                            dve.wait_ge(diag_added, UNITS * g + u + 1)
                            v.tensor_reduce(largest[:, u:u + 1], scores[:, u % 2, :], AX.X, ALU.max).then_inc(reduced, 1)
                    if not end:
                        fill(g + 1, 1 - par)
                    dve.wait_ge(turned, g + 1)
                    v.tensor_scalar(largest_t[:, :], ps_t[0:UNITS, 0:P], -1.0, None, ALU.mult).then_inc(part_step, 1)
                    dve.wait_ge(part_step, 4 * g + 1)
                    if not isinstance(g, int) or g >= 1:
                        dve.wait_ge(shift_stored, 16 * g)
                    v.tensor_copy(shift[:, 0, :], largest_t[:, :]).then_inc(part_step, 1)
                    dve.wait_ge(part_step, 4 * g + 2)
                    v.tensor_tensor(rest[:, :], largest_t[:, :], shift[:, 0, :], ALU.subtract).then_inc(part_step, 1)
                    dve.wait_ge(part_step, 4 * g + 3)
                    v.tensor_copy(shift[:, 1, :], rest[:, :]).then_inc(part_step, 1)
                    dve.wait_ge(part_step, 4 * g + 4)
                    v.tensor_tensor(shift[:, 2, :], rest[:, :], shift[:, 1, :], ALU.subtract).then_inc(shift_ready, 1)

                fill(0, 0)
                group(0, 0, False)
                with dve.Fori(0, NGRP // 2 - 1) as pair:
                    group(2 * pair + 1, 1, False)
                    group(2 * pair + 2, 0, False)
                group(NGRP - 1, 1, True)


def attention(nc, sem, env):
    diag, head_scale = env["diag"], env["head_scale"]
    with ExitStack() as own:
        def sb(name, shape, dt=F32):
            return own.enter_context(nc.sbuf_tensor(f"at_{name}", shape, dt))

        def s(name):
            return sem(f"at_{name}")

        q_op, k_op = env["q_op"], env["k_op"]
        now = sb("now", [P, 2, GH, 3])
        v_op = [sb(f"v_op{i}", [P, KT, GH * VW]) for i in range(2)]
        weights = sb("weights", [P, PSTEPS, GH, SEQ])
        o_out = sb("o_out", [P, SEQ])
        start = sb("start", [1, 3])
        scores = own.enter_context(nc.psum_tensor("at_scores", [P, SLOTS, SEQ], F32))
        acc = own.enter_context(nc.psum_tensor("at_acc", [P, SEQ], F32))

        qk_loaded, v_loaded = env["qk_loaded"], [s("v_loaded0"), s("v_loaded1")]
        now_set, bias_set = s("now_set"), s("bias_set")
        scores_made, diag_added = s("scores_made"), s("diag_added")
        slots_free = s("slots_free")
        steps_free = s("steps_free")
        o_ready, o_stored = s("o_ready"), s("o_stored")
        block = own.enter_context(nc.Block())

        def in_groups(eng, body):
            body(0, 0, 0, False)
            with eng.Fori(0, NGRP // 2 - 1) as pair:
                body(2 * pair + 1, 1, pair, False)
                body(2 * pair + 2, 0, pair + 1, False)
            body(NGRP - 1, 1, NGRP // 2 - 1, True)

        @block.sync
        def _(sp):
            def load(g, par):
                load_parts(sp, env, g, q_op[par], k_op[par], qk_loaded[par])
                sp.dma_start(q_op[par][SHIFT_ROW:PLAIN_K], env["shift_group"][g]).then_inc(qk_loaded[par], 16)

            def load_v(g, par):
                sp.dma_start(v_op[par][:, :, :], env["v_group"][g]).then_inc(v_loaded[par], 16)

            def store(g):
                sp.wait_ge(o_ready, 2 * g + 4)
                for j in range(GH):
                    sp.dma_start(env["o_group"][g, j], o_out[32 * j:32 * j + VW, :]).then_inc(o_stored, 16)

            load_v(0, 0)
            sp.wait_ge(env["shift_stored"], 16 * PARTS)
            load(1, 1)
            load_v(1, 1)
            with sp.Fori(0, NGRP // 2 - 1) as pair:
                for par in range(2):
                    g = 2 * pair + par
                    sp.wait_ge(scores_made, UNITS * (g + 1))
                    load(g + 2, par)
                    sp.wait_ge(steps_free, KT * (g + 1) + PSTEPS)
                    load_v(g + 2, par)
                    store(g)
            for b in range(BATCH - 1):
                load_sums(sp, env, b)
            store(NGRP - 2)
            for b in range(BATCH - 1):
                store_reciprocals(sp, env, b)
            sp.wait_ge(env["den_stored"], 16 * (BATCH - 1))
            load_merge(sp, env, Chunk(0, 0))
            load_merge(sp, env, Chunk(0, 1))
            store(NGRP - 1)
            sp.wait_ge(o_stored, 16 * GH * NGRP + 1)

        @block.gpsimd
        def _(pool):
            nc.gpsimd.memset(start[:, 0:1], 0.0).then_inc(slots_free, SLOTS)
            nc.gpsimd.memset(start[:, 1:2], 0.0).then_inc(steps_free, PSTEPS)
            nc.gpsimd.memset(start[:, 2:3], 0.0).then_inc(o_stored, 1)

        @block.tensor
        def _(pe):
            def score(g, par, seen, u):
                kt, j = divmod(u, GH)
                if u == 0:
                    if isinstance(g, int) and g == 0:
                        pe.wait_ge(qk_loaded[0], 16 * PART_LOADS)
                        pe.wait_ge(env["first_shift"], 16 * PARTS)
                    else:
                        pe.wait_ge(qk_loaded[par], 16 * ((PART_LOADS + 1) * (seen + 1) - (1 - par)))
                    if not (isinstance(g, int) and g == 0):
                        pe.wait_ge(bias_set, g)
                before = {0: 2, 1: 3, 2: 1}.get(u, u + 1)
                pe.wait_ge(slots_free, UNITS * g + before)
                for lo, hi, ahead in pieces((kt + 1) * P):
                    rows = PLAIN_K if ahead else FULL_K
                    last = nc.tensor.matmul(scores[:, u % SLOTS, lo:hi], k_op[par][0:rows, j, kt * P:(kt + 1) * P],
                                            q_op[par][0:rows, j, lo:hi], start=True, stop=True)
                last.then_inc(scores_made, 1)

            def weigh(g, par, seen, kt, half):
                if half == 0:
                    pe.wait_ge(slots_free, SLOTS + UNITS * g + GH * (kt + 1))
                    if kt == 0:
                        pe.wait_ge(v_loaded[par], 16 * (seen + 1))
                if kt == 0:
                    pe.wait_ge(o_ready, 2 * g + 1 + half)
                cols = slice(half * CHUNK, (half + 1) * CHUNK)
                for j in range(GH):
                    last = nc.tensor.matmul(acc[32 * j:32 * j + VW, cols], v_op[par][:, kt, VW * j:VW * (j + 1)],
                                            weights[:, kt % PSTEPS, j, cols], start=(kt == 0), stop=(kt == KT - 1))
                if half == 1:
                    last.then_inc(steps_free, 1)

            def body(g, par, seen, end):
                def ahead(kt, j):
                    if kt < KT:
                        score(g, par, seen, GH * kt + j)
                    elif not end:
                        score(g + 1, 1 - par, seen + par, GH * (kt - KT) + j)

                for kt in range(KT):
                    ahead(kt + 1, 2)
                    weigh(g, par, seen, kt, 0)
                    ahead(kt + 1, 3)
                    ahead(kt + 2, 0)
                    weigh(g, par, seen, kt, 1)
                    ahead(kt + 2, 1)

            for u in range(GH + 2):
                score(0, 0, 0, u)
            in_groups(pe, body)

        @block.vector
        def _(dve):
            v = nc.vector

            def take_scales(g, par):
                v.tensor_copy(now[:, par], head_scale[:, bass.ds(GH * g, GH), :]).then_inc(now_set, 1)

            def read_acc(g, half):
                if half == 0:
                    dve.wait_ge(steps_free, KT * (g + 1) + PSTEPS)
                    dve.wait_ge(o_stored, 16 * GH * g + 1)
                cols = slice(half * CHUNK, (half + 1) * CHUNK)
                v.tensor_copy(o_out[:, cols], acc[:, cols]).then_inc(o_ready, 1)

            def body(g, par, seen, end):
                for u in range(UNITS):
                    kt, j = divmod(u, GH)
                    if u in (GH + 1, GH + 2) and (not isinstance(g, int) or g > 0):
                        read_acc(g - 1, u - GH - 1)
                    dve.wait_ge(scores_made, UNITS * g + u + 1)
                    block_at = scores[:, u % SLOTS, kt * P:(kt + 1) * P]
                    v.scalar_tensor_tensor(out=block_at, in0=diag[:, 0, :], scalar=now[:, par, j, 0:1],
                                           in1=block_at, op0=ALU.mult, op1=ALU.add).then_inc(diag_added, 1)
                    if u == FILL_FROM - 1 and not end:
                        take_scales(g + 1, 1 - par)
                    if end and u % FILL_FROM == FILL_FROM - 1 and u // FILL_FROM < BATCH - 1:
                        reciprocals(nc, dve, env, u // FILL_FROM)
                    n = (u - FILL_FROM) // 2
                    if u >= FILL_FROM and u % 2 == 0 and n < 2 * GH and not end:
                        if n == 0:
                            dve.wait_ge(now_set, g + 2)
                        row = fill_bias_row(on_vector(nc), env, now[:, 1 - par], (q_op[1 - par], k_op[1 - par]), n)
                        if n == 2 * GH - 1:
                            row.then_inc(bias_set, 1)

            v.memset(acc[:, :], 0.0).then_inc(o_ready, 2)
            take_scales(0, 0)
            dve.wait_ge(now_set, 1)
            in_groups(dve, body)
            read_acc(NGRP - 1, 0)
            read_acc(NGRP - 1, 1)

        @block.scalar
        def _(act):
            with act.Fori(0, NGRP) as g:
                for u in range(UNITS):
                    kt, j = divmod(u, GH)
                    if j == 0:
                        act.wait_ge(steps_free, KT * g + kt + 1)
                    act.wait_ge(diag_added, UNITS * g + u + 1)
                    nc.scalar.activation(weights[:, kt % PSTEPS, j, :], scores[:, u % SLOTS, :],
                                         ACT.Exp).then_inc(slots_free, 1)


_INS = ["L0_attn_x", "L0_attn_qkv_w", "L0_attn_proj_w", "L0_attn_proj_b", "L0_attn_slopes", "L0_ffn_gate",
        "L0_ffn_corr_bias", "L0_ffn_w1", "L0_ffn_w2", "L0_ffn_fc1_w", "L0_ffn_fc2_w", "L0_ffn_up_w",
        "L0_ffn_down_w"]


def kernel(**inputs):
    import concourse.bacc as _bacc
    from concourse.bass_utils import run_bass_kernel_spmd as _run

    nc = _bacc.Bacc("TRN2", target_bir_lowering=False, num_devices=1)
    arrays, io, consts = {}, {}, {}
    for name in _INS:
        a = np.ascontiguousarray(inputs[name])
        arrays[f"in_{name}_dram"] = a
        io[name] = nc.dram_tensor(f"in_{name}_dram", a.shape, mybir.dt.from_np(a.dtype), kind="ExternalInput").ap()
    for name, a in shape_constants().items():
        arrays[f"const_{name}"] = a
        consts[name] = nc.dram_tensor(f"const_{name}", a.shape, mybir.dt.from_np(a.dtype), kind="ExternalInput").ap()
    out = nc.dram_tensor("out_0_dram", (BATCH, SEQ, DIM), F32, kind="ExternalOutput").ap()
    program(nc, io, consts, out)
    r = _run(nc, [arrays], core_ids=[0])
    return r.results[0]["out_0_dram"]
```
